# Optimizing a Trainium2 kernel written in Bass

```python
import numpy as np
import jax
import jax.numpy as jnp

def _softmax(x, axis=-1):
    return jax.nn.softmax(x, axis=axis)

def _gelu(x):
    return jax.nn.gelu(x, approximate=True)

def _silu(x):
    return jax.nn.silu(x)

def _sigmoid(x):
    return jax.nn.sigmoid(x)

def _layernorm(x, axis=-1, eps=1e-05):
    m = jnp.mean(x, axis=axis, keepdims=True)
    v = jnp.var(x, axis=axis, keepdims=True)
    return (x - m) / jnp.sqrt(v + eps)

def _scatter_add(tgt, idx, src, axis=0):
    return tgt.at[idx].add(src)

def _segment_sum(src, seg, n):
    return jax.ops.segment_sum(src, seg, n)
kernel_name = 'mk_hybrid_d1_jaxref_r4_b74f23'

def setup_inputs(seed: int=0):
    np.random.seed(seed)
    _w = jnp.asarray

    def _L0_attn_a_setup():
        import jax, jax.numpy as jnp
        import numpy as np
        B, S, C, H = (2, 1024, 256, 8)
        D = C // H
        KCONV = 7

        def _ripple(x, Wqkv, Wo, conv_w):
            b, s, c = x.shape
            d = c // H
            qkv = x @ Wqkv
            q, k, v = jnp.split(qkv, 3, axis=-1)

            def heads(t):
                return t.reshape(b, s, H, d).transpose(0, 2, 1, 3)
            qh, kh, vh = (heads(q), heads(k), heads(v))
            n_pow = int(np.floor(np.log2(s))) + 1
            offsets = jnp.concatenate([jnp.zeros((1,), jnp.int32), (2 ** jnp.arange(n_pow)).astype(jnp.int32)])
            pos = jnp.arange(s, dtype=jnp.int32)[:, None] - offsets[None, :]
            valid = pos >= 0
            posc = jnp.clip(pos, 0)
            kg = kh[:, :, posc]
            vg = vh[:, :, posc]
            sc = jnp.einsum('bhsd,bhskd->bhsk', qh, kg) / np.sqrt(d)
            sc = jnp.where(valid[None, None], sc, -jnp.inf)
            w = jax.nn.softmax(sc, axis=-1)
            tele = jnp.einsum('bhsk,bhskd->bhsd', w, vg)
            vpad = jnp.pad(v, ((0, 0), (KCONV - 1, 0), (0, 0)))
            conv = jax.lax.conv_general_dilated(vpad.transpose(0, 2, 1), conv_w[:, None, :], window_strides=(1,), padding='VALID', feature_group_count=c, dimension_numbers=('NCH', 'OIH', 'NCH')).transpose(0, 2, 1)
            conv_h = conv.reshape(b, s, H, d).transpose(0, 2, 1, 3)
            fq = jax.nn.elu(qh) + 1.0
            fk = jax.nn.elu(kh) + 1.0
            kv = jnp.einsum('bhsd,bhse->bhde', fk, vh)
            z = jnp.einsum('bhsd,bhd->bhs', fq, fk.sum(2))
            low = jnp.einsum('bhsd,bhde->bhse', fq, kv) / (z[..., None] + 1e-06)
            h = (tele + conv_h + low).transpose(0, 2, 1, 3).reshape(b, s, c)
            return h @ Wo
        key = jax.random.key(seed)
        k1, k2, k3, k4 = jax.random.split(key, 4)
        x = jax.random.normal(k1, (B, S, C), jnp.float32)
        Wqkv = jax.random.normal(k2, (C, 3 * C), jnp.float32) * (1.0 / np.sqrt(C))
        Wo = jax.random.normal(k3, (C, C), jnp.float32) * (1.0 / np.sqrt(C))
        conv_w = jax.random.normal(k4, (C, KCONV), jnp.float32) * (1.0 / np.sqrt(KCONV))
        return {'x': x, 'Wqkv': Wqkv, 'Wo': Wo, 'conv_w': conv_w}
    _L0_attn_a_in = _L0_attn_a_setup()

    def _L0_attn_b_setup():
        import jax, jax.numpy as jnp
        from jax import lax
        import numpy as np
        D_MODEL = 256
        K = 32
        K_Q = 4
        N_ANCHOR = 4
        N_DECAY = K - N_ANCHOR
        M = 8
        KS = 4
        H = D_MODEL // K
        N_REP = K // K_Q
        DIM_K = D_MODEL
        DIM_DECAY = K
        DIM_Q = K_Q * H * M * 2
        TOTAL = DIM_K + DIM_DECAY + DIM_Q
        B, L = (2, 512)
        key = jax.random.key(seed)
        ks = jax.random.split(key, 8)
        x = jax.random.normal(ks[0], (B, L, D_MODEL), jnp.float32)
        W_in = jax.random.normal(ks[1], (D_MODEL, TOTAL), jnp.float32) * D_MODEL ** (-0.5)
        conv_k = jax.random.normal(ks[2], (KS, 1, DIM_K + DIM_DECAY), jnp.float32) * 0.3
        grid = np.linspace(-np.pi / 3, np.pi / 3, M)
        theta = jnp.asarray(np.tile(grid.reshape(1, 1, 1, 1, M), (1, 1, K, H, 1)), jnp.float32)
        decay_slopes = jnp.log(jnp.exp(jnp.asarray(np.geomspace(0.001, 0.1, N_DECAY), jnp.float32)) - 1.0)
        anchor_slopes = jnp.log(jnp.exp(jnp.asarray(np.geomspace(0.01, 0.1, N_ANCHOR), jnp.float32)) - 1.0)
        score_scale = jnp.ones((K,), jnp.float32)
        lim = float(np.sqrt(6.0 / (H + H)))
        W_re = jax.random.uniform(ks[3], (H, H), jnp.float32, -lim, lim)
        W_im = jax.random.uniform(ks[4], (H, H), jnp.float32, -lim, lim)
        norm_scale = jnp.ones((2 * H,), jnp.float32)
        W_out = jax.random.normal(ks[5], (D_MODEL, D_MODEL), jnp.float32) * D_MODEL ** (-0.5)
        return dict(x=x, W_in=W_in, conv_k=conv_k, theta=theta, decay_slopes=decay_slopes, anchor_slopes=anchor_slopes, score_scale=score_scale, W_re=W_re, W_im=W_im, norm_scale=norm_scale, W_out=W_out)
    _L0_attn_b_in = _L0_attn_b_setup()

    def _L0_ffn_setup():
        import jax, jax.numpy as jnp
        import numpy as np
        DIM = 256

        def _reference_tuple_inner(x, W_r, W_k, W_v, mu_r, mu_k):
            B, T, C = x.shape
            x_prev = jnp.concatenate([jnp.zeros((B, 1, C), x.dtype), x[:, :-1, :]], axis=1)
            xr = mu_r * x + (1.0 - mu_r) * x_prev
            xk = mu_k * x + (1.0 - mu_k) * x_prev
            r = jax.nn.sigmoid(jnp.einsum('btc,dc->btd', xr, W_r))
            k = jnp.einsum('btc,dc->btd', xk, W_k)
            k_act = jnp.square(jax.nn.relu(k))
            out = r * jnp.einsum('btc,dc->btd', k_act, W_v)
            new_state = x[:, -1, :]
            return (out, new_state)
        key = jax.random.key(seed)
        ks = jax.random.split(key, 6)
        B, T, C = (8, 512, DIM)
        x = jax.random.normal(ks[0], (B, T, C), dtype=jnp.float32)
        s = 1.0 / np.sqrt(C)
        W_r = jax.random.uniform(ks[1], (C, C), jnp.float32, -s, s)
        W_k = jax.random.uniform(ks[2], (C, C), jnp.float32, -s, s)
        W_v = jax.random.uniform(ks[3], (C, C), jnp.float32, -s, s)
        mu_r = jax.random.uniform(ks[4], (C,), jnp.float32)
        mu_k = jax.random.uniform(ks[5], (C,), jnp.float32)
        return {'x': x, 'W_r': W_r, 'W_k': W_k, 'W_v': W_v, 'mu_r': mu_r, 'mu_k': mu_k}
    _L0_ffn_in = _L0_ffn_setup()
    _d = {'L0_attn_a_x': _L0_attn_a_in['x'], 'L0_attn_a_Wqkv': _L0_attn_a_in['Wqkv'], 'L0_attn_a_Wo': _L0_attn_a_in['Wo'], 'L0_attn_a_conv_w': _L0_attn_a_in['conv_w'], 'L0_attn_b_W_in': _L0_attn_b_in['W_in'], 'L0_attn_b_conv_k': _L0_attn_b_in['conv_k'], 'L0_attn_b_theta': _L0_attn_b_in['theta'], 'L0_attn_b_decay_slopes': _L0_attn_b_in['decay_slopes'], 'L0_attn_b_anchor_slopes': _L0_attn_b_in['anchor_slopes'], 'L0_attn_b_score_scale': _L0_attn_b_in['score_scale'], 'L0_attn_b_W_re': _L0_attn_b_in['W_re'], 'L0_attn_b_W_im': _L0_attn_b_in['W_im'], 'L0_attn_b_norm_scale': _L0_attn_b_in['norm_scale'], 'L0_attn_b_W_out': _L0_attn_b_in['W_out'], 'L0_ffn_W_r': _L0_ffn_in['W_r'], 'L0_ffn_W_k': _L0_ffn_in['W_k'], 'L0_ffn_W_v': _L0_ffn_in['W_v'], 'L0_ffn_mu_r': _L0_ffn_in['mu_r'], 'L0_ffn_mu_k': _L0_ffn_in['mu_k']}
    _x0 = _d['L0_attn_a_x']
    _d['L0_attn_a_x'] = jax.random.normal(jax.random.fold_in(jax.random.key(seed), 1), (8, 1024, 256), dtype=_x0.dtype)
    del _x0
    return _d

def reference(L0_attn_a_x, L0_attn_a_Wqkv, L0_attn_a_Wo, L0_attn_a_conv_w, L0_attn_b_W_in, L0_attn_b_conv_k, L0_attn_b_theta, L0_attn_b_decay_slopes, L0_attn_b_anchor_slopes, L0_attn_b_score_scale, L0_attn_b_W_re, L0_attn_b_W_im, L0_attn_b_norm_scale, L0_attn_b_W_out, L0_ffn_W_r, L0_ffn_W_k, L0_ffn_W_v, L0_ffn_mu_r, L0_ffn_mu_k):

    def _L0_attn_a_ref(x, Wqkv, Wo, conv_w):
        import jax, jax.numpy as jnp
        import numpy as np
        B, S, C, H = (2, 1024, 256, 8)
        D = C // H
        KCONV = 7

        def _ripple(x, Wqkv, Wo, conv_w):
            b, s, c = x.shape
            d = c // H
            qkv = x @ Wqkv
            q, k, v = jnp.split(qkv, 3, axis=-1)

            def heads(t):
                return t.reshape(b, s, H, d).transpose(0, 2, 1, 3)
            qh, kh, vh = (heads(q), heads(k), heads(v))
            n_pow = int(np.floor(np.log2(s))) + 1
            offsets = jnp.concatenate([jnp.zeros((1,), jnp.int32), (2 ** jnp.arange(n_pow)).astype(jnp.int32)])
            pos = jnp.arange(s, dtype=jnp.int32)[:, None] - offsets[None, :]
            valid = pos >= 0
            posc = jnp.clip(pos, 0)
            kg = kh[:, :, posc]
            vg = vh[:, :, posc]
            sc = jnp.einsum('bhsd,bhskd->bhsk', qh, kg) / np.sqrt(d)
            sc = jnp.where(valid[None, None], sc, -jnp.inf)
            w = jax.nn.softmax(sc, axis=-1)
            tele = jnp.einsum('bhsk,bhskd->bhsd', w, vg)
            vpad = jnp.pad(v, ((0, 0), (KCONV - 1, 0), (0, 0)))
            conv = jax.lax.conv_general_dilated(vpad.transpose(0, 2, 1), conv_w[:, None, :], window_strides=(1,), padding='VALID', feature_group_count=c, dimension_numbers=('NCH', 'OIH', 'NCH')).transpose(0, 2, 1)
            conv_h = conv.reshape(b, s, H, d).transpose(0, 2, 1, 3)
            fq = jax.nn.elu(qh) + 1.0
            fk = jax.nn.elu(kh) + 1.0
            kv = jnp.einsum('bhsd,bhse->bhde', fk, vh)
            z = jnp.einsum('bhsd,bhd->bhs', fq, fk.sum(2))
            low = jnp.einsum('bhsd,bhde->bhse', fq, kv) / (z[..., None] + 1e-06)
            h = (tele + conv_h + low).transpose(0, 2, 1, 3).reshape(b, s, c)
            return h @ Wo
        return x + _ripple(x, Wqkv, Wo, conv_w)

    def _L0_attn_b_ref(x, W_in, conv_k, theta, decay_slopes, anchor_slopes, score_scale, W_re, W_im, norm_scale, W_out):
        import jax, jax.numpy as jnp
        from jax import lax
        import numpy as np
        D_MODEL = 256
        K = 32
        K_Q = 4
        N_ANCHOR = 4
        N_DECAY = K - N_ANCHOR
        M = 8
        KS = 4
        H = D_MODEL // K
        N_REP = K // K_Q
        DIM_K = D_MODEL
        DIM_DECAY = K
        DIM_Q = K_Q * H * M * 2
        TOTAL = DIM_K + DIM_DECAY + DIM_Q
        B, L = (2, 512)
        b, l, _ = x.shape
        z = x @ W_in
        z_mem = z[..., :DIM_K + DIM_DECAY]
        q_raw = z[..., DIM_K + DIM_DECAY:]
        zp = jnp.pad(z_mem, ((0, 0), (KS - 1, 0), (0, 0)))
        z_mem = lax.conv_general_dilated(zp, conv_k, window_strides=(1,), padding='VALID', dimension_numbers=('NWC', 'WIO', 'NWC'), feature_group_count=DIM_K + DIM_DECAY)
        k_val = z_mem[..., :DIM_K].reshape(b, l, K, H)
        s_raw = z_mem[..., -K:].reshape(b, l, K, 1)
        q = q_raw.reshape(b, l, K_Q, H, M, 2)
        q_re, q_im = (q[..., 0], q[..., 1])
        pos = jnp.arange(l, dtype=jnp.float32)
        slopes_d = jax.nn.softplus(decay_slopes).reshape(1, 1, N_DECAY, 1)
        dist = jnp.maximum(jnp.float32(l - 1) - pos, 0.0)
        lw_d = -slopes_d * dist[None, :, None, None]
        slopes_a = jax.nn.softplus(anchor_slopes).reshape(1, 1, N_ANCHOR, 1)
        lw_a = -slopes_a * pos[None, :, None, None]
        log_tw = jnp.concatenate([lw_d, lw_a], axis=2)
        log_p = jnp.clip(score_scale[None, None, :, None] * s_raw, -20.0, 20.0)
        p_w = jnp.exp(log_p + log_tw)
        phi = k_val[..., None] * theta
        re_k = jnp.cos(phi)
        im_k = jnp.sin(phi)
        den = jnp.cumsum(p_w[..., 0], axis=1)
        pwb = p_w[..., None]
        num_re = jnp.cumsum(pwb * re_k, axis=1)
        num_im = jnp.cumsum(pwb * im_k, axis=1)
        inv = lax.rsqrt(jnp.maximum(den, 0.0001))
        inv = (inv * inv)[..., None, None]
        s_re = (num_re * inv).reshape(b, l, K_Q, N_REP, H, M)
        s_im = (num_im * inv).reshape(b, l, K_Q, N_REP, H, M)
        qr = q_re.reshape(b, l, K_Q, 1, H, M)
        qi = q_im.reshape(b, l, K_Q, 1, H, M)
        out_re = jnp.sum(s_re * qr + s_im * qi, axis=-1).reshape(b, l, K, H)
        out_im = jnp.sum(s_im * qr - s_re * qi, axis=-1).reshape(b, l, K, H)
        y_re = out_re * norm_scale[:H] * jnp.diagonal(W_re)
        y_im = out_im * norm_scale[H:] * jnp.diagonal(W_im)
        y = jax.nn.silu((y_re + y_im).reshape(b, l, DIM_K))
        return y @ W_out

    def _L0_ffn_ref(x, W_r, W_k, W_v, mu_r, mu_k):
        import jax, jax.numpy as jnp
        import numpy as np
        DIM = 256

        def _reference_tuple_inner(x, W_r, W_k, W_v, mu_r, mu_k):
            B, T, C = x.shape
            x_prev = jnp.concatenate([jnp.zeros((B, 1, C), x.dtype), x[:, :-1, :]], axis=1)
            xr = mu_r * x + (1.0 - mu_r) * x_prev
            xk = mu_k * x + (1.0 - mu_k) * x_prev
            r = jax.nn.sigmoid(jnp.einsum('btc,dc->btd', xr, W_r))
            k = jnp.einsum('btc,dc->btd', xk, W_k)
            k_act = jnp.square(jax.nn.relu(k))
            out = r * jnp.einsum('btc,dc->btd', k_act, W_v)
            new_state = x[:, -1, :]
            return (out, new_state)
        return _reference_tuple_inner(x, W_r, W_k, W_v, mu_r, mu_k)[0]
    x = L0_attn_a_x
    x = x + _L0_attn_a_ref(_layernorm(x, axis=-1), L0_attn_a_Wqkv, L0_attn_a_Wo, L0_attn_a_conv_w)
    x = x + _L0_ffn_ref(_layernorm(x, axis=-1), L0_ffn_W_r, L0_ffn_W_k, L0_ffn_W_v, L0_ffn_mu_r, L0_ffn_mu_k)
    x = x + _L0_attn_b_ref(_layernorm(x, axis=-1), L0_attn_b_W_in, L0_attn_b_conv_k, L0_attn_b_theta, L0_attn_b_decay_slopes, L0_attn_b_anchor_slopes, L0_attn_b_score_scale, L0_attn_b_W_re, L0_attn_b_W_im, L0_attn_b_norm_scale, L0_attn_b_W_out)
    x = x + _L0_ffn_ref(_layernorm(x, axis=-1), L0_ffn_W_r, L0_ffn_W_k, L0_ffn_W_v, L0_ffn_mu_r, L0_ffn_mu_k)
    return x

_drawn_inputs = setup_inputs


def setup_inputs(seed=0):
    import zlib

    import numpy as np

    out = dict(_drawn_inputs(seed))
    spreads = {'L0_attn_b_score_scale': (1.0, 0.6), 'L0_attn_b_norm_scale': (1.0, 0.2)}
    factors = {'L0_attn_b_anchor_slopes': 64.0, 'L0_ffn_W_r': 3.292, 'L0_ffn_mu_r': 6.605}
    for name, (base, spread) in spreads.items():
        noise = np.random.default_rng([zlib.crc32(name.encode()), seed]).standard_normal(out[name].shape)
        drawn = base * np.exp(spread * noise) if base else spread * noise
        out[name] = jnp.asarray(drawn.astype(out[name].dtype))
    for name, factor in factors.items():
        out[name] = (out[name] * factor).astype(out[name].dtype)
    return out
```

```python
import concourse.bass as bass
from concourse import mybir
from contextlib import ExitStack

import numpy as np

P = 128
NSEQ, S, C = 8, 1024, 256
T = S // P
HALF = 512
TH = T // 2
NC = C // P
H = 8
D = C // H
OFFS = [0] + [2 ** n for n in range(10)]
NO = len(OFFS)
LOW = NO
NJ, NS = 4, 3
PAD = 512
KCONV = 7
TAPS = [t for t in range(KCONV) if t not in OFFS]
NTAP = len(TAPS)
K2, H2, M2, KQ = 32, 8, 8, 4
NPAIR = K2 // 2
KS = 4
NDECAY = 28
EPS = 1e-5
ROUND = 12582912.0
TWO_PI = 6.283185
ORDER = [8 * c + u for c in range(2) for u in (0, 2, 1, 3, 4, 6, 5, 7)]


def constants():
    f, p = np.arange(P), np.arange(P)[:, None]
    ident = np.eye(P, dtype=np.float32)
    headsum = np.zeros((P, NS, NC, 32), np.float32)
    spread = np.zeros((3, NJ, H, NJ, NC, P), np.float32)
    for s in range(NS):
        for c in range(NC):
            headsum[f, s, c, s * H + c * (H // NC) + f // D] = 1.0
    for j in range(NJ):
        for c in range(NC):
            spread[:, j, c * (H // NC) + f // D, j, c, f] = 1.0
    spread = spread.reshape(3 * NJ * H, NJ * NC * P)
    mask = np.zeros((P, T, NS, NJ, H), np.float32)
    time = (np.arange(T)[None, :] * P + np.arange(P)[:, None])
    for o in range(NS * NJ):
        bad = time < OFFS[o] if o < NO else time >= 0
        mask[:, :, o // NJ, o % NJ, :] = np.where(bad, -1e30, 0.0)[:, :, None]
    sameheads = (p // D == f[None, :] // D).astype(np.float32)
    headof = np.zeros((P, NC, H), np.float32)
    for c in range(NC):
        headof[f, c, c * (H // NC) + f // D] = 1.0
    pairof = np.zeros((3, K2, NPAIR, P), np.float32)
    for i in range(NPAIR):
        pairof[:, 2 * i + f // 64, i, f] = 1.0
    pairof = pairof.reshape(3 * K2, NPAIR * P)
    phasesum = np.zeros((P, 2, 32), np.float32)
    for par in range(2):
        phasesum[f, par, par * 16 + f // M2] = 1.0
    kernelof = np.zeros((P, 4, 2, P), np.float32)
    for c in range(2):
        for q in range(4):
            kernelof[32 * q + 16 * c + f // H2, q, c, f] = 1.0
    t = np.arange(S, dtype=np.float32)
    dist = np.where(np.arange(K2)[:, None] < NDECAY, S - 1 - t, t).astype(np.float32)
    return dict(ident=ident, headsum=headsum.reshape(P, -1), spread=spread, mask=mask.reshape(P, -1),
                sameheads=sameheads, headof=headof.reshape(P, -1), pairof=pairof,
                phasesum=phasesum.reshape(P, -1), kernelof=kernelof.reshape(P, -1),
                dist=np.tile(dist, (4, 1)))


def build(nc, w, k, x_dram, out_dram):
    fp32, bf16 = mybir.dt.float32, mybir.dt.bfloat16
    ALU, ACT, AX = mybir.AluOpType, mybir.ActivationFunctionType, mybir.AxisListType.X
    ctx = ExitStack()
    with ctx:
        def sb(name, shape, dt=fp32):
            return ctx.enter_context(nc.sbuf_tensor(name, shape, dt))

        per, names = {}, {}

        def sem(name, per_sequence=0):
            s = ctx.enter_context(nc.semaphore(name))
            per[name] = per_sequence
            names[id(s)] = name
            return s

        def nth(seq, s, n):
            return seq * per[names[id(s)]] + n

        ident = sb("ident", [P, P])
        ident_b = sb("ident_b", [P, P], bf16)
        headsum = sb("headsum", [P, NS, NC, 32])
        spread = sb("spread", [96, NJ, NC, P], bf16)
        mask = sb("mask", [P, T, NS, NJ * H])
        sameheads = sb("sameheads", [P, P])
        headof = sb("headof", [P, NC, H])
        pairof = sb("pairof", [96, NPAIR, P], bf16)
        phasesum = sb("phasesum", [P, 2, 32])
        kernelof = sb("kernelof", [P, 4, 2, P])
        log_time = sb("log_time", [P, S])
        wqkv = sb("wqkv", [P, NC, 3 * C])
        wo = sb("wo", [P, NC, C])
        wr = sb("wr", [P, NC, C])
        wk = sb("wk", [P, NC, C])
        wv = sb("wv", [P, NC, C])
        w_in_k = sb("w_in_k", [P, NC, C])
        w_in_s = sb("w_in_s", [P, NC, 4, K2])
        w_in_q = sb("w_in_q", [P, NC, 2 * KQ, 2, 64])
        w_out = sb("w_out", [P, NC, C])
        theta_w = sb("theta_w", [P, NC, 8, P])
        tap_w = sb("tap_w", [P, NTAP, NC, P])
        conv_a = sb("conv_a", [P, NC, KCONV])
        conv_bk = sb("conv_bk", [P, NC, KS])
        conv_bs = sb("conv_bs", [P, KS])
        mu_r = sb("mu_r", [P, NC])
        mu_k = sb("mu_k", [P, NC])
        theta = sb("theta", [P, NC, M2])
        slope = sb("slope", [P, 8])
        score_scale = sb("score_scale", [P, 1])
        gains = sb("gains", [P, 6, H2])
        half_pi = sb("half_pi", [P, 1])
        round_c = sb("round_c", [P, 1])
        minus_half = sb("minus_half", [P, TH])
        eps = sb("eps", [P, TH])

        x_in = sb("x_in", [P, T, C])
        xs = sb("xs", [P, T, C])
        h = sb("h", [P, T, C])
        x_out = h
        hT = sb("hT", [P, NC, 1 + S])
        stats = sb("stats", [P, T, 6])
        mv = sb("mv", [P, T, 2])
        rstd = sb("rstd", [P, T])
        veps = sb("veps", [P, T])
        count = sb("count", [P, 1])
        neg_mr = sb("neg_mr", [P, T])

        ARENA = 28480
        arena = sb("arena", [P, ARENA])
        top = [0]

        def take(cols):
            a = arena[:, top[0]:top[0] + cols]
            top[0] += cols
            assert top[0] <= ARENA, top[0]
            return a

        qT = take(NC * S).rearrange("p (c n) -> p c n", c=NC)
        kT = take(NC * (PAD + S)).rearrange("p (c n) -> p c n", c=NC)
        vT = take(NC * (PAD + S)).rearrange("p (c n) -> p c n", c=NC)
        fqT = take(NC * S).rearrange("p (c n) -> p c n", c=NC)
        fkT = take(NC * S).rearrange("p (c n) -> p c n", c=NC)
        low_num = fkT
        hsumT = qT
        relus = take(4 * HALF).rearrange("p (r n) -> p r n", r=4)
        FKV = 2 * P + 1
        fkv = take(T * NC * FKV).rearrange("p (t c n) -> p t c n", t=T, c=NC)
        NPROD = 6
        prods = take(NPROD * NC * HALF).rearrange("p (r c n) -> p r c n", r=NPROD, c=NC)
        sT = take(HALF)
        sm = take(T * 96).rearrange("p (t s w) -> p t s w", t=T, s=NS)
        smx = take(TH * (4 * 32)).rearrange("p (t w) -> p t w", t=TH)
        srec = take(TH * H).rearrange("p (t w) -> p t w", t=TH)
        zrec = take(T * H).rearrange("p (t w) -> p t w", t=T)
        wrest = take(TH * 96).rearrange("p (t w) -> p t w", t=TH * NS)
        kvbd = take(NC * P).rearrange("p (c n) -> p c n", c=NC)
        zsel = take(NC * H).rearrange("p (c n) -> p c n", c=NC)
        w3 = take(TH * NS * 96 // 2).bitcast(bf16).rearrange("p (t s q w) -> p t s q w", t=TH, s=NS, q=3)
        w3T = take(NS * HALF // 2).bitcast(bf16).rearrange("p (s n) -> p s n", s=NS)[0:96]
        top[0] = 0
        dT = take(NC * S).rearrange("p (c n) -> p c n", c=NC)
        xkT = take(NC * S).rearrange("p (c n) -> p c n", c=NC)
        xrT = take(NC * S).rearrange("p (c n) -> p c n", c=NC)
        kact = take(NC * S).rearrange("p (c n) -> p c n", c=NC)
        gate = take(4 * HALF).rearrange("p (r n) -> p r n", r=4)
        gated = take(4 * HALF).rearrange("p (r n) -> p r n", r=4)
        top[0] = 0
        ZP = KS - 1 + S
        z_raw = take(NC * ZP).rearrange("p (c n) -> p c n", c=NC)
        yT = z_raw[:, :, 0:S]
        zc = take(NC * S).rearrange("p (c n) -> p c n", c=NC)
        qpT = take(2 * KQ * S).rearrange("p (q n) -> p q n", q=2 * KQ)
        turns = take(2 * S).rearrange("p (r n) -> p r n", r=2)
        trig = take(2 * 2 * S).rearrange("p (r a n) -> p r a n", r=2, a=2)
        NNUM = 4
        nums = take(NNUM * 2 * S).rearrange("p (r a n) -> p r a n", r=NNUM, a=2)
        p3 = take(S // 2).bitcast(bf16)
        den_inv = take(S // 4)
        thT = trig[:, 0]
        zs_raw = nums[:, 0].rearrange("p a n -> p (a n)")[:, 0:ZP]
        zs = nums[:, 1, 0]
        pw = nums[:, 2, 0]
        prest = nums[:, 3, 0]
        den = nums[:, 3, 1]
        top[0] = 0
        wq_raw = take(NC * 512).rearrange("p (c n) -> p c n", c=NC)
        spread_f = take(NJ * NC * P)[0:96]
        pairof_f = take(NPAIR * P)[0:96]

        PS = ctx.enter_context(nc.psum_tensor("PS", [P, 8, HALF], fp32))

        weights_in = sem("weights_in")
        prologue = sem("prologue")
        pro_act = sem("pro_act")
        pro_pool = sem("pro_pool")
        x_loaded = sem("x_loaded", 16)
        out_stored = sem("out_stored", 16)
        stats_ready = sem("stats_ready", 8)
        mv_ready = sem("mv_ready", 8)
        veps_ready = sem("veps_ready", 8)
        rstd_ready = sem("rstd_ready", 8)
        neg_mr_ready = sem("neg_mr_ready", 8)
        h_ready = sem("h_ready", 32)
        hT_psum = sem("hT_psum", 16)
        hT_ready = sem("hT_ready", 16)
        xs_ready = sem("xs_ready", 12)
        out_ready = sem("out_ready", 4)
        qkv_psum = sem("qkv_psum", 12)
        qkv_sb = sem("qkv_sb", 12)
        exp_ready = sem("exp_ready", 8)
        elu_ready = sem("elu_ready", 8)
        xh_ready = sem("xh_ready", 2)
        pads_ready = sem("pads_ready", 1)
        zpads_ready = sem("zpads_ready", 1)
        qk_prod = sem("qk_prod", 21)
        qk_summed = sem("qk_summed", 21)
        sT_ready = sem("sT_ready", 2)
        stok_psum = sem("stok_psum", 2)
        soft = sem("soft", 2 * 15)
        exps_ready = sem("exps_ready", 2)
        whi_ready = sem("whi_ready", 2)
        wmid_ready = sem("wmid_ready", 2)
        w3T_psum = sem("w3T_psum", 4)
        w3T_ready = sem("w3T_ready", 4)
        fkv_psum = sem("fkv_psum", 8)
        fkv_ready = sem("fkv_ready", 8)
        kv_psum = sem("kv_psum", 1)
        kvbd_ready = sem("kvbd_ready", 2)
        z_psum = sem("z_psum", 1)
        z_ready = sem("z_ready", 2)
        low_psum = sem("low_psum", 4)
        low_ready = sem("low_ready", 4)
        wbc_psum = sem("wbc_psum", 24)
        wv_prod = sem("wv_prod", 24)
        wv_pool = sem("wv_pool", 16)
        wv_acc = sem("wv_acc", 8)
        hsumT_ready = sem("hsumT_ready", 4)
        wo_psum = sem("wo_psum", 4)
        d_ready = sem("d_ready", 8)
        xk_ready = sem("xk_ready", 8)
        xr_ready = sem("xr_ready", 8)
        k_psum = sem("k_psum", 8)
        relu_ready = sem("relu_ready", 8)
        kact_ready = sem("kact_ready", 8)
        r_psum = sem("r_psum", 8)
        gate_ready = sem("gate_ready", 8)
        v_psum = sem("v_psum", 8)
        gated_ready = sem("gated_ready", 8)
        z_out = sem("z_out", 22)
        z_sb = sem("z_sb", 22)
        sconv = sem("sconv", 5)
        p_ready = sem("p_ready", 1)
        phi_ready = sem("phi_ready", 1)
        prest_ready = sem("prest_ready", 1)
        pmid_ready = sem("pmid_ready", 1)
        p3_ready = sem("p3_ready", 1)
        den_step = sem("den_step", 3)
        kconv = sem("kconv", 6)
        turn_psum = sem("turn_psum", NPAIR)
        turn_rounded = sem("turn_rounded", NPAIR)
        turn_ready = sem("turn_ready", NPAIR)
        abs_ready = sem("abs_ready", NPAIR)
        trig_ready = sem("trig_ready", NPAIR)
        pbc_psum = sem("pbc_psum", NPAIR)
        weighted = sem("weighted", NPAIR)
        num_ready = sem("num_ready", NPAIR)
        prod_re = sem("prod_re", NPAIR)
        prod_im = sem("prod_im", NPAIR)
        y_psum = sem("y_psum", 2 * 8)
        y_sb = sem("y_sb", 4)
        ibc_psum = sem("ibc_psum", 4)
        yn_ready = sem("yn_ready", 4)
        tanh_ready = sem("tanh_ready", 4)
        ys_ready = sem("ys_ready", 4)
        wout_psum = sem("wout_psum", 4)

        block = ctx.enter_context(nc.Block())

        step = [2]

        @block.sync
        def _(sp):
            def load(dst, src):
                sp.dma_start(dst, src).then_inc(weights_in, 16)

            chunked = "(c p) n -> p c n"
            for dst, src in ((wqkv, "Wqkv"), (wo, "Wo"), (wr, "WrT"), (wk, "WkT"), (wv, "WvT"),
                             (w_out, "W_out"), (conv_a, "conv_w"), (theta, "theta")):
                load(dst[:], w[src].rearrange(chunked, p=P))
            w_in = w["W_in"].rearrange(chunked, p=P)
            load(w_in_k[:], w_in[:, :, 0:C])
            for r in range(4):
                load(w_in_s[:, :, r, :], w_in[:, :, C:C + K2])
                load(conv_bs[32 * r:32 * r + 32, :], w["conv_kT"][C:C + K2, :])
                load(slope[32 * r:32 * r + 32, 0:1], w["slopes"])
                load(score_scale[32 * r:32 * r + 32, :], w["score_scale"])
            load(wq_raw, w_in[:, :, C + K2:])
            load(conv_bk[:], w["conv_kT"][0:C, :].rearrange(chunked, p=P))
            for c in range(NC):
                load(mu_r[:, c:c + 1], w["mu_r"][P * c:P * c + P, :])
                load(mu_k[:, c:c + 1], w["mu_k"][P * c:P * c + P, :])
            for n, src in enumerate(("norm_scale_re", "norm_scale_im", "diag_re", "diag_im")):
                load(gains[:, n, :], w[src].to_broadcast([P, H2]))
            load(ident[:], k["ident"])
            load(headsum[:].rearrange("p s c m -> p (s c m)"), k["headsum"])
            load(spread_f, k["spread"])
            load(mask[:].rearrange("p t s w -> p (t s w)"), k["mask"])
            load(sameheads[:], k["sameheads"])
            load(headof[:].rearrange("p c h -> p (c h)"), k["headof"])
            load(pairof_f, k["pairof"])
            load(phasesum[:].rearrange("p a m -> p (a m)"), k["phasesum"])
            load(kernelof[:].rearrange("p q a m -> p (q a m)"), k["kernelof"])
            sp.dma_start(log_time[:], k["dist"]).then_inc(out_stored, 16)
            def load_x(seq):
                sp.dma_start(x_in[:], x_dram[seq].rearrange("(t p) c -> p t c", p=P))\
                    .then_inc(x_loaded, 16)

            def store(seq):
                sp.wait_ge(out_ready, nth(seq, out_ready, 4))
                sp.dma_start(out_dram[seq].rearrange("(t p) c -> p t c", p=P), x_out[:])\
                    .then_inc(out_stored, 16)

            load_x(0)
            with sp.Fori(0, NSEQ - 1) as seq:
                sp.wait_ge(xh_ready, nth(seq, xh_ready, 2))
                load_x(seq + 1)
                store(seq)
            store(NSEQ - 1)
            sp.wait_ge(out_stored, (NSEQ + 1) * 16)

        N_LOADS = 8 + 1 + 4 * 4 + 2 + 2 * NC + 4 + 9

        @block.gpsimd
        def _(pool):
            pool.memset(minus_half[:], -0.5)
            pool.memset(eps[:], EPS)
            pool.memset(half_pi[:], float(np.pi / 2))
            pool.memset(hT[:, :, 0:1], 0.0)
            pool.memset(round_c[:], ROUND).then_inc(pro_pool, 1)
            pool.wait_ge(pro_pool, 1)

            def rstd_of(seq, ln):
                for hf in range(2):
                    n = 2 * ln + hf + 1
                    cols = slice(TH * hf, TH * hf + TH)
                    pool.wait_ge(mv_ready, nth(seq, mv_ready, n))
                    pool.tensor_tensor(veps[:, cols], mv[:, cols, 1], eps[:], ALU.add)\
                        .then_inc(veps_ready, 1)
                    pool.wait_ge(veps_ready, nth(seq, veps_ready, n))
                    pool.tensor_tensor(rstd[:, cols], veps[:, cols], minus_half[:], ALU.pow)\
                        .then_inc(rstd_ready, 1)

            def ripple(seq):
                for hf in range(2):
                    pool.wait_ge(h_ready, nth(seq, h_ready, TH * (hf + 1)))
                    t = slice(TH * hf, TH * hf + TH)
                    pool.tensor_tensor(xs[:, t, :], x_in[:, t, :], h[:, t, :], ALU.add)\
                        .then_inc(xh_ready, 1)
                for hf in range(2):
                    for g in range(4):
                        for a in range(2):
                            u = 12 * hf + 3 * g + a + 1
                            pool.wait_ge(wv_prod, nth(seq, wv_prod, u + 1))
                            if a == 1:
                                pool.wait_ge(wv_pool, nth(seq, wv_pool, 8 * hf + 2 * g + 1))
                            pool.tensor_tensor(prods[:, u % NPROD], prods[:, u % NPROD],
                                               prods[:, (u - 1) % NPROD], ALU.add)\
                                .then_inc(wv_pool, 1)

            def ffn(seq, f):
                for hf in range(2):
                    for c in range(NC):
                        pool.wait_ge(hT_ready, nth(seq, hT_ready, (4 if f == 0 else 12) + 2 * hf + c + 1))
                        a = HALF * hf
                        pool.tensor_tensor(dT[:, c, a:a + HALF], hT[:, c, a + 1:a + 1 + HALF],
                                           hT[:, c, a:a + HALF], ALU.subtract).then_inc(d_ready, 1)

            def phase(seq):
                for n, i in enumerate(ORDER):
                    pool.wait_ge(num_ready, nth(seq, num_ready, n + 1))
                    pool.tensor_tensor(nums[:, n % NNUM, 0], nums[:, n % NNUM, 0],
                                       qpT[:, 2 * (i // 4)], ALU.mult).then_inc(prod_re, 1)

            with pool.Fori(0, NSEQ) as seq:
                rstd_of(seq, 0)
                ripple(seq)
                rstd_of(seq, 1)
                ffn(seq, 0)
                rstd_of(seq, 2)
                phase(seq)
                rstd_of(seq, 3)
                ffn(seq, 1)

        @block.scalar
        def _(act):
            act.wait_ge(pro_pool, 1)
            act.wait_ge(prologue, 1)
            act.activation(slope[:, 2:3], slope[:, 1:2], ACT.Exp, scale=-1.0).then_inc(pro_act, 1)
            act.wait_ge(prologue, 2)
            act.activation(slope[:, 4:5], slope[:, 3:4], ACT.Ln).then_inc(pro_act, 1)

            def normalise(seq, ln, x):
                for t in range(T):
                    if t % TH == 0:
                        act.wait_ge(neg_mr_ready, nth(seq, neg_mr_ready, 2 * ln + t // TH + 1))
                        if ln == 0:
                            act.wait_ge(out_stored, nth(seq, out_stored, 16))
                    act.activation(h[:, t, :], x[:, t, :], ACT.Identity, bias=neg_mr[:, t:t + 1],
                                   scale=rstd[:, t:t + 1]).then_inc(h_ready, 1)

            def evacuate_hT(seq, ln):
                for hf in range(2):
                    for c in range(NC):
                        act.wait_ge(hT_psum, nth(seq, hT_psum, 4 * ln + 2 * hf + c + 1))
                        a = 1 + HALF * hf
                        act.activation(hT[:, c, a:a + HALF], PS[:, 2 * hf + c], ACT.Copy)\
                            .then_inc(hT_ready, 1)

            def qkv_out(seq, hf):
                for m in range(6):
                    n = 6 * hf + m
                    c = m % 2
                    a = HALF * hf
                    bank = PS[:, 4 + n % 4]
                    act.wait_ge(qkv_psum, nth(seq, qkv_psum, n + 1))
                    if m < 4:
                        e = 4 * hf + m
                        dst = (fkT if m < 2 else fqT)[:, c, a:a + HALF]
                        act.activation(dst, bank, ACT.Exp)
                        if e >= 4:
                            act.wait_ge(elu_ready, nth(seq, elu_ready, e - 3))
                        act.activation(relus[:, e % 4], bank, ACT.Relu).then_inc(exp_ready, 1)
                    if m < 2:
                        dst = kT[:, c, PAD + a:PAD + a + HALF]
                    elif m < 4:
                        dst = qT[:, c, a:a + HALF]
                    else:
                        dst = vT[:, c, PAD + a:PAD + a + HALF]
                    act.activation(dst, bank, ACT.Copy).then_inc(qkv_sb, 1)

            def ripple(seq):
                qkv_out(seq, 0)
                qkv_out(seq, 1)
                act.wait_ge(qk_summed, nth(seq, qk_summed, 10))
                act.activation(sT, PS[:, 0], ACT.Copy).then_inc(sT_ready, 1)
                for t in range(T):
                    act.wait_ge(fkv_psum, nth(seq, fkv_psum, t + 1))
                    act.activation(fkv[:, t, :, 0:2 * P],
                                   PS[:, 4 + t % 4].rearrange("p (c n) -> p c n", c=NC), ACT.Copy)\
                        .then_inc(fkv_ready, 1)
                softmax_exp(seq, 0)
                for n in range(4):
                    act.wait_ge(low_psum, nth(seq, low_psum, n + 1))
                    c, hf = n % 2, n // 2
                    act.activation(low_num[:, c, HALF * hf:HALF * hf + HALF], PS[:, 4 + (n + 1) % 4],
                                   ACT.Copy).then_inc(low_ready, 1)
                act.wait_ge(qk_summed, nth(seq, qk_summed, 21))
                act.activation(sT, PS[:, 0], ACT.Copy).then_inc(sT_ready, 1)
                softmax_split(seq, 0)
                softmax_exp(seq, 1)
                softmax_split(seq, 1)
                for hf in range(2):
                    for c in range(NC):
                        act.wait_ge(wv_acc, nth(seq, wv_acc, 4 * hf + 4))
                        act.activation(hsumT[:, c, HALF * hf:HALF * hf + HALF], PS[:, 2 + c], ACT.Copy)\
                            .then_inc(hsumT_ready, 1)

            def softmax_exp(seq, hf):
                act.wait_ge(soft, nth(seq, soft, 15 * hf + 6))
                t = slice(TH * hf, TH * hf + TH)
                act.activation(sm[:, t], sm[:, t], ACT.Exp, scale=float(D) ** -0.5)\
                    .then_inc(exps_ready, 1)

            def softmax_split(seq, hf):
                t = slice(TH * hf, TH * hf + TH)
                flat = sm[:, t].rearrange("p t s w -> p (t s) w")
                parts = w3.rearrange("p t s q w -> p (t s) q w")
                act.wait_ge(soft, nth(seq, soft, 15 * hf + 13))
                act.activation(parts[:, :, 0], flat, ACT.Copy).then_inc(whi_ready, 1)
                act.wait_ge(soft, nth(seq, soft, 15 * hf + 14))
                act.activation(parts[:, :, 1], wrest, ACT.Copy).then_inc(wmid_ready, 1)
                bank = PS[0:96, 1].bitcast(bf16).rearrange("p (s n) -> p s n", s=2)
                act.wait_ge(w3T_psum, nth(seq, w3T_psum, 2 * hf + 1))
                if hf == 1:
                    act.wait_ge(wbc_psum, nth(seq, wbc_psum, 12))
                act.activation(w3T[:, 0:2], bank, ACT.Copy).then_inc(w3T_ready, 1)
                act.wait_ge(w3T_psum, nth(seq, w3T_psum, 2 * hf + 2))
                act.activation(w3T[:, 2], bank[:, 0], ACT.Copy).then_inc(w3T_ready, 1)

            def ffn(seq, f):
                for hf in range(2):
                    for m in range(NC):
                        n = 4 * f + 2 * hf + m + 1
                        a = slice(HALF * hf, HALF * hf + HALF)
                        act.wait_ge(k_psum, nth(seq, k_psum, n))
                        act.activation(kact[:, m, a], PS[:, 4 + 2 * hf + m], ACT.Relu)\
                            .then_inc(relu_ready, 1)
                        act.wait_ge(relu_ready, nth(seq, relu_ready, n))
                        act.activation(kact[:, m, a], kact[:, m, a], ACT.Square)\
                            .then_inc(kact_ready, 1)
                for tp in range(4):
                    act.wait_ge(r_psum, nth(seq, r_psum, 4 * f + tp + 1))
                    act.activation(gate[:, tp], PS[:, tp], ACT.Tanh, scale=0.5)\
                        .then_inc(gate_ready, 1)

            def phase_project(seq):
                for n in range(22):
                    bank = PS[:, 4 + n % 4]
                    act.wait_ge(z_out, nth(seq, z_out, n + 1))
                    if n < 6:
                        hf = n % 2
                        c = (n - 2) // 2
                        a = HALF * hf
                        raw = zs_raw if n < 2 else z_raw[:, c]
                        first = zs if n < 2 else zc[:, c]
                        tap = conv_bs[:, KS - 1:KS] if n < 2 else conv_bk[:, c, KS - 1:KS]
                        act.activation(first[:, a:a + HALF], bank, ACT.Copy, scale=tap)
                        act.activation(raw[:, KS - 1 + a:KS - 1 + a + HALF], bank, ACT.Copy)\
                            .then_inc(z_sb, 1)
                    else:
                        q, hf = (n - 6) // 2, n % 2
                        act.activation(qpT[:, q, HALF * hf:HALF * hf + HALF], bank, ACT.Copy)\
                            .then_inc(z_sb, 1)
                    if n == 13:
                        act.wait_ge(sconv, nth(seq, sconv, 5))
                        act.activation(pw, zs, ACT.Exp).then_inc(p_ready, 1)
                        act.wait_ge(p_ready, nth(seq, p_ready, 1))
                        act.activation(p3[0:96], pw[0:96], ACT.Copy).then_inc(phi_ready, 1)
                        act.wait_ge(prest_ready, nth(seq, prest_ready, 1))
                        for q in (1, 2):
                            r = slice(32 * q, 32 * q + 32)
                            mid = act.activation(p3[r], prest[r], ACT.Copy)
                        mid.then_inc(pmid_ready, 1)

            def phase_units(seq):
                def rounded(n):
                    act.wait_ge(turn_psum, nth(seq, turn_psum, n + 1))
                    if n >= 2:
                        act.wait_ge(trig_ready, nth(seq, trig_ready, n - 1))
                    a = 2 * (n % 2)
                    act.activation(turns[:, n % 2].rearrange("p (b n) -> p b n", b=2), PS[:, a:a + 2],
                                   ACT.Identity, bias=round_c[:]).then_inc(turn_rounded, 1)

                rounded(0)
                rounded(1)
                for n in range(NPAIR):
                    act.wait_ge(turn_ready, nth(seq, turn_ready, n + 1))
                    if n >= 2:
                        act.wait_ge(weighted, nth(seq, weighted, n - 1))
                    act.activation(trig[:, n % 2, 0], turns[:, n % 2], ACT.Abs).then_inc(abs_ready, 1)
                    act.activation(trig[:, n % 2, 1], turns[:, n % 2], ACT.Sin, scale=-TWO_PI)
                    act.wait_ge(abs_ready, nth(seq, abs_ready, n + 1))
                    act.activation(trig[:, n % 2, 0], trig[:, n % 2, 0], ACT.Sin, bias=half_pi[:],
                                   scale=-TWO_PI).then_inc(trig_ready, 1)
                    if n + 2 < NPAIR:
                        rounded(n + 2)
                    if n == 10 or n == 15:
                        c = 0 if n == 10 else 1
                        for hf in range(2):
                            act.wait_ge(y_psum, nth(seq, y_psum, 8 * c + 8))
                            act.activation(yT[:, c, HALF * hf:HALF * hf + HALF], PS[:, 6 + hf], ACT.Copy)\
                                .then_inc(y_sb, 1)
                for n in range(4):
                    c, a = n // 2, HALF * (n % 2)
                    act.wait_ge(yn_ready, nth(seq, yn_ready, n + 1))
                    act.activation(thT[:, c, a:a + HALF], yT[:, c, a:a + HALF], ACT.Tanh, scale=0.5)\
                        .then_inc(tanh_ready, 1)

            with act.Fori(0, NSEQ) as seq:
                normalise(seq, 0, x_in)
                evacuate_hT(seq, 0)
                ripple(seq)
                normalise(seq, 1, xs)
                evacuate_hT(seq, 1)
                ffn(seq, 0)
                normalise(seq, 2, xs)
                evacuate_hT(seq, 2)
                phase_project(seq)
                phase_units(seq)
                normalise(seq, 3, xs)
                evacuate_hT(seq, 3)
                ffn(seq, 1)

        @block.vector
        def _(dve):

            def link(i):
                step[0] += 1
                i.then_inc(prologue, 1)
                dve.wait_ge(prologue, step[0])

            dve.wait_ge(weights_in, 16 * N_LOADS)
            dve.wait_ge(out_stored, 16)
            dve.scalar_tensor_tensor(slope[:, 1:2], slope[:, 0:1], -1.0, slope[:, 0:1], ALU.mult, ALU.max)\
                .then_inc(prologue, 1)
            dve.wait_ge(pro_act, 1)
            dve.tensor_scalar(slope[:, 3:4], slope[:, 2:3], 1.0, None, ALU.add).then_inc(prologue, 1)
            dve.wait_ge(pro_act, 2)
            link(dve.tensor_scalar(slope[:, 5:6], slope[:, 3:4], -1.0, None, ALU.add))
            link(dve.tensor_scalar(slope[:, 6:7], slope[:, 5:6], 0.0, None, ALU.is_equal))
            link(dve.tensor_tensor(slope[:, 4:5], slope[:, 4:5], slope[:, 6:7], ALU.add))
            link(dve.tensor_tensor(slope[:, 5:6], slope[:, 5:6], slope[:, 6:7], ALU.add))
            link(dve.reciprocal(slope[:, 5:6], slope[:, 5:6]))
            link(dve.tensor_tensor(slope[:, 4:5], slope[:, 4:5], slope[:, 5:6], ALU.mult))
            link(dve.tensor_tensor(slope[:, 4:5], slope[:, 4:5], slope[:, 2:3], ALU.mult))
            link(dve.scalar_tensor_tensor(slope[:, 7:8], slope[:, 0:1], 0.0, slope[:, 4:5], ALU.max, ALU.add))
            link(dve.tensor_scalar(log_time[:], log_time[:], slope[:, 7:8], -1.0, ALU.mult, ALU.mult))
            link(dve.tensor_tensor(gains[:, 4], gains[:, 0], gains[:, 2], ALU.mult))
            link(dve.tensor_tensor(gains[:, 5], gains[:, 1], gains[:, 3], ALU.mult))
            scratch = xs[:].rearrange("p t c -> p (t c)")[:, 0:64].rearrange("p (h m) -> p h m", h=H2)
            for c in range(NC):
                raw = wq_raw[:, c].rearrange("p (q h m r) -> p q h m r", q=KQ, h=H2, m=M2)
                for q in range(KQ):
                    q_re, q_im = raw[:, q, :, :, 0], raw[:, q, :, :, 1]
                    g_re = gains[:, 4, :].unsqueeze(2).to_broadcast([P, H2, M2])
                    g_im = gains[:, 5, :].unsqueeze(2).to_broadcast([P, H2, M2])
                    for part, (a, b, op) in enumerate(((q_re, q_im, ALU.subtract), (q_im, q_re, ALU.add))):
                        dst = w_in_q[:, c, 2 * q + part]
                        once = dst[:, 0].rearrange("p (h m) -> p h m", h=H2)
                        link(dve.tensor_tensor(scratch, b, g_im, ALU.mult))
                        link(dve.tensor_tensor(once, a, g_re, ALU.mult))
                        link(dve.tensor_tensor(once, once, scratch, op))
                        link(dve.tensor_copy(dst[:, 1], dst[:, 0]))
                link(dve.tensor_scalar(theta[:, c], theta[:, c], float(1 / (2 * np.pi)), None, ALU.mult))
                link(dve.tensor_tensor(theta_w[:, c].rearrange("p i (a m) -> p (i a) m", m=M2),
                                       ident[:].unsqueeze(2).to_broadcast([P, P, M2]),
                                       theta[:, c:c + 1, :].to_broadcast([P, P, M2]), ALU.mult))
                for n, tap in enumerate(TAPS):
                    j = KCONV - 1 - tap
                    link(dve.tensor_scalar(tap_w[:, n, c], ident[:], conv_a[:, c, j:j + 1], None, ALU.mult))
            link(dve.tensor_copy(ident_b[:], ident[:]))
            link(dve.tensor_copy(spread[:].rearrange("p j c m -> p (j c m)"), spread_f))
            link(dve.tensor_copy(pairof[:].rearrange("p i m -> p (i m)"), pairof_f))
            link(dve.tensor_scalar(wv[:], wv[:], 0.5, None, ALU.mult))
            link(dve.tensor_scalar(w_out[:], w_out[:], 0.5, None, ALU.mult))

            def moments(seq, ln, x, hf):
                n = 2 * ln + hf + 1
                if ln == 0:
                    dve.wait_ge(x_loaded, nth(seq, x_loaded, 16))
                else:
                    dve.wait_ge(xs_ready, nth(seq, xs_ready, 4 * (ln - 1) + 2 * hf + 2))
                for t in range(TH * hf, TH * hf + TH):
                    last = dve.bn_stats(stats[:, t], x[:, t, :])
                last.then_inc(stats_ready, 1)
                dve.wait_ge(stats_ready, nth(seq, stats_ready, n))
                dve.tensor_copy(count[:], stats[:, TH * hf, 0:1])
                for t in range(TH * hf, TH * hf + TH):
                    last = dve.bn_aggr(mv[:, t], stats[:, t])
                last.then_inc(mv_ready, 1)

            def shift_of(seq, ln, hf):
                n = 2 * ln + hf + 1
                t = slice(TH * hf, TH * hf + TH)
                dve.wait_ge(rstd_ready, nth(seq, rstd_ready, n))
                dve.scalar_tensor_tensor(neg_mr[:, t], mv[:, t, 0], -1.0, rstd[:, t], ALU.mult, ALU.mult)\
                    .then_inc(neg_mr_ready, 1)

            def ripple(seq):
                for buf in (kT, vT):
                    dve.memset(buf[:, :, 0:PAD], 0.0)
                dve.memset(fkv[:, :, :, 2 * P:2 * P + 1], 1.0).then_inc(pads_ready, 1)
                dve.wait_ge(pads_ready, nth(seq, pads_ready, 1))

                def scores(u):
                    hf, o = (0, u) if u < 10 else (1, u - 10)
                    a = HALF * hf
                    if u % 10 == 0 and u < 20:
                        dve.wait_ge(qkv_sb, nth(seq, qkv_sb, 6 * hf + 4))
                    if u >= 4:
                        dve.wait_ge(qk_summed, nth(seq, qk_summed, u - 3))
                    b = PAD + a - OFFS[o]
                    dve.tensor_tensor(prods[:, u % 4], qT[:, :, a:a + HALF], kT[:, :, b:b + HALF],
                                      ALU.mult).then_inc(qk_prod, 1)

                def elu(e):
                    hf, m = e // 4, e % 4
                    dst = (fkT if m < 2 else fqT)[:, m % 2, HALF * hf:HALF * hf + HALF]
                    dve.wait_ge(exp_ready, nth(seq, exp_ready, e + 1))
                    dve.scalar_tensor_tensor(dst, dst, 1.0, relus[:, e % 4], ALU.min, ALU.add)\
                        .then_inc(elu_ready, 1)

                def chained(hf, n, i):
                    i.then_inc(soft, 1)
                    dve.wait_ge(soft, nth(seq, soft, 15 * hf + n))

                def over_slots(hf, n, op, src, dst):
                    chained(hf, n, dve.tensor_tensor(smx[:, :, 0:48], src[:, :, 0:48], src[:, :, 48:96], op))
                    chained(hf, n + 1, dve.tensor_tensor(smx[:, :, 48:72], smx[:, :, 0:24], smx[:, :, 24:48], op))
                    chained(hf, n + 2, dve.tensor_tensor(smx[:, :, 72:80], smx[:, :, 48:56], smx[:, :, 56:64], op))
                    chained(hf, n + 3, dve.tensor_tensor(dst, smx[:, :, 72:80], smx[:, :, 64:72], op))

                def soft_max(hf):
                    t = slice(TH * hf, TH * hf + TH)
                    flat = sm[:, t].rearrange("p t s w -> p t (s w)")
                    bank = PS[:, 1].rearrange("p (t j w) -> p t j w", t=TH, j=NJ)
                    dve.wait_ge(stok_psum, nth(seq, stok_psum, hf + 1))
                    for s in range(NS):
                        last = dve.tensor_tensor(sm[:, t, s].rearrange("p t (j h) -> p t j h", j=NJ),
                                                 bank[:, :, :, s * H:s * H + H],
                                                 mask[:, t, s].rearrange("p t (j h) -> p t j h", j=NJ), ALU.add)
                    chained(hf, 1, last)
                    over_slots(hf, 2, ALU.max, flat, srec)
                    chained(hf, 6, dve.tensor_tensor(
                        flat.rearrange("p t (o h) -> p t o h", h=H), flat.rearrange("p t (o h) -> p t o h", h=H),
                        srec.unsqueeze(2).to_broadcast([P, TH, NS * NJ, H]), ALU.subtract))

                def soft_norm(hf):
                    t = slice(TH * hf, TH * hf + TH)
                    flat = sm[:, t].rearrange("p t s w -> p t (s w)")
                    dve.wait_ge(exps_ready, nth(seq, exps_ready, hf + 1))
                    over_slots(hf, 7, ALU.add, flat, srec)
                    chained(hf, 11, dve.reciprocal(srec, srec))
                    chained(hf, 12, dve.tensor_tensor(
                        flat.rearrange("p t (o h) -> p t o h", h=H), flat.rearrange("p t (o h) -> p t o h", h=H),
                        srec.unsqueeze(2).to_broadcast([P, TH, NS * NJ, H]), ALU.mult))

                def soft_low(hf):
                    t = slice(TH * hf, TH * hf + TH)
                    flat = sm[:, t].rearrange("p t s w -> p (t s) w")
                    parts = w3.rearrange("p t s q w -> p (t s) q w")
                    if hf == 1:
                        dve.wait_ge(w3T_psum, nth(seq, w3T_psum, 2))
                    dve.wait_ge(z_ready, nth(seq, z_ready, 2))
                    slot = LOW % NJ * H
                    chained(hf, 13, dve.tensor_copy(sm[:, t, LOW // NJ, slot:slot + H], zrec[:, t]))
                    dve.wait_ge(whi_ready, nth(seq, whi_ready, hf + 1))
                    chained(hf, 14, dve.tensor_tensor(wrest, flat, parts[:, :, 0], ALU.subtract))
                    dve.wait_ge(wmid_ready, nth(seq, wmid_ready, hf + 1))
                    chained(hf, 15, dve.tensor_tensor(parts[:, :, 2], wrest, parts[:, :, 1], ALU.subtract))

                def low_state():
                    dve.wait_ge(kv_psum, nth(seq, kv_psum, 1))
                    for c in range(NC):
                        dve.tensor_tensor(kvbd[:, c], PS[:, 2 + c, 0:P], sameheads[:], ALU.mult)
                        dve.tensor_scalar(zsel[:, c], headof[:, c], PS[:, 2 + c, P:P + 1], None, ALU.mult)\
                            .then_inc(kvbd_ready, 1)

                def low_z():
                    dve.wait_ge(z_psum, nth(seq, z_psum, 1))
                    dve.tensor_scalar(zrec, PS[:, 4, 0:T * H].rearrange("p (t h) -> p t h", t=T),
                                      1e-6, None, ALU.add).then_inc(z_ready, 1)
                    dve.wait_ge(z_ready, nth(seq, z_ready, 1))
                    dve.reciprocal(zrec, zrec).then_inc(z_ready, 1)

                def values(hf, o):
                    u = 12 * hf + o
                    a = HALF * hf
                    dve.wait_ge(wbc_psum, nth(seq, wbc_psum, u + 1))
                    if u >= NPROD:
                        v = u - NPROD
                        if v % 3 == 2:
                            dve.wait_ge(wv_acc, nth(seq, wv_acc, v // 3 + 1))
                        else:
                            dve.wait_ge(wv_pool, nth(seq, wv_pool, 2 * (v // 3) + v % 3 + 1))
                    pair = 4 + 2 * (u % 2)
                    dst = prods[:, u % NPROD]
                    if o == LOW:
                        dve.wait_ge(low_ready, nth(seq, low_ready, 4))
                        dve.tensor_tensor(dst, PS[:, pair:pair + 2], low_num[:, :, a:a + HALF], ALU.mult)\
                            .then_inc(wv_prod, 1)
                        return
                    if o == 0 and hf == 0:
                        dve.wait_ge(qkv_sb, nth(seq, qkv_sb, 12))
                    b = PAD + a - OFFS[o]
                    if OFFS[o] < KCONV:
                        j = KCONV - 1 - OFFS[o]
                        dve.scalar_tensor_tensor(dst[:, 0], PS[:, pair], conv_a[:, 0, j:j + 1],
                                                 vT[:, 0, b:b + HALF], ALU.add, ALU.mult)
                        dve.scalar_tensor_tensor(dst[:, 1], PS[:, pair + 1], conv_a[:, 1, j:j + 1],
                                                 vT[:, 1, b:b + HALF], ALU.add, ALU.mult)\
                            .then_inc(wv_prod, 1)
                    else:
                        dve.tensor_tensor(dst, PS[:, pair:pair + 2], vT[:, :, b:b + HALF], ALU.mult)\
                            .then_inc(wv_prod, 1)

                for u in range(21):
                    scores(u)
                    if u < 4:
                        elu(u)
                    if 10 <= u < 14:
                        elu(u - 6)
                    if u == 14:
                        soft_max(0)
                    if u == 16:
                        soft_norm(0)
                    if u == 18:
                        low_state()
                low_z()
                soft_low(0)
                soft_max(1)
                for o in range(NO + 1):
                    values(0, o)
                    if o == 1:
                        soft_norm(1)
                    if o == 3:
                        soft_low(1)
                for o in range(NO + 1):
                    values(1, o)

            def residual(seq, layer, tp, psum, ready, bank):
                dve.wait_ge(ready, nth(seq, ready, tp + 1))
                if layer == 0:
                    dve.wait_ge(xh_ready, nth(seq, xh_ready, 2))
                x = xs[:, 2 * tp:2 * tp + 2, :]
                dve.tensor_tensor(x, x, PS[:, bank].rearrange("p (t c) -> p t c", t=2), ALU.add)\
                    .then_inc(xs_ready, 1)

            def ffn(seq, f):
                for hf in range(2):
                    a = HALF * hf
                    for which, (mu, dst, done) in enumerate(((mu_k, xkT, xk_ready), (mu_r, xrT, xr_ready))):
                        for c in range(NC):
                            dve.wait_ge(d_ready, nth(seq, d_ready, 4 * f + 2 * hf + c + 1))
                            dve.scalar_tensor_tensor(dst[:, c, a:a + HALF], dT[:, c, a:a + HALF],
                                                     mu[:, c:c + 1], hT[:, c, a:a + HALF], ALU.mult, ALU.add)\
                                .then_inc(done, 1)

            def ffn_out(seq, f, tp):
                n = 4 * f + tp + 1
                dve.wait_ge(gate_ready, nth(seq, gate_ready, n))
                dve.wait_ge(v_psum, nth(seq, v_psum, n))
                dve.scalar_tensor_tensor(gated[:, tp], gate[:, tp], 1.0, PS[:, 4 + tp], ALU.add, ALU.mult)\
                    .then_inc(gated_ready, 1)
                dve.wait_ge(gated_ready, nth(seq, gated_ready, n))
                t = slice(2 * tp, 2 * tp + 2)
                add = gated[:, tp].rearrange("p (t c) -> p t c", t=2)
                if f == 0:
                    dve.tensor_tensor(xs[:, t, :], xs[:, t, :], add, ALU.add).then_inc(xs_ready, 1)
                else:
                    dve.tensor_tensor(x_out[:, t, :], xs[:, t, :], add, ALU.add).then_inc(out_ready, 1)

            def phase(seq):
                dve.memset(z_raw[:, :, 0:KS - 1], 0.0)
                dve.memset(zs_raw[:, 0:KS - 1], 0.0).then_inc(zpads_ready, 1)
                dve.wait_ge(zpads_ready, nth(seq, zpads_ready, 1))
                dve.wait_ge(z_sb, nth(seq, z_sb, 2))
                for j in range(KS - 1):
                    dve.scalar_tensor_tensor(zs, zs_raw[:, j:j + S], conv_bs[:, j:j + 1], zs, ALU.mult, ALU.add)\
                        .then_inc(sconv, 1)
                    dve.wait_ge(sconv, nth(seq, sconv, j + 1))
                dve.tensor_scalar(zs, zs, score_scale[:], 20.0, ALU.mult, ALU.min).then_inc(sconv, 1)
                dve.wait_ge(sconv, nth(seq, sconv, 4))
                dve.scalar_tensor_tensor(zs, zs, -20.0, log_time[:], ALU.max, ALU.add).then_inc(sconv, 1)
                for j in range(KS - 1):
                    for c in range(NC):
                        n = 2 * j + c + 1
                        if j == 0:
                            dve.wait_ge(z_sb, nth(seq, z_sb, 2 * c + 4))
                        else:
                            dve.wait_ge(kconv, nth(seq, kconv, n - 2))
                        dve.scalar_tensor_tensor(zc[:, c], z_raw[:, c, j:j + S], conv_bk[:, c, j:j + 1], zc[:, c],
                                                 ALU.mult, ALU.add).then_inc(kconv, 1)
                dve.wait_ge(phi_ready, nth(seq, phi_ready, 1))
                for q in (1, 2):
                    r = slice(32 * q, 32 * q + 32)
                    rest = dve.tensor_tensor(prest[r], pw[r], p3[r], ALU.subtract)
                rest.then_inc(prest_ready, 1)
                dve.tensor_tensor_scan(den, pw, pw, 0.0, ALU.add, ALU.bypass).then_inc(den_step, 1)
                dve.wait_ge(den_step, nth(seq, den_step, 1))
                for q in range(4):
                    r = slice(32 * q, 32 * q + 32)
                    last = dve.tensor_scalar(den_inv[r], den[r, 256 * q:256 * q + 256], 0.0001, None, ALU.max)
                last.then_inc(den_step, 1)
                dve.wait_ge(pmid_ready, nth(seq, pmid_ready, 1))
                dve.tensor_tensor(p3[64:96], prest[64:96], p3[64:96], ALU.subtract).then_inc(p3_ready, 1)
                dve.wait_ge(den_step, nth(seq, den_step, 2))
                dve.reciprocal(den_inv, den_inv).then_inc(den_step, 1)

                def turn(n):
                    a = 2 * (n % 2)
                    dve.wait_ge(turn_rounded, nth(seq, turn_rounded, n + 1))
                    t = turns[:, n % 2].rearrange("p (b n) -> p b n", b=2)
                    dve.scalar_tensor_tensor(t, t, -ROUND, PS[:, a:a + 2], ALU.add, ALU.subtract)\
                        .then_inc(turn_ready, 1)

                turn(0)
                for n, i in enumerate(ORDER):
                    if n + 1 < NPAIR:
                        turn(n + 1)
                    g = nums[:, n % NNUM]
                    dve.wait_ge(trig_ready, nth(seq, trig_ready, n + 1))
                    dve.wait_ge(pbc_psum, nth(seq, pbc_psum, n + 1))
                    if n >= NNUM:
                        dve.wait_ge(y_psum, nth(seq, y_psum, n - NNUM + 1))
                    if n == 0:
                        dve.wait_ge(den_step, nth(seq, den_step, 3))
                        dve.wait_ge(p3_ready, nth(seq, p3_ready, 1))
                    for a in range(2):
                        last = dve.tensor_tensor(g[:, a].rearrange("p (b n) -> p b n", b=2),
                                                 trig[:, n % 2, a].rearrange("p (b n) -> p b n", b=2),
                                                 PS[:, 4:6], ALU.mult)
                    last.then_inc(weighted, 1)
                    dve.wait_ge(weighted, nth(seq, weighted, n + 1))
                    for a in range(2):
                        last = dve.tensor_tensor_scan(g[:, a], g[:, a], g[:, a], 0.0, ALU.add, ALU.bypass)
                    last.then_inc(num_ready, 1)
                    dve.wait_ge(num_ready, nth(seq, num_ready, n + 1))
                    dve.tensor_tensor(g[:, 1], g[:, 1], qpT[:, 2 * (i // 4) + 1], ALU.mult)\
                        .then_inc(prod_im, 1)
                for n in range(4):
                    c, a = n // 2, HALF * (n % 2)
                    dve.wait_ge(y_sb, nth(seq, y_sb, n + 1))
                    dve.wait_ge(ibc_psum, nth(seq, ibc_psum, n + 1))
                    dve.tensor_tensor(yT[:, c, a:a + HALF], yT[:, c, a:a + HALF], PS[:, n], ALU.mult)\
                        .then_inc(yn_ready, 1)
                for n in range(4):
                    c, a = n // 2, HALF * (n % 2)
                    dve.wait_ge(tanh_ready, nth(seq, tanh_ready, n + 1))
                    dve.scalar_tensor_tensor(yT[:, c, a:a + HALF], thT[:, c, a:a + HALF], 1.0,
                                             yT[:, c, a:a + HALF], ALU.add, ALU.mult).then_inc(ys_ready, 1)

            with dve.Fori(0, NSEQ) as seq:
                moments(seq, 0, x_in, 0)
                moments(seq, 0, x_in, 1)
                shift_of(seq, 0, 0)
                shift_of(seq, 0, 1)
                ripple(seq)
                for tp in range(4):
                    residual(seq, 0, tp, PS, wo_psum, tp % 2)
                    if tp == 1:
                        moments(seq, 1, xs, 0)
                moments(seq, 1, xs, 1)
                shift_of(seq, 1, 0)
                shift_of(seq, 1, 1)
                ffn(seq, 0)
                for tp in range(4):
                    ffn_out(seq, 0, tp)
                    if tp == 1:
                        moments(seq, 2, xs, 0)
                moments(seq, 2, xs, 1)
                shift_of(seq, 2, 0)
                shift_of(seq, 2, 1)
                phase(seq)
                for tp in range(4):
                    residual(seq, 2, tp, PS, wout_psum, 4 + tp)
                    if tp == 1:
                        moments(seq, 3, xs, 0)
                moments(seq, 3, xs, 1)
                shift_of(seq, 3, 0)
                shift_of(seq, 3, 1)
                ffn(seq, 1)
                for tp in range(4):
                    ffn_out(seq, 1, tp)

        @block.tensor
        def _(pe):
            pe.wait_ge(prologue, step[0])
            pe.wait_ge(pro_pool, 1)

            def transpose_h(seq, ln):
                for hf in range(2):
                    pe.wait_ge(h_ready, nth(seq, h_ready, T * ln + TH * hf + TH))
                    for c in range(NC):
                        for t in range(TH):
                            last = pe.transpose(PS[:, 2 * hf + c, P * t:P * t + P],
                                                h[:, TH * hf + t, P * c:P * c + P], ident[:])
                        last.then_inc(hT_psum, 1)

            def project(bank, weight, hf, src=None, lead=1):
                src = hT if src is None else src
                a = lead + HALF * hf
                for c in range(NC):
                    last = pe.matmul(PS[:, bank], weight[:, c], src[:, c, a:a + HALF],
                                     start=(c == 0), stop=(c == NC - 1))
                return last

            def project_tokens(bank, tp, src, weight):
                for t in range(2):
                    for c in range(NC):
                        a = P * (2 * tp + t)
                        last = pe.matmul(PS[:, bank, C * t:C * t + C], src[:, c, a:a + P], weight[:, c, :],
                                         start=(c == 0), stop=(c == NC - 1))
                return last

            def ripple(seq):
                def qkv(n):
                    hf, m = n // 6, n % 6
                    col = (C, C + P, 0, P, 2 * C, 2 * C + P)[m]
                    if m == 0:
                        pe.wait_ge(hT_ready, nth(seq, hT_ready, 2 * hf + 2))
                    if n >= 4:
                        pe.wait_ge(qkv_sb, nth(seq, qkv_sb, n - 3))
                    project(4 + n % 4, wqkv[:, :, col:col + P], hf).then_inc(qkv_psum, 1)

                def scores(us):
                    hf = 0 if us[0] < 10 else 1
                    if us[0] == 10:
                        pe.wait_ge(sT_ready, nth(seq, sT_ready, 1))
                    for c in range(NC):
                        for u in us:
                            o = u - 10 * hf
                            j, s = o % NJ, o // NJ
                            if c == 0:
                                pe.wait_ge(qk_prod, nth(seq, qk_prod, u + 1))
                            last_o = j + NJ * ((9 + hf - j) // NJ)
                            mm = pe.matmul(PS[32 * j:32 * j + 32, 0], headsum[:, s, c], prods[:, u % 4, c],
                                           start=(o < NJ and c == 0), stop=(o == last_o and c == NC - 1))
                            if c == NC - 1:
                                mm.then_inc(qk_summed, 1)

                def scores_to_tokens(hf):
                    pe.wait_ge(sT_ready, nth(seq, sT_ready, hf + 1))
                    if hf == 1:
                        pe.wait_ge(w3T_ready, nth(seq, w3T_ready, 2))
                    for t in range(TH):
                        last = pe.transpose(PS[:, 1, P * t:P * t + P], sT[:, P * t:P * t + P], ident[:])
                    last.then_inc(stok_psum, 1)

                def fkv_tile(t):
                    pe.wait_ge(elu_ready, nth(seq, elu_ready, 4 * (t // TH) + 2))
                    if t == 0:
                        pe.wait_ge(qkv_sb, nth(seq, qkv_sb, 12))
                    if t >= 4:
                        pe.wait_ge(fkv_ready, nth(seq, fkv_ready, t - 3))
                    a = P * t
                    for c in range(NC):
                        pe.transpose(PS[:, 4 + t % 4, 2 * P * c:2 * P * c + P], fkT[:, c, a:a + P], ident[:])
                        last = pe.transpose(PS[:, 4 + t % 4, 2 * P * c + P:2 * P * c + 2 * P],
                                            vT[:, c, PAD + a:PAD + a + P], ident[:])
                    last.then_inc(fkv_psum, 1)

                def kv_sum():
                    pe.wait_ge(fkv_ready, nth(seq, fkv_ready, T))
                    for c in range(NC):
                        for t in range(T):
                            last = pe.matmul(PS[:, 2 + c, 0:P + 1], fkv[:, t, c, 0:P], fkv[:, t, c, P:2 * P + 1],
                                             start=(t == 0), stop=(t == T - 1))
                    last.then_inc(kv_psum, 1)

                def low_z():
                    pe.wait_ge(kvbd_ready, nth(seq, kvbd_ready, 2))
                    pe.wait_ge(elu_ready, nth(seq, elu_ready, 8))
                    for t in range(T):
                        for c in range(NC):
                            last = pe.matmul(PS[:, 4, H * t:H * t + H], fqT[:, c, P * t:P * t + P], zsel[:, c],
                                             start=(c == 0), stop=(c == NC - 1))
                    last.then_inc(z_psum, 1)

                def low(n):
                    c, hf = n % 2, n // 2
                    if n == 3:
                        pe.wait_ge(z_ready, nth(seq, z_ready, 1))
                    pe.matmul(PS[:, 4 + (n + 1) % 4], kvbd[:, c], fqT[:, c, HALF * hf:HALF * hf + HALF],
                              start=True, stop=True).then_inc(low_psum, 1)

                def weights_to_channels(hf):
                    pe.wait_ge(soft, nth(seq, soft, 15 * hf + 15))
                    bank = PS[0:96, 1].bitcast(bf16).rearrange("p (s n) -> p s n", s=2)
                    for s in range(NS):
                        if s == 2:
                            pe.wait_ge(w3T_ready, nth(seq, w3T_ready, 2 * hf + 1))
                        for t in range(TH):
                            last = pe.transpose(bank[:, s % 2, P * t:P * t + P],
                                                w3[:, t, s].rearrange("p q w -> p (q w)"), ident_b[:])
                        if s > 0:
                            last.then_inc(w3T_psum, 1)

                def spread_weight(hf, o):
                    u = 12 * hf + o
                    if o == 0:
                        pe.wait_ge(w3T_ready, nth(seq, w3T_ready, 2 * hf + 2))
                        if hf == 0:
                            pe.wait_ge(low_ready, nth(seq, low_ready, 4))
                    if u >= 2:
                        pe.wait_ge(wv_prod, nth(seq, wv_prod, u - 1))
                    for c in range(NC):
                        last = pe.matmul(PS[:, 4 + 2 * (u % 2) + c], spread[:, o % NJ, c], w3T[:, o // NJ],
                                         start=True, stop=True)
                    last.then_inc(wbc_psum, 1)

                def taps(hf):
                    if hf == 0:
                        pe.wait_ge(kvbd_ready, nth(seq, kvbd_ready, 2))
                    else:
                        pe.wait_ge(hsumT_ready, nth(seq, hsumT_ready, 2))
                    for n, tap in enumerate(TAPS):
                        for c in range(NC):
                            b = PAD + HALF * hf - tap
                            pe.matmul(PS[:, 2 + c], tap_w[:, n, c], vT[:, c, b:b + HALF],
                                      start=(n == 0), stop=False)

                def accumulate(hf, g):
                    pe.wait_ge(wv_pool, nth(seq, wv_pool, 8 * hf + 2 * g + 2))
                    u = 12 * hf + 3 * g + 2
                    for c in range(NC):
                        last = pe.matmul(PS[:, 2 + c], ident[:], prods[:, u % NPROD, c], start=False, stop=(g == 3))
                    last.then_inc(wv_acc, 1)

                def out_tokens(tp):
                    pe.wait_ge(hsumT_ready, nth(seq, hsumT_ready, 2 * (tp // 2) + 2))
                    if tp >= 2:
                        pe.wait_ge(xs_ready, nth(seq, xs_ready, tp - 1))
                    project_tokens(tp % 2, tp, hsumT, wo).then_inc(wo_psum, 1)

                for n in range(6):
                    qkv(n)
                for p in range(5):
                    scores((2 * p, 2 * p + 1))
                    qkv(6 + p)
                qkv(11)
                for p in range(5):
                    scores((10 + 2 * p, 11 + 2 * p))
                    if p == 0:
                        scores_to_tokens(0)
                        for t in range(4):
                            fkv_tile(t)
                    if p == 1:
                        for t in range(4, T):
                            fkv_tile(t)
                    if p == 2:
                        kv_sum()
                scores((20,))
                low_z()
                for n in range(4):
                    low(n)
                weights_to_channels(0)
                taps(0)
                spread_weight(0, 0)
                spread_weight(0, 1)
                scores_to_tokens(1)
                for o in range(2, NO + 1):
                    spread_weight(0, o)
                    if o % 3 == 2 and o > 2:
                        accumulate(0, o // 3 - 1)
                weights_to_channels(1)
                accumulate(0, 3)
                taps(1)
                for o in range(NO + 1):
                    spread_weight(1, o)
                    if o % 3 == 2 and o > 2:
                        accumulate(1, o // 3 - 1)
                accumulate(1, 3)
                for tp in range(4):
                    out_tokens(tp)

            def ffn(seq, f):
                for hf in range(2):
                    pe.wait_ge(xk_ready, nth(seq, xk_ready, 4 * f + 2 * hf + 2))
                    for m in range(NC):
                        project(4 + 2 * hf + m, wk[:, :, P * m:P * m + P], hf, xkT, 0).then_inc(k_psum, 1)
                for tp in range(4):
                    pe.wait_ge(xr_ready, nth(seq, xr_ready, 4 * f + 2 * (tp // 2) + 2))
                    if tp == 0:
                        pe.wait_ge(hT_ready, nth(seq, hT_ready, 4 * (1 + 2 * f) + 4))
                    project_tokens(tp, tp, xrT, wr).then_inc(r_psum, 1)
                for tp in range(4):
                    pe.wait_ge(kact_ready, nth(seq, kact_ready, 4 * f + 4))
                    project_tokens(4 + tp, tp, kact, wv).then_inc(v_psum, 1)

            def phase(seq):
                for n in range(22):
                    hf = n % 2
                    if n < 2:
                        weight = w_in_s[:].rearrange("p c r k -> p c (r k)")
                    elif n < 6:
                        c = (n - 2) // 2
                        weight = w_in_k[:, :, P * c:P * c + P]
                    else:
                        weight = w_in_q[:, :, (n - 6) // 2].rearrange("p c r f -> p c (r f)")
                    pe.wait_ge(hT_ready, nth(seq, hT_ready, 8 + 2 * hf + 2))
                    if n >= 4:
                        pe.wait_ge(z_sb, nth(seq, z_sb, n - 3))
                    project(4 + n % 4, weight, hf).then_inc(z_out, 1)

                def turn(n):
                    i = ORDER[n]
                    if n == 0:
                        pe.wait_ge(kconv, nth(seq, kconv, 6))
                    if n >= 2:
                        pe.wait_ge(turn_ready, nth(seq, turn_ready, n - 1))
                    for hf in range(2):
                        last = pe.matmul(PS[:, 2 * (n % 2) + hf], theta_w[:, i // 8, i % 8],
                                         zc[:, i // 8, HALF * hf:HALF * hf + HALF], start=True, stop=True)
                    last.then_inc(turn_psum, 1)

                def spread_decay(n):
                    if n == 0:
                        pe.wait_ge(p3_ready, nth(seq, p3_ready, 1))
                        pe.wait_ge(z_sb, nth(seq, z_sb, 22))
                    else:
                        pe.wait_ge(weighted, nth(seq, weighted, n))
                    for hf in range(2):
                        last = pe.matmul(PS[:, 4 + hf], pairof[:, ORDER[n]], p3[0:96, HALF * hf:HALF * hf + HALF],
                                         start=True, stop=True)
                    last.then_inc(pbc_psum, 1)

                def head_sums(n):
                    units = ((n, ORDER[n]), (n + 1, ORDER[n + 1]))
                    c = ORDER[n] // 8
                    if n == 8:
                        pe.wait_ge(y_sb, nth(seq, y_sb, 2))
                    for part, done in ((0, prod_re), (1, prod_im)):
                        pe.wait_ge(done, nth(seq, done, n + 2))
                        for hf in range(2):
                            for m, i in units:
                                g = 32 * (i % 8 // 2)
                                mm = pe.matmul(PS[g:g + 32, 6 + hf], phasesum[:, i % 2],
                                               nums[:, m % NNUM, part, HALF * hf:HALF * hf + HALF],
                                               start=(i % 2 == 0 and part == 0), stop=(i % 2 == 1 and part == 1))
                                if part == 1 and hf == 1:
                                    mm.then_inc(y_psum, 1)

                turn(0)
                turn(1)
                for n in range(NPAIR):
                    spread_decay(n)
                    if n + 2 < NPAIR:
                        turn(n + 2)
                    if n % 2 == 1 and n >= 3:
                        head_sums(n - 3)
                head_sums(NPAIR - 2)
                pe.wait_ge(turn_ready, nth(seq, turn_ready, NPAIR))
                for n in range(4):
                    c, hf = n // 2, n % 2
                    for b in range(2):
                        q = 2 * hf + b
                        last = pe.matmul(PS[:, n, 256 * b:256 * b + 256], kernelof[:, q, c], den_inv,
                                         start=True, stop=True)
                    last.then_inc(ibc_psum, 1)
                pe.wait_ge(y_sb, nth(seq, y_sb, 4))
                for tp in range(4):
                    pe.wait_ge(ys_ready, nth(seq, ys_ready, 4))
                    project_tokens(4 + tp, tp, yT, w_out).then_inc(wout_psum, 1)

            with pe.Fori(0, NSEQ) as seq:
                transpose_h(seq, 0)
                ripple(seq)
                transpose_h(seq, 1)
                ffn(seq, 0)
                transpose_h(seq, 2)
                phase(seq)
                transpose_h(seq, 3)
                ffn(seq, 1)


_WEIGHTS = {
    "Wqkv": "L0_attn_a_Wqkv", "Wo": "L0_attn_a_Wo", "conv_w": "L0_attn_a_conv_w",
    "W_in": "L0_attn_b_W_in", "W_out": "L0_attn_b_W_out", "mu_r": "L0_ffn_mu_r", "mu_k": "L0_ffn_mu_k",
}


def kernel(**inputs):
    import numpy as _np
    import concourse.bacc as _bacc
    from concourse import mybir as _mybir
    from concourse.bass_utils import run_bass_kernel_spmd as _run

    get = lambda name: _np.asarray(inputs[name])
    weights = {name: get(full) for name, full in _WEIGHTS.items()}
    for name in ("W_r", "W_k", "W_v"):
        weights[name.replace("_", "") + "T"] = get("L0_ffn_" + name).T
    for name in ("mu_r", "mu_k"):
        weights[name] = weights[name][:, None]
    weights["conv_kT"] = get("L0_attn_b_conv_k")[:, 0, :].T
    weights["theta"] = get("L0_attn_b_theta").reshape(C, M2)
    weights["slopes"] = _np.concatenate([get("L0_attn_b_decay_slopes"), get("L0_attn_b_anchor_slopes")])[:, None]
    weights["score_scale"] = get("L0_attn_b_score_scale")[:, None]
    weights["norm_scale_re"] = get("L0_attn_b_norm_scale")[None, :H2]
    weights["norm_scale_im"] = get("L0_attn_b_norm_scale")[None, H2:]
    weights["diag_re"] = _np.diagonal(get("L0_attn_b_W_re"))[None, :]
    weights["diag_im"] = _np.diagonal(get("L0_attn_b_W_im"))[None, :]

    nc = _bacc.Bacc("TRN2", target_bir_lowering=False, num_devices=1)
    arrays = {}

    def dram(name, a):
        a = _np.ascontiguousarray(a)
        arrays[name] = a
        return nc.dram_tensor(name, a.shape, _mybir.dt.from_np(a.dtype), kind="ExternalInput").ap()

    w = {name: dram(f"in_{name}_dram", a) for name, a in weights.items()}
    k = {name: dram(f"const_{name}_dram", a) for name, a in constants().items()}
    x = dram("in_x_dram", inputs["L0_attn_a_x"])
    out = nc.dram_tensor("out_0_dram", (NSEQ, S, C), _mybir.dt.float32, kind="ExternalOutput").ap()
    build(nc, w, k, x, out)
    r = _run(nc, [arrays], core_ids=[0])
    return r.results[0]["out_0_dram"]
```

```python
import concourse.bass as bass
from concourse import mybir
from contextlib import ExitStack

import numpy as np

P = 128
NSEQ, S, C = 8, 1024, 256
T = S // P
HALF = 512
TH = T // 2
NC = C // P
H = 8
D = C // H
OFFS = [0] + [2 ** n for n in range(10)]
NO = len(OFFS)
LOW = NO
NJ, NS = 4, 3
PAD = 512
KCONV = 7
TAPS = [t for t in range(KCONV) if t not in OFFS]
NTAP = len(TAPS)
K2, H2, M2, KQ = 32, 8, 8, 4
NPROJ = 6 + 2 * KQ
EXP_AT, HIGH_AT = 8, 11
NPAIR = K2 // 2
KS = 4
NDECAY = 28
EPS = 1e-5
LOG_MIN = -85.0
ROUND = 12582912.0
TWO_PI = 6.283185
OWN_FIRST = (1, 3)
ORDER = [8 * c + u for c in range(2) for u in (0, 2, 1, 3, 4, 6, 5, 7)]


def pool_adds(group):
    return sum(1 if g % 4 in OWN_FIRST else 2 for g in range(group + 1))


def own_adds(group):
    return sum(g % 4 in OWN_FIRST for g in range(group + 1))


def constants():
    f, p = np.arange(P), np.arange(P)[:, None]
    ident = np.eye(P, dtype=np.float32)
    headsum = np.zeros((P, NS, NC, 32), np.float32)
    spread = np.zeros((3, NJ, H, NJ, NC, P), np.float32)
    for s in range(NS):
        for c in range(NC):
            headsum[f, s, c, s * H + c * (H // NC) + f // D] = 1.0
    for j in range(NJ):
        for c in range(NC):
            spread[:, j, c * (H // NC) + f // D, j, c, f] = 1.0
    spread = spread.reshape(3 * NJ * H, NJ * NC * P)
    mask = np.zeros((P, T, NS, NJ, H), np.float32)
    time = (np.arange(T)[None, :] * P + np.arange(P)[:, None])
    for o in range(NS * NJ):
        bad = time < OFFS[o] if o < NO else time >= 0
        mask[:, :, o // NJ, o % NJ, :] = np.where(bad, -1e30, 0.0)[:, :, None]
    sameheads = (p // D == f[None, :] // D).astype(np.float32)
    headof = np.zeros((P, NC, 32), np.float32)
    for c in range(NC):
        headof[:, c, :] = np.arange(32)[None, :] // (32 // H) == c * (H // NC) + p // D
    pairof = np.zeros((3, K2, NPAIR, P), np.float32)
    for i in range(NPAIR):
        pairof[:, 2 * i + f // 64, i, f] = 1.0
    pairof = pairof.reshape(3 * K2, NPAIR * P)
    phasesum = np.zeros((P, 2, 32), np.float32)
    for par in range(2):
        phasesum[f, par, par * 16 + f // M2] = 1.0
    kernelof = np.zeros((P, 4, 2, P), np.float32)
    for c in range(2):
        for q in range(4):
            kernelof[32 * q + 16 * c + f // H2, q, c, f] = 1.0
    t = np.arange(S, dtype=np.float32)
    dist = np.where(np.arange(K2)[:, None] < NDECAY, S - 1 - t, t).astype(np.float32)
    is_decay = (np.arange(P)[:, None] % K2 < NDECAY).astype(np.float32)
    kind = np.concatenate([is_decay, 1 - is_decay, -is_decay], axis=1)
    return dict(ident=ident, kind=kind, headsum=headsum.reshape(P, -1), spread=spread, mask=mask.reshape(P, -1),
                sameheads=sameheads, headof=headof.reshape(P, -1), pairof=pairof,
                phasesum=phasesum.reshape(P, -1), kernelof=kernelof.reshape(P, -1),
                dist=np.tile(dist, (4, 1)))


def build(nc, w, k, x_dram, out_dram):
    fp32, bf16 = mybir.dt.float32, mybir.dt.bfloat16
    ALU, ACT, AX = mybir.AluOpType, mybir.ActivationFunctionType, mybir.AxisListType.X
    ctx = ExitStack()
    with ctx:
        def sb(name, shape, dt=fp32):
            return ctx.enter_context(nc.sbuf_tensor(name, shape, dt))

        per, names = {}, {}

        def sem(name, per_sequence=0):
            s = ctx.enter_context(nc.semaphore(name))
            per[name] = per_sequence
            names[id(s)] = name
            return s

        def nth(seq, s, n):
            return seq * per[names[id(s)]] + n

        ident = sb("ident", [P, P])
        ident_b = sb("ident_b", [P, P], bf16)
        headsum = sb("headsum", [P, NS, NC, 32])
        spread = sb("spread", [96, NJ, NC, P], bf16)
        mask = sb("mask", [P, T, NS, NJ * H])
        sameheads = sb("sameheads", [P, P])
        headof = sb("headof", [P, NC, 32])
        pairof = sb("pairof", [96, NPAIR, P], bf16)
        phasesum = sb("phasesum", [P, 2, 32])
        kernelof = sb("kernelof", [P, 4, 2, P])
        log_time = sb("log_time", [P, S])
        wqkv = sb("wqkv", [P, NC, 3 * C])
        wo = sb("wo", [P, NC, C])
        wr = sb("wr", [P, NC, C])
        wk = sb("wk", [P, NC, C])
        wv = sb("wv", [P, NC, C])
        w_in_k = sb("w_in_k", [P, NC, C])
        w_in_s = sb("w_in_s", [P, NC, 4, K2])
        w_in_q = sb("w_in_q", [P, NC, KQ, 2, 64])
        w_out = sb("w_out", [P, NC, C])
        theta_w = sb("theta_w", [P, NC, 8, P])
        tap_w = sb("tap_w", [P, NTAP, NC, P])
        conv_a = sb("conv_a", [P, NC, KCONV])
        conv_bk = sb("conv_bk", [P, NC, KS])
        conv_bs = sb("conv_bs", [P, KS])
        mu_r = sb("mu_r", [P, NC])
        mu_k = sb("mu_k", [P, NC])
        theta = sb("theta", [P, NC, M2])
        slope = sb("slope", [P, 8])
        score_scale = sb("score_scale", [P, 1])
        gains = sb("gains", [P, 6, H2])
        kind = sb("kind", [P, 3])
        half_pi = sb("half_pi", [P, 1])
        round_c = sb("round_c", [P, 1])
        minus_half = sb("minus_half", [P, TH])
        eps = sb("eps", [P, TH])

        x_in = sb("x_in", [P, T, C])
        xs = sb("xs", [P, T, C])
        h = sb("h", [P, T, C])
        x_out = h
        hT = sb("hT", [P, NC, 1 + S])
        stats = sb("stats", [P, T, 6])
        mv = sb("mv", [P, T, 2])
        rstd = sb("rstd", [P, T])
        veps = sb("veps", [P, T])
        count = sb("count", [P, 1])
        neg_mr = sb("neg_mr", [P, T])

        ARENA = 28480
        arena = sb("arena", [P, ARENA])
        top = [0]

        def take(cols):
            a = arena[:, top[0]:top[0] + cols]
            top[0] += cols
            assert top[0] <= ARENA, top[0]
            return a

        qT = take(NC * S).rearrange("p (c n) -> p c n", c=NC)
        kT = take(NC * (PAD + S)).rearrange("p (c n) -> p c n", c=NC)
        vT = take(NC * (PAD + S)).rearrange("p (c n) -> p c n", c=NC)
        fqT = take(NC * S).rearrange("p (c n) -> p c n", c=NC)
        fkT = take(NC * S).rearrange("p (c n) -> p c n", c=NC)
        low_num = fkT
        hsumT = qT
        relus = take(4 * HALF).rearrange("p (r n) -> p r n", r=4)
        FKV = 2 * P + 1
        fkv = take(T * NC * FKV).rearrange("p (t c n) -> p t c n", t=T, c=NC)
        NPROD = 6
        prods = take(NPROD * NC * HALF).rearrange("p (r c n) -> p r c n", r=NPROD, c=NC)
        sT = take(HALF)
        sm = take(T * 96).rearrange("p (t s w) -> p t s w", t=T, s=NS)
        smx = take(TH * (4 * 32)).rearrange("p (t w) -> p t w", t=TH)
        srec = take(TH * H).rearrange("p (t w) -> p t w", t=TH)
        zrec = take(S // 4)
        wrest = take(TH * 96).rearrange("p (t w) -> p t w", t=TH * NS)
        kvbd = take(NC * P).rearrange("p (c n) -> p c n", c=NC)
        zsel = take(NC * 32).rearrange("p (c n) -> p c n", c=NC)
        w3 = take(TH * NS * 96 // 2).bitcast(bf16).rearrange("p (t s q w) -> p t s q w", t=TH, s=NS, q=3)
        w3T = relus.rearrange("p r n -> p (r n)")[:, 0:NS * HALF].bitcast(bf16)\
            .rearrange("p (f s n) -> p f s n", f=2, s=NS)[0:96]
        top[0] = 0
        dT = take(NC * S).rearrange("p (c n) -> p c n", c=NC)
        xkT = take(NC * S).rearrange("p (c n) -> p c n", c=NC)
        xrT = take(NC * S).rearrange("p (c n) -> p c n", c=NC)
        kact = take(NC * S).rearrange("p (c n) -> p c n", c=NC)
        gate = take(4 * HALF).rearrange("p (r n) -> p r n", r=4)
        gated = take(4 * HALF).rearrange("p (r n) -> p r n", r=4)
        top[0] = 0
        ZP = KS - 1 + S
        z_raw = take(NC * ZP).rearrange("p (c n) -> p c n", c=NC)
        yT = z_raw[:, :, 0:S]
        zc = take(NC * S).rearrange("p (c n) -> p c n", c=NC)
        qpT = take(2 * KQ * S).rearrange("p (q n) -> p q n", q=2 * KQ)
        turns = take(2 * S).rearrange("p (r n) -> p r n", r=2)
        trig = take(2 * 2 * S).rearrange("p (r a n) -> p r a n", r=2, a=2)
        NNUM = 4
        nums = take(NNUM * 2 * S).rearrange("p (r a n) -> p r a n", r=NNUM, a=2)
        p3 = take(S // 2).bitcast(bf16)
        den_inv = take(S // 4)
        p_back = take(S // 4)
        thT = trig[:, 0]
        zs_raw = nums[:, 0].rearrange("p a n -> p (a n)")[:, 0:ZP]
        zs = nums[:, 1, 0]
        pz = nums[:, 2].rearrange("p a n -> p (a n)")[:, 0:1 + S]
        pw = pz[:, 1:1 + S]
        ratio = nums[:, 0, 0]
        p_inv = nums[:, 0, 1]
        prest = nums[:, 3, 0]
        den = nums[:, 3, 1]
        p_anchor = trig[:, 0, 0]
        top[0] = 0
        wq_raw = take(NC * 512).rearrange("p (c n) -> p c n", c=NC)
        spread_f = take(NJ * NC * P)[0:96]
        pairof_f = take(NPAIR * P)[0:96]

        PS = ctx.enter_context(nc.psum_tensor("PS", [P, 8, HALF], fp32))

        weights_in = sem("weights_in")
        prologue = sem("prologue")
        pro_act = sem("pro_act")
        pro_pool = sem("pro_pool")
        x_loaded = sem("x_loaded", 16)
        out_stored = sem("out_stored", 16)
        stats_ready = sem("stats_ready", 8)
        mv_ready = sem("mv_ready", 8)
        veps_ready = sem("veps_ready", 8)
        rstd_ready = sem("rstd_ready", 8)
        neg_mr_ready = sem("neg_mr_ready", 8)
        h_ready = sem("h_ready", 32)
        hT_psum = sem("hT_psum", 16)
        hT_ready = sem("hT_ready", 16)
        xs_ready = sem("xs_ready", 12)
        out_ready = sem("out_ready", 4)
        qkv_psum = sem("qkv_psum", 12)
        qkv_sb = sem("qkv_sb", 12)
        exp_ready = sem("exp_ready", 8)
        elu_ready = sem("elu_ready", 8)
        xh_ready = sem("xh_ready", 2)
        pads_ready = sem("pads_ready", 1)
        zpads_ready = sem("zpads_ready", 1)
        qk_prod = sem("qk_prod", 21)
        qk_summed = sem("qk_summed", 21)
        sT_ready = sem("sT_ready", 2)
        stok_psum = sem("stok_psum", 2)
        soft = sem("soft", 2 * 14)
        exps_ready = sem("exps_ready", 2)
        whi_ready = sem("whi_ready", 2)
        wmid_ready = sem("wmid_ready", 2)
        w3T_psum = sem("w3T_psum", 4)
        w3T_ready = sem("w3T_ready", 4)
        fkv_psum = sem("fkv_psum", 8)
        fkv_ready = sem("fkv_ready", 8)
        kv_psum = sem("kv_psum", 1)
        kvbd_ready = sem("kvbd_ready", 2)
        z_psum = sem("z_psum", 1)
        z_ready = sem("z_ready", 2)
        low_psum = sem("low_psum", 4)
        low_ready = sem("low_ready", 4)
        wbc_psum = sem("wbc_psum", 24)
        wv_prod = sem("wv_prod", 24)
        wv_pool = sem("wv_pool", pool_adds(7))
        wv_own = sem("wv_own", own_adds(7))
        wv_acc = sem("wv_acc", 8)
        hsumT_ready = sem("hsumT_ready", 4)
        wo_psum = sem("wo_psum", 4)
        d_ready = sem("d_ready", 8)
        xk_ready = sem("xk_ready", 8)
        xr_ready = sem("xr_ready", 8)
        k_psum = sem("k_psum", 8)
        relu_ready = sem("relu_ready", 8)
        kact_ready = sem("kact_ready", 8)
        r_psum = sem("r_psum", 8)
        gate_ready = sem("gate_ready", 8)
        v_psum = sem("v_psum", 8)
        gated_ready = sem("gated_ready", 8)
        z_out = sem("z_out", NPROJ)
        z_sb = sem("z_sb", NPROJ)
        q_copied = sem("q_copied", 16 * 2 * KQ)
        sconv = sem("sconv", 6)
        p_ready = sem("p_ready", 1)
        p_inv_ready = sem("p_inv_ready", 1)
        p_anchor_ready = sem("p_anchor_ready", 1)
        ratio_step = sem("ratio_step", 4)
        phi_ready = sem("phi_ready", 1)
        prest_ready = sem("prest_ready", 1)
        pmid_ready = sem("pmid_ready", 1)
        p3_ready = sem("p3_ready", 1)
        den_step = sem("den_step", 4)
        kconv = sem("kconv", 6)
        turn_psum = sem("turn_psum", NPAIR)
        turn_rounded = sem("turn_rounded", NPAIR)
        turn_ready = sem("turn_ready", NPAIR)
        abs_ready = sem("abs_ready", NPAIR)
        trig_ready = sem("trig_ready", NPAIR)
        pbc_psum = sem("pbc_psum", NPAIR)
        weighted = sem("weighted", (K2 - NDECAY) // 2)
        num_re_ready = sem("num_re_ready", NPAIR)
        num_ready = sem("num_ready", NPAIR)
        prod_re = sem("prod_re", NPAIR)
        prod_im_even = sem("prod_im_even", NPAIR // 2)
        prod_im_odd = sem("prod_im_odd", NPAIR // 2)
        y_psum = sem("y_psum", 2 * 8)
        y_sb = sem("y_sb", 4)
        ibc_psum = sem("ibc_psum", 4)
        yn_ready = sem("yn_ready", 4)
        tanh_ready = sem("tanh_ready", 4)
        ys_ready = sem("ys_ready", 4)
        wout_psum = sem("wout_psum", 4)

        def sum_bank(hf):
            return 0 if hf else 2

        block = ctx.enter_context(nc.Block())

        step = [2]

        @block.sync
        def _(sp):
            def load(dst, src):
                sp.dma_start(dst, src).then_inc(weights_in, 16)

            chunked = "(c p) n -> p c n"
            for dst, src in ((wqkv, "Wqkv"), (wo, "Wo"), (wr, "WrT"), (wk, "WkT"), (wv, "WvT"),
                             (w_out, "W_out"), (conv_a, "conv_w"), (theta, "theta")):
                load(dst[:], w[src].rearrange(chunked, p=P))
            w_in = w["W_in"].rearrange(chunked, p=P)
            load(w_in_k[:], w_in[:, :, 0:C])
            for r in range(4):
                load(w_in_s[:, :, r, :], w_in[:, :, C:C + K2])
                load(conv_bs[32 * r:32 * r + 32, :], w["conv_kT"][C:C + K2, :])
                load(slope[32 * r:32 * r + 32, 0:1], w["slopes"])
                load(score_scale[32 * r:32 * r + 32, :], w["score_scale"])
            load(wq_raw, w_in[:, :, C + K2:])
            load(conv_bk[:], w["conv_kT"][0:C, :].rearrange(chunked, p=P))
            for c in range(NC):
                load(mu_r[:, c:c + 1], w["mu_r"][P * c:P * c + P, :])
                load(mu_k[:, c:c + 1], w["mu_k"][P * c:P * c + P, :])
            for n, src in enumerate(("norm_scale_re", "norm_scale_im", "diag_re", "diag_im")):
                load(gains[:, n, :], w[src].to_broadcast([P, H2]))
            load(ident[:], k["ident"])
            load(headsum[:].rearrange("p s c m -> p (s c m)"), k["headsum"])
            load(spread_f, k["spread"])
            load(mask[:].rearrange("p t s w -> p (t s w)"), k["mask"])
            load(sameheads[:], k["sameheads"])
            load(headof[:].rearrange("p c h -> p (c h)"), k["headof"])
            load(pairof_f, k["pairof"])
            load(phasesum[:].rearrange("p a m -> p (a m)"), k["phasesum"])
            load(kind[:], k["kind"])
            load(kernelof[:].rearrange("p q a m -> p (q a m)"), k["kernelof"])
            sp.dma_start(log_time[:], k["dist"]).then_inc(out_stored, 16)
            def load_x(seq):
                sp.dma_start(x_in[:], x_dram[seq].rearrange("(t p) c -> p t c", p=P))\
                    .then_inc(x_loaded, 16)

            def store(seq):
                sp.wait_ge(out_ready, nth(seq, out_ready, 4))
                sp.dma_start(out_dram[seq].rearrange("(t p) c -> p t c", p=P), x_out[:])\
                    .then_inc(out_stored, 16)

            def copy_queries(seq):
                for q in range(KQ):
                    sp.wait_ge(z_sb, nth(seq, z_sb, 6 + 2 * q + 2))
                    sp.dma_start(qpT[64:128, 2 * q], qpT[0:64, 2 * q]).then_inc(q_copied, 16)
                    sp.dma_start(qpT[0:64, 2 * q + 1], qpT[64:128, 2 * q + 1]).then_inc(q_copied, 16)

            load_x(0)
            with sp.Fori(0, NSEQ - 1) as seq:
                sp.wait_ge(xh_ready, nth(seq, xh_ready, 2))
                load_x(seq + 1)
                copy_queries(seq)
                store(seq)
            copy_queries(NSEQ - 1)
            store(NSEQ - 1)
            sp.wait_ge(out_stored, (NSEQ + 1) * 16)

        N_LOADS = 8 + 1 + 4 * 4 + 2 + 2 * NC + 4 + 10

        @block.gpsimd
        def _(pool):
            pool.memset(minus_half[:], -0.5)
            pool.memset(eps[:], EPS)
            pool.memset(half_pi[:], float(np.pi / 2))
            pool.memset(hT[:, :, 0:1], 0.0)
            pool.memset(round_c[:], ROUND).then_inc(pro_pool, 1)
            pool.wait_ge(pro_pool, 1)

            def rstd_of(seq, ln):
                for hf in range(2):
                    n = 2 * ln + hf + 1
                    cols = slice(TH * hf, TH * hf + TH)
                    pool.wait_ge(mv_ready, nth(seq, mv_ready, n))
                    pool.tensor_tensor(veps[:, cols], mv[:, cols, 1], eps[:], ALU.add)\
                        .then_inc(veps_ready, 1)
                    pool.wait_ge(veps_ready, nth(seq, veps_ready, n))
                    pool.tensor_tensor(rstd[:, cols], veps[:, cols], minus_half[:], ALU.pow)\
                        .then_inc(rstd_ready, 1)

            def ripple(seq):
                for hf in range(2):
                    pool.wait_ge(h_ready, nth(seq, h_ready, TH * (hf + 1)))
                    t = slice(TH * hf, TH * hf + TH)
                    pool.tensor_tensor(xs[:, t, :], x_in[:, t, :], h[:, t, :], ALU.add)\
                        .then_inc(xh_ready, 1)
                for hf in range(2):
                    for g in range(4):
                        first = 1 if g in OWN_FIRST else 0
                        for a in range(first, 2):
                            u = 12 * hf + 3 * g + a + 1
                            pool.wait_ge(wv_prod, nth(seq, wv_prod, u + 1))
                            if a == 1 and first:
                                pool.wait_ge(wv_own, nth(seq, wv_own, own_adds(4 * hf + g)))
                            elif a == 1:
                                pool.wait_ge(wv_pool, nth(seq, wv_pool, pool_adds(4 * hf + g) - 1))
                            pool.tensor_tensor(prods[:, u % NPROD], prods[:, u % NPROD],
                                               prods[:, (u - 1) % NPROD], ALU.add)\
                                .then_inc(wv_pool, 1)

            def ffn(seq, f):
                for hf in range(2):
                    for c in range(NC):
                        pool.wait_ge(hT_ready, nth(seq, hT_ready, (4 if f == 0 else 12) + 2 * hf + c + 1))
                        a = HALF * hf
                        pool.tensor_tensor(dT[:, c, a:a + HALF], hT[:, c, a + 1:a + 1 + HALF],
                                           hT[:, c, a:a + HALF], ALU.subtract).then_inc(d_ready, 1)

            def phase(seq):
                pool.wait_ge(q_copied, nth(seq, q_copied, 16 * 2 * KQ))
                for n, i in enumerate(ORDER):
                    g = nums[:, n % NNUM]
                    pool.wait_ge(num_re_ready, nth(seq, num_re_ready, n + 1))
                    pool.tensor_tensor(g[:, 0], g[:, 0], qpT[:, 2 * (i // 4)], ALU.mult)\
                        .then_inc(prod_re, 1)
                    if n % 2 == 0:
                        pool.wait_ge(num_ready, nth(seq, num_ready, n + 1))
                        pool.tensor_tensor(g[:, 1], g[:, 1], qpT[:, 2 * (i // 4) + 1], ALU.mult)\
                            .then_inc(prod_im_even, 1)

            with pool.Fori(0, NSEQ) as seq:
                rstd_of(seq, 0)
                ripple(seq)
                rstd_of(seq, 1)
                ffn(seq, 0)
                rstd_of(seq, 2)
                phase(seq)
                rstd_of(seq, 3)
                ffn(seq, 1)

        @block.scalar
        def _(act):
            act.wait_ge(pro_pool, 1)
            act.wait_ge(prologue, 1)
            act.activation(slope[:, 2:3], slope[:, 1:2], ACT.Exp, scale=-1.0).then_inc(pro_act, 1)
            act.wait_ge(prologue, 2)
            act.activation(slope[:, 4:5], slope[:, 3:4], ACT.Ln).then_inc(pro_act, 1)

            def normalise(seq, ln, x):
                for t in range(T):
                    if t % TH == 0:
                        act.wait_ge(neg_mr_ready, nth(seq, neg_mr_ready, 2 * ln + t // TH + 1))
                        if ln == 0:
                            act.wait_ge(out_stored, nth(seq, out_stored, 16))
                    act.activation(h[:, t, :], x[:, t, :], ACT.Identity, bias=neg_mr[:, t:t + 1],
                                   scale=rstd[:, t:t + 1]).then_inc(h_ready, 1)

            def evacuate_hT(seq, ln):
                for hf in range(2):
                    for c in range(NC):
                        act.wait_ge(hT_psum, nth(seq, hT_psum, 4 * ln + 2 * hf + c + 1))
                        a = 1 + HALF * hf
                        act.activation(hT[:, c, a:a + HALF], PS[:, 2 * hf + c], ACT.Copy)\
                            .then_inc(hT_ready, 1)

            def qkv_out(seq, hf):
                for m in range(6):
                    n = 6 * hf + m
                    c = m % 2
                    a = HALF * hf
                    bank = PS[:, 4 + n % 4]
                    act.wait_ge(qkv_psum, nth(seq, qkv_psum, n + 1))
                    if m < 4:
                        e = 4 * hf + m
                        dst = (fkT if m < 2 else fqT)[:, c, a:a + HALF]
                        act.activation(dst, bank, ACT.Exp)
                        if e >= 4:
                            act.wait_ge(elu_ready, nth(seq, elu_ready, e - 3))
                        act.activation(relus[:, e % 4], bank, ACT.Relu).then_inc(exp_ready, 1)
                    if m < 2:
                        dst = kT[:, c, PAD + a:PAD + a + HALF]
                    elif m < 4:
                        dst = qT[:, c, a:a + HALF]
                    else:
                        dst = vT[:, c, PAD + a:PAD + a + HALF]
                    act.activation(dst, bank, ACT.Copy).then_inc(qkv_sb, 1)

            def ripple(seq):
                qkv_out(seq, 0)
                qkv_out(seq, 1)
                act.wait_ge(qk_summed, nth(seq, qk_summed, 10))
                act.activation(sT, PS[:, 0], ACT.Copy).then_inc(sT_ready, 1)
                for t in range(T):
                    act.wait_ge(fkv_psum, nth(seq, fkv_psum, t + 1))
                    act.activation(fkv[:, t, :, 0:2 * P],
                                   PS[:, 4 + t % 4].rearrange("p (c n) -> p c n", c=NC), ACT.Copy)\
                        .then_inc(fkv_ready, 1)
                softmax_exp(seq, 0)
                high_part(seq, 0)
                middle_part(seq, 0)
                evacuate_w3T(seq, 0)
                act.wait_ge(qk_summed, nth(seq, qk_summed, 21))
                act.activation(sT, PS[:, 0], ACT.Copy).then_inc(sT_ready, 1)
                softmax_exp(seq, 1)
                low_out(seq, 0)
                low_out(seq, 1)
                high_part(seq, 1)
                low_out(seq, 2)
                middle_part(seq, 1)
                low_out(seq, 3)
                evacuate_w3T(seq, 1)
                for hf in range(2):
                    for c in range(NC):
                        act.wait_ge(wv_acc, nth(seq, wv_acc, 4 * hf + 4))
                        act.activation(hsumT[:, c, HALF * hf:HALF * hf + HALF], PS[:, sum_bank(hf) + c], ACT.Copy)\
                            .then_inc(hsumT_ready, 1)

            def softmax_exp(seq, hf):
                act.wait_ge(soft, nth(seq, soft, 14 * hf + 6))
                t = slice(TH * hf, TH * hf + TH)
                act.activation(sm[:, t], sm[:, t], ACT.Exp, scale=float(D) ** -0.5)\
                    .then_inc(exps_ready, 1)

            def low_out(seq, n):
                act.wait_ge(low_psum, nth(seq, low_psum, n + 1))
                c, hf = n % 2, n // 2
                act.activation(low_num[:, c, HALF * hf:HALF * hf + HALF], PS[:, 0], ACT.Copy)\
                    .then_inc(low_ready, 1)

            def high_part(seq, hf):
                act.wait_ge(soft, nth(seq, soft, 14 * hf + 12))
                if hf == 1:
                    act.wait_ge(w3T_psum, nth(seq, w3T_psum, 2))
                t = slice(TH * hf, TH * hf + TH)
                act.activation(w3.rearrange("p t s q w -> p (t s) q w")[:, :, 0],
                               sm[:, t].rearrange("p t s w -> p (t s) w"), ACT.Copy).then_inc(whi_ready, 1)

            def middle_part(seq, hf):
                act.wait_ge(soft, nth(seq, soft, 14 * hf + 13))
                act.activation(w3.rearrange("p t s q w -> p (t s) q w")[:, :, 1], wrest, ACT.Copy)\
                    .then_inc(wmid_ready, 1)

            def evacuate_w3T(seq, hf):
                bank = PS[0:96, 1].bitcast(bf16).rearrange("p (s n) -> p s n", s=2)
                act.wait_ge(w3T_psum, nth(seq, w3T_psum, 2 * hf + 1))
                act.activation(w3T[:, hf, 0:2], bank, ACT.Copy).then_inc(w3T_ready, 1)
                act.wait_ge(w3T_psum, nth(seq, w3T_psum, 2 * hf + 2))
                act.activation(w3T[:, hf, 2], bank[:, 0], ACT.Copy).then_inc(w3T_ready, 1)

            def ffn(seq, f):
                for hf in range(2):
                    for m in range(NC):
                        n = 4 * f + 2 * hf + m + 1
                        a = slice(HALF * hf, HALF * hf + HALF)
                        act.wait_ge(k_psum, nth(seq, k_psum, n))
                        act.activation(kact[:, m, a], PS[:, 4 + 2 * hf + m], ACT.Relu)\
                            .then_inc(relu_ready, 1)
                        act.wait_ge(relu_ready, nth(seq, relu_ready, n))
                        act.activation(kact[:, m, a], kact[:, m, a], ACT.Square)\
                            .then_inc(kact_ready, 1)
                for tp in range(4):
                    act.wait_ge(r_psum, nth(seq, r_psum, 4 * f + tp + 1))
                    act.activation(gate[:, tp], PS[:, tp], ACT.Tanh, scale=0.5)\
                        .then_inc(gate_ready, 1)

            def phase_project(seq):
                for n in range(NPROJ):
                    bank = PS[:, 4 + n % 4]
                    act.wait_ge(z_out, nth(seq, z_out, n + 1))
                    if n < 6:
                        hf = n % 2
                        c = (n - 2) // 2
                        a = HALF * hf
                        raw = zs_raw if n < 2 else z_raw[:, c]
                        first = zs if n < 2 else zc[:, c]
                        tap = conv_bs[:, KS - 1:KS] if n < 2 else conv_bk[:, c, KS - 1:KS]
                        act.activation(first[:, a:a + HALF], bank, ACT.Copy, scale=tap)
                        act.activation(raw[:, KS - 1 + a:KS - 1 + a + HALF], bank, ACT.Copy)\
                            .then_inc(z_sb, 1)
                    else:
                        q, a = (n - 6) // 2, HALF * (n % 2)
                        act.activation(qpT[0:64, 2 * q, a:a + HALF], bank[0:64], ACT.Copy)
                        act.activation(qpT[64:128, 2 * q + 1, a:a + HALF], bank[64:128], ACT.Copy)\
                            .then_inc(z_sb, 1)
                    if n == EXP_AT:
                        act.wait_ge(sconv, nth(seq, sconv, 6))
                        act.activation(pw, zs, ACT.Exp).then_inc(p_ready, 1)
                        act.activation(p_inv, zs, ACT.Exp, scale=kind[:, 2:3]).then_inc(p_inv_ready, 1)
                        act.wait_ge(p_ready, nth(seq, p_ready, 1))
                        act.activation(p_anchor, pw, ACT.Copy, scale=kind[:, 1:2]).then_inc(p_anchor_ready, 1)
                    if n == HIGH_AT:
                        act.wait_ge(ratio_step, nth(seq, ratio_step, 4))
                        act.activation(p3[0:96], ratio[0:96], ACT.Copy).then_inc(phi_ready, 1)
                    if n == NPROJ - 1:
                        act.wait_ge(prest_ready, nth(seq, prest_ready, 1))
                        for q in (1, 2):
                            r = slice(32 * q, 32 * q + 32)
                            mid = act.activation(p3[r], prest[r], ACT.Copy)
                        mid.then_inc(pmid_ready, 1)

            def phase_units(seq):
                def rounded(n):
                    act.wait_ge(turn_psum, nth(seq, turn_psum, n + 1))
                    if n >= 2:
                        act.wait_ge(trig_ready, nth(seq, trig_ready, n - 1))
                    a = 2 * (n % 2)
                    act.activation(turns[:, n % 2].rearrange("p (b n) -> p b n", b=2), PS[:, a:a + 2],
                                   ACT.Identity, bias=round_c[:]).then_inc(turn_rounded, 1)

                rounded(0)
                rounded(1)
                for n in range(NPAIR):
                    act.wait_ge(turn_ready, nth(seq, turn_ready, n + 1))
                    if n >= 2:
                        act.wait_ge(num_ready, nth(seq, num_ready, n - 1))
                    act.activation(trig[:, n % 2, 0], turns[:, n % 2], ACT.Abs).then_inc(abs_ready, 1)
                    act.activation(trig[:, n % 2, 1], turns[:, n % 2], ACT.Sin, scale=-TWO_PI)
                    act.wait_ge(abs_ready, nth(seq, abs_ready, n + 1))
                    act.activation(trig[:, n % 2, 0], trig[:, n % 2, 0], ACT.Sin, bias=half_pi[:],
                                   scale=-TWO_PI).then_inc(trig_ready, 1)
                    if n + 2 < NPAIR:
                        rounded(n + 2)
                    if n == 10 or n == 15:
                        c = 0 if n == 10 else 1
                        for hf in range(2):
                            act.wait_ge(y_psum, nth(seq, y_psum, 8 * c + 8))
                            act.activation(yT[:, c, HALF * hf:HALF * hf + HALF], PS[:, 6 + hf], ACT.Copy)\
                                .then_inc(y_sb, 1)
                for n in range(4):
                    c, a = n // 2, HALF * (n % 2)
                    act.wait_ge(yn_ready, nth(seq, yn_ready, n + 1))
                    act.activation(thT[:, c, a:a + HALF], yT[:, c, a:a + HALF], ACT.Tanh, scale=0.5)\
                        .then_inc(tanh_ready, 1)

            with act.Fori(0, NSEQ) as seq:
                normalise(seq, 0, x_in)
                evacuate_hT(seq, 0)
                ripple(seq)
                normalise(seq, 1, xs)
                evacuate_hT(seq, 1)
                ffn(seq, 0)
                normalise(seq, 2, xs)
                evacuate_hT(seq, 2)
                phase_project(seq)
                phase_units(seq)
                normalise(seq, 3, xs)
                evacuate_hT(seq, 3)
                ffn(seq, 1)

        @block.vector
        def _(dve):

            def link(i):
                step[0] += 1
                i.then_inc(prologue, 1)
                dve.wait_ge(prologue, step[0])

            dve.wait_ge(weights_in, 16 * N_LOADS)
            dve.wait_ge(out_stored, 16)
            dve.scalar_tensor_tensor(slope[:, 1:2], slope[:, 0:1], -1.0, slope[:, 0:1], ALU.mult, ALU.max)\
                .then_inc(prologue, 1)
            dve.wait_ge(pro_act, 1)
            dve.tensor_scalar(slope[:, 3:4], slope[:, 2:3], 1.0, None, ALU.add).then_inc(prologue, 1)
            dve.wait_ge(pro_act, 2)
            link(dve.tensor_scalar(slope[:, 5:6], slope[:, 3:4], -1.0, None, ALU.add))
            link(dve.tensor_scalar(slope[:, 6:7], slope[:, 5:6], 0.0, None, ALU.is_equal))
            link(dve.tensor_tensor(slope[:, 4:5], slope[:, 4:5], slope[:, 6:7], ALU.add))
            link(dve.tensor_tensor(slope[:, 5:6], slope[:, 5:6], slope[:, 6:7], ALU.add))
            link(dve.reciprocal(slope[:, 5:6], slope[:, 5:6]))
            link(dve.tensor_tensor(slope[:, 4:5], slope[:, 4:5], slope[:, 5:6], ALU.mult))
            link(dve.tensor_tensor(slope[:, 4:5], slope[:, 4:5], slope[:, 2:3], ALU.mult))
            link(dve.scalar_tensor_tensor(slope[:, 7:8], slope[:, 0:1], 0.0, slope[:, 4:5], ALU.max, ALU.add))
            link(dve.tensor_scalar(log_time[:], log_time[:], slope[:, 7:8], -1.0, ALU.mult, ALU.mult))
            link(dve.tensor_tensor(gains[:, 4], gains[:, 0], gains[:, 2], ALU.mult))
            link(dve.tensor_tensor(gains[:, 5], gains[:, 1], gains[:, 3], ALU.mult))
            scratch = xs[:].rearrange("p t c -> p (t c)")[:, 0:64].rearrange("p (h m) -> p h m", h=H2)
            for c in range(NC):
                raw = wq_raw[:, c].rearrange("p (q h m r) -> p q h m r", q=KQ, h=H2, m=M2)
                for q in range(KQ):
                    q_re, q_im = raw[:, q, :, :, 0], raw[:, q, :, :, 1]
                    g_re = gains[:, 4, :].unsqueeze(2).to_broadcast([P, H2, M2])
                    g_im = gains[:, 5, :].unsqueeze(2).to_broadcast([P, H2, M2])
                    for part, (a, b, op) in enumerate(((q_re, q_im, ALU.subtract), (q_im, q_re, ALU.add))):
                        once = w_in_q[:, c, q, part].rearrange("p (h m) -> p h m", h=H2)
                        link(dve.tensor_tensor(scratch, b, g_im, ALU.mult))
                        link(dve.tensor_tensor(once, a, g_re, ALU.mult))
                        link(dve.tensor_tensor(once, once, scratch, op))
                link(dve.tensor_scalar(theta[:, c], theta[:, c], float(1 / (2 * np.pi)), None, ALU.mult))
                link(dve.tensor_tensor(theta_w[:, c].rearrange("p i (a m) -> p (i a) m", m=M2),
                                       ident[:].unsqueeze(2).to_broadcast([P, P, M2]),
                                       theta[:, c:c + 1, :].to_broadcast([P, P, M2]), ALU.mult))
                for n, tap in enumerate(TAPS):
                    j = KCONV - 1 - tap
                    link(dve.tensor_scalar(tap_w[:, n, c], ident[:], conv_a[:, c, j:j + 1], None, ALU.mult))
            link(dve.tensor_copy(ident_b[:], ident[:]))
            link(dve.tensor_copy(spread[:].rearrange("p j c m -> p (j c m)"), spread_f))
            link(dve.tensor_copy(pairof[:].rearrange("p i m -> p (i m)"), pairof_f))
            link(dve.tensor_scalar(wv[:], wv[:], 0.5, None, ALU.mult))
            link(dve.tensor_scalar(w_out[:], w_out[:], 0.5, None, ALU.mult))

            def moments(seq, ln, x, hf):
                n = 2 * ln + hf + 1
                if ln == 0:
                    dve.wait_ge(x_loaded, nth(seq, x_loaded, 16))
                else:
                    dve.wait_ge(xs_ready, nth(seq, xs_ready, 4 * (ln - 1) + 2 * hf + 2))
                for t in range(TH * hf, TH * hf + TH):
                    last = dve.bn_stats(stats[:, t], x[:, t, :])
                last.then_inc(stats_ready, 1)
                dve.wait_ge(stats_ready, nth(seq, stats_ready, n))
                dve.tensor_copy(count[:], stats[:, TH * hf, 0:1])
                for t in range(TH * hf, TH * hf + TH):
                    last = dve.bn_aggr(mv[:, t], stats[:, t])
                last.then_inc(mv_ready, 1)

            def shift_of(seq, ln, hf):
                n = 2 * ln + hf + 1
                t = slice(TH * hf, TH * hf + TH)
                dve.wait_ge(rstd_ready, nth(seq, rstd_ready, n))
                dve.scalar_tensor_tensor(neg_mr[:, t], mv[:, t, 0], -1.0, rstd[:, t], ALU.mult, ALU.mult)\
                    .then_inc(neg_mr_ready, 1)

            def ripple(seq):
                for buf in (kT, vT):
                    dve.memset(buf[:, :, 0:PAD], 0.0)
                dve.memset(fkv[:, :, :, 2 * P:2 * P + 1], 1.0).then_inc(pads_ready, 1)
                dve.wait_ge(pads_ready, nth(seq, pads_ready, 1))

                def scores(u):
                    hf, o = (0, u) if u < 10 else (1, u - 10)
                    a = HALF * hf
                    if u % 10 == 0 and u < 20:
                        dve.wait_ge(qkv_sb, nth(seq, qkv_sb, 6 * hf + 4))
                    if u >= 4:
                        dve.wait_ge(qk_summed, nth(seq, qk_summed, u - 3))
                    b = PAD + a - OFFS[o]
                    dve.tensor_tensor(prods[:, u % 4], qT[:, :, a:a + HALF], kT[:, :, b:b + HALF],
                                      ALU.mult).then_inc(qk_prod, 1)

                def elu(e):
                    hf, m = e // 4, e % 4
                    dst = (fkT if m < 2 else fqT)[:, m % 2, HALF * hf:HALF * hf + HALF]
                    dve.wait_ge(exp_ready, nth(seq, exp_ready, e + 1))
                    dve.scalar_tensor_tensor(dst, dst, 1.0, relus[:, e % 4], ALU.min, ALU.add)\
                        .then_inc(elu_ready, 1)

                def chained(hf, n, i):
                    i.then_inc(soft, 1)
                    dve.wait_ge(soft, nth(seq, soft, 14 * hf + n))

                def over_slots(hf, n, op, src, dst):
                    chained(hf, n, dve.tensor_tensor(smx[:, :, 0:48], src[:, :, 0:48], src[:, :, 48:96], op))
                    chained(hf, n + 1, dve.tensor_tensor(smx[:, :, 48:72], smx[:, :, 0:24], smx[:, :, 24:48], op))
                    chained(hf, n + 2, dve.tensor_tensor(smx[:, :, 72:80], smx[:, :, 48:56], smx[:, :, 56:64], op))
                    chained(hf, n + 3, dve.tensor_tensor(dst, smx[:, :, 72:80], smx[:, :, 64:72], op))

                def soft_max(hf):
                    t = slice(TH * hf, TH * hf + TH)
                    flat = sm[:, t].rearrange("p t s w -> p t (s w)")
                    bank = PS[:, 1].rearrange("p (t j w) -> p t j w", t=TH, j=NJ)
                    dve.wait_ge(stok_psum, nth(seq, stok_psum, hf + 1))
                    for s in range(NS):
                        last = dve.tensor_tensor(sm[:, t, s].rearrange("p t (j h) -> p t j h", j=NJ),
                                                 bank[:, :, :, s * H:s * H + H],
                                                 mask[:, t, s].rearrange("p t (j h) -> p t j h", j=NJ), ALU.add)
                    chained(hf, 1, last)
                    over_slots(hf, 2, ALU.max, flat, srec)
                    chained(hf, 6, dve.tensor_tensor(
                        flat.rearrange("p t (o h) -> p t o h", h=H), flat.rearrange("p t (o h) -> p t o h", h=H),
                        srec.unsqueeze(2).to_broadcast([P, TH, NS * NJ, H]), ALU.subtract))

                def soft_norm(hf):
                    t = slice(TH * hf, TH * hf + TH)
                    flat = sm[:, t].rearrange("p t s w -> p t (s w)")
                    dve.wait_ge(exps_ready, nth(seq, exps_ready, hf + 1))
                    over_slots(hf, 7, ALU.add, flat, srec)
                    chained(hf, 11, dve.reciprocal(srec, srec))
                    chained(hf, 12, dve.tensor_tensor(
                        flat.rearrange("p t (o h) -> p t o h", h=H), flat.rearrange("p t (o h) -> p t o h", h=H),
                        srec.unsqueeze(2).to_broadcast([P, TH, NS * NJ, H]), ALU.mult))

                def soft_split(hf):
                    t = slice(TH * hf, TH * hf + TH)
                    flat = sm[:, t].rearrange("p t s w -> p (t s) w")
                    parts = w3.rearrange("p t s q w -> p (t s) q w")
                    dve.wait_ge(whi_ready, nth(seq, whi_ready, hf + 1))
                    chained(hf, 13, dve.tensor_tensor(wrest, flat, parts[:, :, 0], ALU.subtract))
                    dve.wait_ge(wmid_ready, nth(seq, wmid_ready, hf + 1))
                    chained(hf, 14, dve.tensor_tensor(parts[:, :, 2], wrest, parts[:, :, 1], ALU.subtract))

                def low_state():
                    dve.wait_ge(kv_psum, nth(seq, kv_psum, 1))
                    for c in range(NC):
                        dve.tensor_tensor(kvbd[:, c], PS[:, 2 + c, 0:P], sameheads[:], ALU.mult)
                        dve.tensor_scalar(zsel[:, c], headof[:, c], PS[:, 2 + c, P:P + 1], None, ALU.mult)\
                            .then_inc(kvbd_ready, 1)

                def low_z():
                    dve.wait_ge(z_psum, nth(seq, z_psum, 1))
                    dve.tensor_scalar(zrec, PS[:, 0, 0:S // 4], 1e-6, None, ALU.add).then_inc(z_ready, 1)
                    dve.wait_ge(z_ready, nth(seq, z_ready, 1))
                    dve.reciprocal(zrec, zrec).then_inc(z_ready, 1)

                def values(hf, o):
                    u = 12 * hf + o
                    a = HALF * hf
                    dve.wait_ge(wbc_psum, nth(seq, wbc_psum, u + 1))
                    if u >= NPROD:
                        v = u - NPROD
                        if v % 3 == 2:
                            dve.wait_ge(wv_acc, nth(seq, wv_acc, v // 3 + 1))
                        elif v % 3 == 1:
                            dve.wait_ge(wv_pool, nth(seq, wv_pool, pool_adds(v // 3)))
                        elif v // 3 % 4 not in OWN_FIRST:
                            dve.wait_ge(wv_pool, nth(seq, wv_pool, pool_adds(v // 3) - 1))
                    pair = 4 + 2 * (u % 2)
                    dst = prods[:, u % NPROD]
                    if o == LOW:
                        dve.wait_ge(low_ready, nth(seq, low_ready, 4))
                        dve.tensor_tensor(dst, PS[:, pair:pair + 2], low_num[:, :, a:a + HALF], ALU.mult)\
                            .then_inc(wv_prod, 1)
                        return
                    if o == 0 and hf == 0:
                        dve.wait_ge(qkv_sb, nth(seq, qkv_sb, 12))
                    b = PAD + a - OFFS[o]
                    if OFFS[o] < KCONV:
                        j = KCONV - 1 - OFFS[o]
                        dve.scalar_tensor_tensor(dst[:, 0], PS[:, pair], conv_a[:, 0, j:j + 1],
                                                 vT[:, 0, b:b + HALF], ALU.add, ALU.mult)
                        dve.scalar_tensor_tensor(dst[:, 1], PS[:, pair + 1], conv_a[:, 1, j:j + 1],
                                                 vT[:, 1, b:b + HALF], ALU.add, ALU.mult)\
                            .then_inc(wv_prod, 1)
                    else:
                        dve.tensor_tensor(dst, PS[:, pair:pair + 2], vT[:, :, b:b + HALF], ALU.mult)\
                            .then_inc(wv_prod, 1)

                for u in range(21):
                    scores(u)
                    if u < 4:
                        elu(u)
                    if 10 <= u < 14:
                        elu(u - 6)
                    if u == 14:
                        soft_max(0)
                    if u == 15:
                        soft_norm(0)
                    if u == 17:
                        soft_split(0)
                    if u == 19:
                        low_state()
                dve.wait_ge(qk_summed, nth(seq, qk_summed, 21))

                def own_add(hf, o):
                    u, g = 12 * hf + o, o // 3
                    if o % 3 == 1 and g in OWN_FIRST:
                        dve.wait_ge(wv_prod, nth(seq, wv_prod, u + 1))
                        dve.tensor_tensor(prods[:, u % NPROD], prods[:, u % NPROD], prods[:, (u - 1) % NPROD],
                                          ALU.add).then_inc(wv_own, 1)
                        dve.wait_ge(wv_own, nth(seq, wv_own, own_adds(4 * hf + g)))

                for o in range(NO + 1):
                    values(0, o)
                    own_add(0, o)
                    if o == 1:
                        soft_max(1)
                    if o == 3:
                        soft_norm(1)
                    if o == 4:
                        low_z()
                    if o == 6:
                        soft_split(1)
                for o in range(NO + 1):
                    values(1, o)
                    own_add(1, o)

            def residual(seq, layer, tp, psum, ready, bank):
                dve.wait_ge(ready, nth(seq, ready, tp + 1))
                if layer == 0:
                    dve.wait_ge(xh_ready, nth(seq, xh_ready, 2))
                x = xs[:, 2 * tp:2 * tp + 2, :]
                dve.tensor_tensor(x, x, PS[:, bank].rearrange("p (t c) -> p t c", t=2), ALU.add)\
                    .then_inc(xs_ready, 1)

            def ffn(seq, f):
                for hf in range(2):
                    a = HALF * hf
                    for which, (mu, dst, done) in enumerate(((mu_k, xkT, xk_ready), (mu_r, xrT, xr_ready))):
                        for c in range(NC):
                            dve.wait_ge(d_ready, nth(seq, d_ready, 4 * f + 2 * hf + c + 1))
                            dve.scalar_tensor_tensor(dst[:, c, a:a + HALF], dT[:, c, a:a + HALF],
                                                     mu[:, c:c + 1], hT[:, c, a:a + HALF], ALU.mult, ALU.add)\
                                .then_inc(done, 1)

            def ffn_out(seq, f, tp):
                n = 4 * f + tp + 1
                dve.wait_ge(gate_ready, nth(seq, gate_ready, n))
                dve.wait_ge(v_psum, nth(seq, v_psum, n))
                dve.scalar_tensor_tensor(gated[:, tp], gate[:, tp], 1.0, PS[:, 4 + tp], ALU.add, ALU.mult)\
                    .then_inc(gated_ready, 1)
                dve.wait_ge(gated_ready, nth(seq, gated_ready, n))
                t = slice(2 * tp, 2 * tp + 2)
                add = gated[:, tp].rearrange("p (t c) -> p t c", t=2)
                if f == 0:
                    dve.tensor_tensor(xs[:, t, :], xs[:, t, :], add, ALU.add).then_inc(xs_ready, 1)
                else:
                    dve.tensor_tensor(x_out[:, t, :], xs[:, t, :], add, ALU.add).then_inc(out_ready, 1)

            def phase(seq):
                dve.memset(z_raw[:, :, 0:KS - 1], 0.0)
                dve.memset(pz[:, 0:1], 0.0)
                dve.memset(zs_raw[:, 0:KS - 1], 0.0).then_inc(zpads_ready, 1)
                dve.wait_ge(zpads_ready, nth(seq, zpads_ready, 1))

                def s_step(n, i):
                    i.then_inc(sconv, 1)
                    dve.wait_ge(sconv, nth(seq, sconv, n))

                def k_conv(j, c):
                    if j == 0:
                        dve.wait_ge(z_sb, nth(seq, z_sb, 2 * c + 4))
                    else:
                        dve.wait_ge(kconv, nth(seq, kconv, 2 * j + c - 1))
                    dve.scalar_tensor_tensor(zc[:, c], z_raw[:, c, j:j + S], conv_bk[:, c, j:j + 1], zc[:, c],
                                             ALU.mult, ALU.add).then_inc(kconv, 1)

                def ratio_to(n, i):
                    i.then_inc(ratio_step, 1)
                    dve.wait_ge(ratio_step, nth(seq, ratio_step, n))

                dve.wait_ge(z_sb, nth(seq, z_sb, 2))
                for j in range(KS - 1):
                    s_step(j + 1, dve.scalar_tensor_tensor(zs, zs_raw[:, j:j + S], conv_bs[:, j:j + 1], zs,
                                                           ALU.mult, ALU.add))
                s_step(4, dve.tensor_scalar(zs, zs, score_scale[:], 20.0, ALU.mult, ALU.min))
                s_step(5, dve.scalar_tensor_tensor(zs, zs, -20.0, log_time[:], ALU.max, ALU.add))
                s_step(6, dve.tensor_scalar(zs, zs, LOG_MIN, None, ALU.max))
                k_conv(0, 0)
                k_conv(0, 1)
                dve.wait_ge(p_ready, nth(seq, p_ready, 1))
                dve.wait_ge(p_inv_ready, nth(seq, p_inv_ready, 1))
                ratio_to(1, dve.tensor_tensor(ratio, pw, p_inv, ALU.mult))
                ratio_to(2, dve.scalar_tensor_tensor(ratio, ratio, -2.0, p_inv, ALU.add, ALU.mult))
                ratio_to(3, dve.scalar_tensor_tensor(ratio, pz[:, 0:S], kind[:, 2:3], ratio, ALU.mult, ALU.mult))
                dve.wait_ge(p_anchor_ready, nth(seq, p_anchor_ready, 1))
                ratio_to(4, dve.tensor_tensor(ratio, ratio, p_anchor, ALU.add))
                k_conv(1, 0)
                k_conv(1, 1)
                dve.wait_ge(phi_ready, nth(seq, phi_ready, 1))
                for q in (1, 2):
                    r = slice(32 * q, 32 * q + 32)
                    rest = dve.tensor_tensor(prest[r], ratio[r], p3[r], ALU.subtract)
                rest.then_inc(prest_ready, 1)
                k_conv(2, 0)
                k_conv(2, 1)
                dve.wait_ge(pmid_ready, nth(seq, pmid_ready, 1))
                dve.tensor_tensor(p3[64:96], prest[64:96], p3[64:96], ALU.subtract).then_inc(p3_ready, 1)

                def denominators():
                    dve.tensor_tensor_scan(den, pw, pw, 0.0, ALU.add, ALU.bypass).then_inc(den_step, 1)
                    dve.wait_ge(den_step, nth(seq, den_step, 1))
                    for q in range(4):
                        r = slice(32 * q, 32 * q + 32)
                        dve.tensor_scalar(den_inv[r], den[r, 256 * q:256 * q + 256], 0.0001, None, ALU.max)
                        last = dve.tensor_scalar(p_back[r], pw[r, 256 * q:256 * q + 256], kind[r, 0:1],
                                                 kind[r, 1:2], ALU.mult, ALU.add)
                    last.then_inc(den_step, 1)
                    dve.wait_ge(den_step, nth(seq, den_step, 2))
                    dve.reciprocal(den_inv, den_inv).then_inc(den_step, 1)
                    dve.wait_ge(den_step, nth(seq, den_step, 3))
                    dve.tensor_tensor(den_inv, den_inv, p_back, ALU.mult).then_inc(den_step, 1)

                def turn(n):
                    a = 2 * (n % 2)
                    dve.wait_ge(turn_rounded, nth(seq, turn_rounded, n + 1))
                    t = turns[:, n % 2].rearrange("p (b n) -> p b n", b=2)
                    dve.scalar_tensor_tensor(t, t, -ROUND, PS[:, a:a + 2], ALU.add, ALU.subtract)\
                        .then_inc(turn_ready, 1)

                turn(0)
                turn(1)
                denominators()
                for n, i in enumerate(ORDER):
                    if 2 <= n + 1 < NPAIR:
                        turn(n + 1)
                    g = nums[:, n % NNUM]
                    flat = PS[:, 4:6].rearrange("p b n -> p (b n)")
                    dve.wait_ge(trig_ready, nth(seq, trig_ready, n + 1))
                    dve.wait_ge(pbc_psum, nth(seq, pbc_psum, n + 1))
                    if n >= NNUM:
                        dve.wait_ge(y_psum, nth(seq, y_psum, n - NNUM + 1))
                    if i < NDECAY // 2:
                        if n == 0:
                            dve.wait_ge(p3_ready, nth(seq, p3_ready, 1))
                        for a, done in ((0, num_re_ready), (1, num_ready)):
                            if n == NNUM - 2 or n == NNUM - 1:
                                dve.wait_ge(den_step, nth(seq, den_step, 4))
                            dve.tensor_tensor_scan(g[:, a], flat, trig[:, n % 2, a], 0.0, ALU.mult, ALU.add)\
                                .then_inc(done, 1)
                    else:
                        for a in range(2):
                            last = dve.tensor_tensor(g[:, a], trig[:, n % 2, a], flat, ALU.mult)
                        last.then_inc(weighted, 1)
                        dve.wait_ge(weighted, nth(seq, weighted, 1 + (n == NPAIR - 1)))
                        for a, done in ((0, num_re_ready), (1, num_ready)):
                            dve.tensor_tensor_scan(g[:, a], g[:, a], g[:, a], 0.0, ALU.add, ALU.bypass)\
                                .then_inc(done, 1)
                    if n == 0:
                        dve.wait_ge(q_copied, nth(seq, q_copied, 16 * 2 * KQ))
                    if n % 2 == 1:
                        dve.wait_ge(num_ready, nth(seq, num_ready, n + 1))
                        dve.tensor_tensor(g[:, 1], g[:, 1], qpT[:, 2 * (i // 4) + 1], ALU.mult)\
                            .then_inc(prod_im_odd, 1)
                for n in range(4):
                    c, a = n // 2, HALF * (n % 2)
                    dve.wait_ge(y_sb, nth(seq, y_sb, n + 1))
                    dve.wait_ge(ibc_psum, nth(seq, ibc_psum, n + 1))
                    dve.tensor_tensor(yT[:, c, a:a + HALF], yT[:, c, a:a + HALF], PS[:, n], ALU.mult)\
                        .then_inc(yn_ready, 1)
                for n in range(4):
                    c, a = n // 2, HALF * (n % 2)
                    dve.wait_ge(tanh_ready, nth(seq, tanh_ready, n + 1))
                    dve.scalar_tensor_tensor(yT[:, c, a:a + HALF], thT[:, c, a:a + HALF], 1.0,
                                             yT[:, c, a:a + HALF], ALU.add, ALU.mult).then_inc(ys_ready, 1)

            with dve.Fori(0, NSEQ) as seq:
                moments(seq, 0, x_in, 0)
                moments(seq, 0, x_in, 1)
                shift_of(seq, 0, 0)
                shift_of(seq, 0, 1)
                ripple(seq)
                for tp in range(4):
                    residual(seq, 0, tp, PS, wo_psum, 2 + tp % 2)
                    if tp == 1:
                        moments(seq, 1, xs, 0)
                moments(seq, 1, xs, 1)
                shift_of(seq, 1, 0)
                shift_of(seq, 1, 1)
                ffn(seq, 0)
                for tp in range(4):
                    ffn_out(seq, 0, tp)
                    if tp == 1:
                        moments(seq, 2, xs, 0)
                moments(seq, 2, xs, 1)
                shift_of(seq, 2, 0)
                shift_of(seq, 2, 1)
                phase(seq)
                for tp in range(4):
                    residual(seq, 2, tp, PS, wout_psum, 4 + tp)
                    if tp == 1:
                        moments(seq, 3, xs, 0)
                moments(seq, 3, xs, 1)
                shift_of(seq, 3, 0)
                shift_of(seq, 3, 1)
                ffn(seq, 1)
                for tp in range(4):
                    ffn_out(seq, 1, tp)

        @block.tensor
        def _(pe):
            pe.wait_ge(prologue, step[0])
            pe.wait_ge(pro_pool, 1)

            def transpose_h(seq, ln):
                for hf in range(2):
                    pe.wait_ge(h_ready, nth(seq, h_ready, T * ln + TH * hf + TH))
                    for c in range(NC):
                        for t in range(TH):
                            last = pe.transpose(PS[:, 2 * hf + c, P * t:P * t + P],
                                                h[:, TH * hf + t, P * c:P * c + P], ident[:])
                        last.then_inc(hT_psum, 1)

            def project(bank, weight, hf, src=None, lead=1):
                src = hT if src is None else src
                a = lead + HALF * hf
                for c in range(NC):
                    last = pe.matmul(PS[:, bank], weight[:, c], src[:, c, a:a + HALF],
                                     start=(c == 0), stop=(c == NC - 1))
                return last

            def project_tokens(bank, tp, src, weight):
                for t in range(2):
                    for c in range(NC):
                        a = P * (2 * tp + t)
                        last = pe.matmul(PS[:, bank, C * t:C * t + C], src[:, c, a:a + P], weight[:, c, :],
                                         start=(c == 0), stop=(c == NC - 1))
                return last

            def ripple(seq):
                def qkv(n):
                    hf, m = n // 6, n % 6
                    col = (C, C + P, 0, P, 2 * C, 2 * C + P)[m]
                    if m == 0:
                        pe.wait_ge(hT_ready, nth(seq, hT_ready, 2 * hf + 2))
                    if n >= 4:
                        pe.wait_ge(qkv_sb, nth(seq, qkv_sb, n - 3))
                    project(4 + n % 4, wqkv[:, :, col:col + P], hf).then_inc(qkv_psum, 1)

                def scores(us):
                    hf = 0 if us[0] < 10 else 1
                    if us[0] == 10:
                        pe.wait_ge(sT_ready, nth(seq, sT_ready, 1))
                    for c in range(NC):
                        for u in us:
                            o = u - 10 * hf
                            j, s = o % NJ, o // NJ
                            if c == 0:
                                pe.wait_ge(qk_prod, nth(seq, qk_prod, u + 1))
                            last_o = j + NJ * ((9 + hf - j) // NJ)
                            mm = pe.matmul(PS[32 * j:32 * j + 32, 0], headsum[:, s, c], prods[:, u % 4, c],
                                           start=(o < NJ and c == 0), stop=(o == last_o and c == NC - 1))
                            if c == NC - 1:
                                mm.then_inc(qk_summed, 1)

                def scores_to_tokens(hf):
                    pe.wait_ge(sT_ready, nth(seq, sT_ready, hf + 1))
                    for t in range(TH):
                        last = pe.transpose(PS[:, 1, P * t:P * t + P], sT[:, P * t:P * t + P], ident[:])
                    last.then_inc(stok_psum, 1)

                def fkv_tile(t):
                    pe.wait_ge(elu_ready, nth(seq, elu_ready, 4 * (t // TH) + 2))
                    if t == 0:
                        pe.wait_ge(qkv_sb, nth(seq, qkv_sb, 12))
                    if t >= 4:
                        pe.wait_ge(fkv_ready, nth(seq, fkv_ready, t - 3))
                    a = P * t
                    for c in range(NC):
                        pe.transpose(PS[:, 4 + t % 4, 2 * P * c:2 * P * c + P], fkT[:, c, a:a + P], ident[:])
                        last = pe.transpose(PS[:, 4 + t % 4, 2 * P * c + P:2 * P * c + 2 * P],
                                            vT[:, c, PAD + a:PAD + a + P], ident[:])
                    last.then_inc(fkv_psum, 1)

                def kv_sum():
                    pe.wait_ge(fkv_ready, nth(seq, fkv_ready, T))
                    for c in range(NC):
                        for t in range(T):
                            last = pe.matmul(PS[:, 2 + c, 0:P + 1], fkv[:, t, c, 0:P], fkv[:, t, c, P:2 * P + 1],
                                             start=(t == 0), stop=(t == T - 1))
                    last.then_inc(kv_psum, 1)

                def low_z():
                    pe.wait_ge(elu_ready, nth(seq, elu_ready, 8))
                    pe.wait_ge(sT_ready, nth(seq, sT_ready, 2))
                    for c in range(NC):
                        for q in range(4):
                            last = pe.matmul(PS[32 * q:32 * q + 32, 0, 0:S // 4], zsel[:, c],
                                             fqT[:, c, S // 4 * q:S // 4 * q + S // 4],
                                             start=(c == 0), stop=(c == NC - 1))
                    last.then_inc(z_psum, 1)

                def low(n):
                    c, hf = n % 2, n // 2
                    if n == 0:
                        pe.wait_ge(z_ready, nth(seq, z_ready, 1))
                    else:
                        pe.wait_ge(low_ready, nth(seq, low_ready, n))
                    pe.matmul(PS[:, 0], kvbd[:, c], fqT[:, c, HALF * hf:HALF * hf + HALF],
                              start=True, stop=True).then_inc(low_psum, 1)

                def weights_to_channels(hf):
                    pe.wait_ge(soft, nth(seq, soft, 14 * hf + 14))
                    bank = PS[0:96, 1].bitcast(bf16).rearrange("p (s n) -> p s n", s=2)
                    for s in range(NS):
                        if s == 2:
                            pe.wait_ge(w3T_ready, nth(seq, w3T_ready, 2 * hf + 1))
                        for t in range(TH):
                            last = pe.transpose(bank[:, s % 2, P * t:P * t + P],
                                                w3[:, t, s].rearrange("p q w -> p (q w)"), ident_b[:])
                        if s > 0:
                            last.then_inc(w3T_psum, 1)

                def spread_weight(hf, o):
                    u = 12 * hf + o
                    if o == 0:
                        pe.wait_ge(w3T_ready, nth(seq, w3T_ready, 2 * hf + 2))
                    if u >= 2:
                        pe.wait_ge(wv_prod, nth(seq, wv_prod, u - 1))
                    pair = 4 + 2 * (u % 2)
                    if o == LOW:
                        pe.wait_ge(z_ready, nth(seq, z_ready, 2))
                        for c in range(NC):
                            for b in range(2):
                                last = pe.matmul(PS[:, pair + c, 256 * b:256 * b + 256],
                                                 kernelof[:, 2 * hf + b, c], zrec, start=True, stop=True)
                        last.then_inc(wbc_psum, 1)
                        return
                    for c in range(NC):
                        last = pe.matmul(PS[:, pair + c], spread[:, o % NJ, c], w3T[:, hf, o // NJ],
                                         start=True, stop=True)
                    last.then_inc(wbc_psum, 1)

                def taps(hf):
                    if hf == 0:
                        pe.wait_ge(kvbd_ready, nth(seq, kvbd_ready, 2))
                    else:
                        pe.wait_ge(low_ready, nth(seq, low_ready, 4))
                        pe.wait_ge(w3T_ready, nth(seq, w3T_ready, 4))
                    for n, tap in enumerate(TAPS):
                        for c in range(NC):
                            b = PAD + HALF * hf - tap
                            pe.matmul(PS[:, sum_bank(hf) + c], tap_w[:, n, c], vT[:, c, b:b + HALF],
                                      start=(n == 0), stop=False)

                def accumulate(hf, g):
                    pe.wait_ge(wv_pool, nth(seq, wv_pool, pool_adds(4 * hf + g)))
                    u = 12 * hf + 3 * g + 2
                    for c in range(NC):
                        last = pe.matmul(PS[:, sum_bank(hf) + c], ident[:], prods[:, u % NPROD, c], start=False, stop=(g == 3))
                    last.then_inc(wv_acc, 1)

                def out_tokens(tp):
                    pe.wait_ge(hsumT_ready, nth(seq, hsumT_ready, 2 * (tp // 2) + 2))
                    if tp >= 2:
                        pe.wait_ge(xs_ready, nth(seq, xs_ready, tp - 1))
                    project_tokens(2 + tp % 2, tp, hsumT, wo).then_inc(wo_psum, 1)

                for n in range(6):
                    qkv(n)
                for p in range(5):
                    scores((2 * p, 2 * p + 1))
                    qkv(6 + p)
                qkv(11)
                for p in range(5):
                    scores((10 + 2 * p, 11 + 2 * p))
                    if p == 0:
                        scores_to_tokens(0)
                        for t in range(4):
                            fkv_tile(t)
                    if p == 1:
                        for t in range(4, T):
                            fkv_tile(t)
                    if p == 2:
                        kv_sum()
                weights_to_channels(0)
                scores((20,))
                for o in range(NO + 1):
                    spread_weight(0, o)
                    if o == 1:
                        scores_to_tokens(1)
                        taps(0)
                    if o == 2:
                        low_z()
                    if 4 <= o < 8:
                        low(o - 4)
                    if o % 3 == 2 and o > 2:
                        accumulate(0, o // 3 - 1)
                    if o == 9:
                        weights_to_channels(1)
                taps(1)
                for o in range(NO + 1):
                    spread_weight(1, o)
                    if o == 1:
                        accumulate(0, 3)
                    if o % 3 == 2 and o > 2:
                        accumulate(1, o // 3 - 1)
                    if o == 6:
                        out_tokens(0)
                    if o == 8:
                        out_tokens(1)
                accumulate(1, 3)
                for tp in (2, 3):
                    out_tokens(tp)

            def ffn(seq, f):
                for hf in range(2):
                    pe.wait_ge(xk_ready, nth(seq, xk_ready, 4 * f + 2 * hf + 2))
                    for m in range(NC):
                        project(4 + 2 * hf + m, wk[:, :, P * m:P * m + P], hf, xkT, 0).then_inc(k_psum, 1)
                for tp in range(4):
                    pe.wait_ge(xr_ready, nth(seq, xr_ready, 4 * f + 2 * (tp // 2) + 2))
                    if tp == 0:
                        pe.wait_ge(hT_ready, nth(seq, hT_ready, 4 * (1 + 2 * f) + 4))
                    project_tokens(tp, tp, xrT, wr).then_inc(r_psum, 1)
                for tp in range(4):
                    pe.wait_ge(kact_ready, nth(seq, kact_ready, 4 * f + 4))
                    project_tokens(4 + tp, tp, kact, wv).then_inc(v_psum, 1)

            def phase(seq):
                for n in range(NPROJ):
                    hf = n % 2
                    if n < 2:
                        weight = w_in_s[:].rearrange("p c r k -> p c (r k)")
                    elif n < 6:
                        c = (n - 2) // 2
                        weight = w_in_k[:, :, P * c:P * c + P]
                    else:
                        weight = w_in_q[:, :, (n - 6) // 2].rearrange("p c r f -> p c (r f)")
                    pe.wait_ge(hT_ready, nth(seq, hT_ready, 8 + 2 * hf + 2))
                    if n >= 4:
                        pe.wait_ge(z_sb, nth(seq, z_sb, n - 3))
                    project(4 + n % 4, weight, hf).then_inc(z_out, 1)

                def turn(n):
                    i = ORDER[n]
                    if n == 0:
                        pe.wait_ge(kconv, nth(seq, kconv, 6))
                    if n >= 2:
                        pe.wait_ge(turn_ready, nth(seq, turn_ready, n - 1))
                    for hf in range(2):
                        last = pe.matmul(PS[:, 2 * (n % 2) + hf], theta_w[:, i // 8, i % 8],
                                         zc[:, i // 8, HALF * hf:HALF * hf + HALF], start=True, stop=True)
                    last.then_inc(turn_psum, 1)

                def spread_decay(n):
                    if n == 0:
                        pe.wait_ge(p3_ready, nth(seq, p3_ready, 1))
                        pe.wait_ge(z_sb, nth(seq, z_sb, NPROJ))
                    else:
                        pe.wait_ge(num_ready, nth(seq, num_ready, n))
                    for hf in range(2):
                        last = pe.matmul(PS[:, 4 + hf], pairof[:, ORDER[n]], p3[0:96, HALF * hf:HALF * hf + HALF],
                                         start=True, stop=True)
                    last.then_inc(pbc_psum, 1)

                def head_sums(n):
                    units = ((n, ORDER[n]), (n + 1, ORDER[n + 1]))
                    c = ORDER[n] // 8
                    if n == 8:
                        pe.wait_ge(y_sb, nth(seq, y_sb, 2))
                    for part in range(2):
                        if part == 0:
                            pe.wait_ge(prod_re, nth(seq, prod_re, n + 2))
                        else:
                            pe.wait_ge(prod_im_even, nth(seq, prod_im_even, n // 2 + 1))
                            pe.wait_ge(prod_im_odd, nth(seq, prod_im_odd, n // 2 + 1))
                        for hf in range(2):
                            for m, i in units:
                                g = 32 * (i % 8 // 2)
                                mm = pe.matmul(PS[g:g + 32, 6 + hf], phasesum[:, i % 2],
                                               nums[:, m % NNUM, part, HALF * hf:HALF * hf + HALF],
                                               start=(i % 2 == 0 and part == 0), stop=(i % 2 == 1 and part == 1))
                                if part == 1 and hf == 1:
                                    mm.then_inc(y_psum, 1)

                turn(0)
                turn(1)
                for n in range(NPAIR):
                    spread_decay(n)
                    if n + 2 < NPAIR:
                        turn(n + 2)
                    if n % 2 == 1 and n >= 3:
                        head_sums(n - 3)
                head_sums(NPAIR - 2)
                pe.wait_ge(turn_ready, nth(seq, turn_ready, NPAIR))
                pe.wait_ge(den_step, nth(seq, den_step, 4))
                for n in range(4):
                    c, hf = n // 2, n % 2
                    for b in range(2):
                        q = 2 * hf + b
                        last = pe.matmul(PS[:, n, 256 * b:256 * b + 256], kernelof[:, q, c], den_inv,
                                         start=True, stop=True)
                    last.then_inc(ibc_psum, 1)
                pe.wait_ge(y_sb, nth(seq, y_sb, 4))
                for tp in range(4):
                    pe.wait_ge(ys_ready, nth(seq, ys_ready, 4))
                    project_tokens(4 + tp, tp, yT, w_out).then_inc(wout_psum, 1)

            with pe.Fori(0, NSEQ) as seq:
                transpose_h(seq, 0)
                ripple(seq)
                transpose_h(seq, 1)
                ffn(seq, 0)
                transpose_h(seq, 2)
                phase(seq)
                transpose_h(seq, 3)
                ffn(seq, 1)


_WEIGHTS = {
    "Wqkv": "L0_attn_a_Wqkv", "Wo": "L0_attn_a_Wo", "conv_w": "L0_attn_a_conv_w",
    "W_in": "L0_attn_b_W_in", "W_out": "L0_attn_b_W_out", "mu_r": "L0_ffn_mu_r", "mu_k": "L0_ffn_mu_k",
}


def kernel(**inputs):
    import numpy as _np
    import concourse.bacc as _bacc
    from concourse import mybir as _mybir
    from concourse.bass_utils import run_bass_kernel_spmd as _run

    get = lambda name: _np.asarray(inputs[name])
    weights = {name: get(full) for name, full in _WEIGHTS.items()}
    for name in ("W_r", "W_k", "W_v"):
        weights[name.replace("_", "") + "T"] = get("L0_ffn_" + name).T
    for name in ("mu_r", "mu_k"):
        weights[name] = weights[name][:, None]
    weights["conv_kT"] = get("L0_attn_b_conv_k")[:, 0, :].T
    weights["theta"] = get("L0_attn_b_theta").reshape(C, M2)
    weights["slopes"] = _np.concatenate([get("L0_attn_b_decay_slopes"), get("L0_attn_b_anchor_slopes")])[:, None]
    weights["score_scale"] = get("L0_attn_b_score_scale")[:, None]
    weights["norm_scale_re"] = get("L0_attn_b_norm_scale")[None, :H2]
    weights["norm_scale_im"] = get("L0_attn_b_norm_scale")[None, H2:]
    weights["diag_re"] = _np.diagonal(get("L0_attn_b_W_re"))[None, :]
    weights["diag_im"] = _np.diagonal(get("L0_attn_b_W_im"))[None, :]

    nc = _bacc.Bacc("TRN2", target_bir_lowering=False, num_devices=1)
    arrays = {}

    def dram(name, a):
        a = _np.ascontiguousarray(a)
        arrays[name] = a
        return nc.dram_tensor(name, a.shape, _mybir.dt.from_np(a.dtype), kind="ExternalInput").ap()

    w = {name: dram(f"in_{name}_dram", a) for name, a in weights.items()}
    k = {name: dram(f"const_{name}_dram", a) for name, a in constants().items()}
    x = dram("in_x_dram", inputs["L0_attn_a_x"])
    out = nc.dram_tensor("out_0_dram", (NSEQ, S, C), _mybir.dt.float32, kind="ExternalOutput").ap()
    build(nc, w, k, x, out)
    r = _run(nc, [arrays], core_ids=[0])
    return r.results[0]["out_0_dram"]
```

```python
import concourse.bass as bass
from concourse import mybir
from contextlib import ExitStack

import numpy as np

P = 128
NSEQ, S, C = 8, 1024, 256
T = S // P
HALF = 512
TH = T // 2
NC = C // P
H = 8
D = C // H
OFFS = [0] + [2 ** n for n in range(10)]
NO = len(OFFS)
LOW = NO
NJ, NS = 4, 3
PAD = 512
KCONV = 7
TAPS = [t for t in range(KCONV) if t not in OFFS]
NTAP = len(TAPS)
K2, H2, M2, KQ = 32, 8, 8, 4
NPROJ = 6 + 2 * KQ
EXP_AT, HIGH_AT, MID_AT = 6, 10, 12
SUMS_AT = 10
LN_AT = 10
TURN_AT = 12
FIRST_HALF = 2
NPAIR = K2 // 2
KS = 4
NDECAY = 28
EPS = 1e-5
LOG_MIN = -85.0
PROJECTIONS = [("s", 0, 0), ("k", 0, 0), ("k", 1, 0), ("s", 0, 1), ("k", 0, 1), ("k", 1, 1)] + \
    [("q", q, hf) for q in range(KQ) for hf in range(2)]
AFTER_S, AFTER_K = (1, 4), (5, 6)
ROUND = 12582912.0
TWO_PI = 6.283185
OWN_FIRST = (3, 5, 7)
ORDER = [8 * c + u for c in range(2) for u in (0, 2, 1, 3, 4, 6, 5, 7)]


def pool_adds(group):
    return sum(1 if g in OWN_FIRST else 2 for g in range(min(group + 1, 7)))


def own_adds(group):
    return sum(g in OWN_FIRST for g in range(group + 1))


def constants():
    f, p = np.arange(P), np.arange(P)[:, None]
    ident = np.eye(P, dtype=np.float32)
    headsum = np.zeros((P, NS, NC, 32), np.float32)
    spread = np.zeros((3, NJ, H, NJ, NC, P), np.float32)
    for s in range(NS):
        for c in range(NC):
            headsum[f, s, c, s * H + c * (H // NC) + f // D] = 1.0
    for j in range(NJ):
        for c in range(NC):
            spread[:, j, c * (H // NC) + f // D, j, c, f] = 1.0
    spread = spread.reshape(3 * NJ * H, NJ * NC * P)
    mask = np.zeros((P, T, NS, NJ, H), np.float32)
    time = (np.arange(T)[None, :] * P + np.arange(P)[:, None])
    for o in range(NS * NJ):
        bad = time < OFFS[o] if o < NO else time >= 0
        mask[:, :, o // NJ, o % NJ, :] = np.where(bad, -1e30, 0.0)[:, :, None]
    sameheads = (p // D == f[None, :] // D).astype(np.float32)
    headof = np.zeros((P, NC, 32), np.float32)
    for c in range(NC):
        headof[:, c, :] = np.arange(32)[None, :] // (32 // H) == c * (H // NC) + p // D
    pairof = np.zeros((3, K2, NPAIR, P), np.float32)
    for i in range(NPAIR):
        pairof[:, 2 * i + f // 64, i, f] = 1.0
    pairof = pairof.reshape(3 * K2, NPAIR * P)
    phasesum = np.zeros((P, 2, 32), np.float32)
    for par in range(2):
        phasesum[f, par, par * 16 + f // M2] = 1.0
    kernelof = np.zeros((P, 4, 2, P), np.float32)
    for c in range(2):
        for q in range(4):
            kernelof[32 * q + 16 * c + f // H2, q, c, f] = 1.0
    t = np.arange(S, dtype=np.float32)
    dist = np.where(np.arange(K2)[:, None] < NDECAY, S - 1 - t, t).astype(np.float32)
    is_decay = (np.arange(P)[:, None] % K2 < NDECAY).astype(np.float32)
    kind = np.concatenate([is_decay, 1 - is_decay, -is_decay], axis=1)
    return dict(ident=ident, kind=kind, headsum=headsum.reshape(P, -1), spread=spread, mask=mask.reshape(P, -1),
                sameheads=sameheads, headof=headof.reshape(P, -1), pairof=pairof,
                phasesum=phasesum.reshape(P, -1), kernelof=kernelof.reshape(P, -1),
                dist=np.tile(dist, (4, 1)))


def build(nc, w, k, x_dram, out_dram):
    fp32, bf16 = mybir.dt.float32, mybir.dt.bfloat16
    ALU, ACT, AX = mybir.AluOpType, mybir.ActivationFunctionType, mybir.AxisListType.X
    ctx = ExitStack()
    with ctx:
        def sb(name, shape, dt=fp32):
            return ctx.enter_context(nc.sbuf_tensor(name, shape, dt))

        per, names = {}, {}

        def sem(name, per_sequence=0):
            s = ctx.enter_context(nc.semaphore(name))
            per[name] = per_sequence
            names[id(s)] = name
            return s

        def nth(seq, s, n):
            return seq * per[names[id(s)]] + n

        ident = sb("ident", [P, P])
        ident_b = sb("ident_b", [P, P], bf16)
        headsum = sb("headsum", [P, NS, NC, 32])
        spread = sb("spread", [96, NJ, NC, P], bf16)
        mask = sb("mask", [P, T, NS, NJ * H])
        sameheads = sb("sameheads", [P, P])
        headof = sb("headof", [P, NC, 32])
        pairof = sb("pairof", [96, NPAIR, P], bf16)
        phasesum = sb("phasesum", [P, 2, 32])
        kernelof = sb("kernelof", [P, 4, 2, P])
        log_time = sb("log_time", [P, S])
        wqkv = sb("wqkv", [P, NC, 3 * C])
        wo = sb("wo", [P, NC, C])
        wr = sb("wr", [P, NC, C])
        wk = sb("wk", [P, NC, C])
        wv = sb("wv", [P, NC, C])
        w_in_k = sb("w_in_k", [P, NC, C])
        w_in_s = sb("w_in_s", [P, NC, 4, K2])
        w_in_q = sb("w_in_q", [P, NC, KQ, 2, 64])
        w_out = sb("w_out", [P, NC, C])
        theta_w = sb("theta_w", [P, NC, 8, P])
        tap_w = sb("tap_w", [P, NTAP, NC, P])
        conv_a = sb("conv_a", [P, NC, KCONV])
        conv_bk = sb("conv_bk", [P, NC, KS])
        conv_bs = sb("conv_bs", [P, KS])
        mu_r = sb("mu_r", [P, NC])
        mu_k = sb("mu_k", [P, NC])
        theta = sb("theta", [P, NC, M2])
        slope = sb("slope", [P, 8])
        score_scale = sb("score_scale", [P, 1])
        gains = sb("gains", [P, 6, H2])
        kind = sb("kind", [P, 3])
        half_pi = sb("half_pi", [P, 1])
        round_c = sb("round_c", [P, 1])
        minus_half = sb("minus_half", [P, TH])
        eps = sb("eps", [P, TH])

        x_in = sb("x_in", [P, T, C])
        xs = sb("xs", [P, T, C])
        h = sb("h", [P, T, C])
        hT = sb("hT", [P, NC, 1 + S])
        stats = sb("stats", [P, T, 6])
        mv = sb("mv", [P, T, 2])
        rstd = sb("rstd", [P, T])
        veps = sb("veps", [P, T])
        count = sb("count", [P, 1])
        neg_mr = sb("neg_mr", [P, T])

        ARENA = 28480
        arena = sb("arena", [P, ARENA])
        top = [0]

        def take(cols):
            a = arena[:, top[0]:top[0] + cols]
            top[0] += cols
            assert top[0] <= ARENA, top[0]
            return a

        qT = take(NC * S).rearrange("p (c n) -> p c n", c=NC)
        kT = take(NC * (PAD + S)).rearrange("p (c n) -> p c n", c=NC)
        vT = take(NC * (PAD + S)).rearrange("p (c n) -> p c n", c=NC)
        fqT = take(NC * S).rearrange("p (c n) -> p c n", c=NC)
        fkT = take(NC * S).rearrange("p (c n) -> p c n", c=NC)
        low_num = fkT
        hsumT = qT
        relus = take(4 * HALF).rearrange("p (r n) -> p r n", r=4)
        FKV = 2 * P + 1
        fkv = take(T * NC * FKV).rearrange("p (t c n) -> p t c n", t=T, c=NC)
        NPROD = 6
        prods = take(NPROD * NC * HALF).rearrange("p (r c n) -> p r c n", r=NPROD, c=NC)
        sT = take(HALF)
        sm = take(T * 96).rearrange("p (t s w) -> p t s w", t=T, s=NS)
        smx = take(TH * (4 * 32)).rearrange("p (t w) -> p t w", t=TH)
        srec = take(TH * H).rearrange("p (t w) -> p t w", t=TH)
        zrec = take(S // 4)
        wrest = take(TH * 96).rearrange("p (t w) -> p t w", t=TH * NS)
        kvbd = take(NC * P).rearrange("p (c n) -> p c n", c=NC)
        zsel = take(NC * 32).rearrange("p (c n) -> p c n", c=NC)
        w3 = take(TH * NS * 96 // 2).bitcast(bf16).rearrange("p (t s q w) -> p t s q w", t=TH, s=NS, q=3)
        w3T = relus.rearrange("p r n -> p (r n)")[:, 0:NS * HALF].bitcast(bf16)\
            .rearrange("p (f s n) -> p f s n", f=2, s=NS)[0:96]
        top[0] = 0
        dT = take(NC * S).rearrange("p (c n) -> p c n", c=NC)
        xkT = take(NC * S).rearrange("p (c n) -> p c n", c=NC)
        xrT = take(NC * S).rearrange("p (c n) -> p c n", c=NC)
        kact = take(NC * S).rearrange("p (c n) -> p c n", c=NC)
        gate = take(4 * HALF).rearrange("p (r n) -> p r n", r=4)
        gated = take(4 * HALF).rearrange("p (r n) -> p r n", r=4)
        top[0] = ARENA - T * C
        x_out = take(T * C).rearrange("p (t c) -> p t c", t=T)
        top[0] = 0
        ZP = KS - 1 + S
        z_raw = take(NC * ZP).rearrange("p (c n) -> p c n", c=NC)
        yT = z_raw[:, :, 0:S]
        zc = take(NC * S).rearrange("p (c n) -> p c n", c=NC)
        qpT = take(2 * KQ * S).rearrange("p (q n) -> p q n", q=2 * KQ)
        turns = take(2 * S).rearrange("p (r n) -> p r n", r=2)
        trig = take(2 * 2 * S).rearrange("p (r a n) -> p r a n", r=2, a=2)
        NNUM = 5
        nums = take((NNUM - 1) * 2 * S).rearrange("p (r a n) -> p r a n", r=NNUM - 1, a=2)
        num_ring = [nums[:, r] for r in range(NNUM - 1)] + [hT[:, :, 1:1 + S]]
        trig_ring = [trig[:, 0], trig[:, 1], h[:].rearrange("p t c -> p (t c)").rearrange("p (a n) -> p a n", a=2)]
        p3 = take(S // 2).bitcast(bf16)
        den_inv = take(S // 4)
        p_back = take(S // 4)
        thT = trig[:, 0]
        zs_raw = nums[:, 0].rearrange("p a n -> p (a n)")[:, 0:ZP]
        zs = nums[:, 1, 0]
        k1_tap = nums[:, 1, 1]
        pz = nums[:, 2].rearrange("p a n -> p (a n)")[:, 0:1 + S]
        pw = pz[:, 1:1 + S]
        ratio = nums[:, 0, 0]
        p_inv = nums[:, 0, 1]
        prest = nums[:, 3, 0]
        den = nums[:, 3, 1]
        p_anchor = trig[:, 0, 0]
        flat_prods = prods.rearrange("p r c n -> p (r c n)")
        spread_f = flat_prods[0:96, 0:NJ * NC * P]
        pairof_f = flat_prods[0:96, NJ * NC * P:(NJ * NC + NPAIR) * P]
        flat_xs = xs[:].rearrange("p t c -> p (t c)")
        wq_raw = flat_xs[:, 0:NC * 512].rearrange("p (c n) -> p c n", c=NC)
        wq_part = flat_xs[:, NC * 512:NC * 512 + 256].rearrange("p (q h m) -> p q h m", q=KQ, h=H2)

        PS = ctx.enter_context(nc.psum_tensor("PS", [P, 8, HALF], fp32))

        slopes_in = sem("slopes_in")
        attn_in = sem("attn_in")
        phase_in = sem("phase_in")
        slope_step = sem("slope_step")
        slope_act = sem("slope_act")
        pro_dve = sem("pro_dve")
        pro_act = sem("pro_act")
        fills = sem("fills")
        pro_pool = sem("pro_pool")
        x_loaded = sem("x_loaded", 16)
        out_stored = sem("out_stored", 16)
        stats_ready = sem("stats_ready", 8)
        mv_ready = sem("mv_ready", 8)
        veps_ready = sem("veps_ready", 8)
        rstd_ready = sem("rstd_ready", 8)
        neg_mr_ready = sem("neg_mr_ready", 8)
        h_ready = sem("h_ready", 32)
        hT_psum = sem("hT_psum", 16)
        hT_ready = sem("hT_ready", 16)
        xs_ready = sem("xs_ready", 12)
        out_ready = sem("out_ready", 4)
        qkv_psum = sem("qkv_psum", 12)
        qkv_sb = sem("qkv_sb", 12)
        exp_ready = sem("exp_ready", 8)
        elu_ready = sem("elu_ready", 8)
        xh_ready = sem("xh_ready", 2)
        pads_ready = sem("pads_ready", 1)
        zpads_ready = sem("zpads_ready", 1)
        qk_prod = sem("qk_prod", 21)
        qk_summed = sem("qk_summed", 21)
        sT_ready = sem("sT_ready", 2)
        stok_psum = sem("stok_psum", 2)
        soft = sem("soft", 2 * 14)
        exps_ready = sem("exps_ready", 2)
        whi_ready = sem("whi_ready", 2)
        wmid_ready = sem("wmid_ready", 2)
        w3T_psum = sem("w3T_psum", 4)
        w3T_ready = sem("w3T_ready", 4)
        fkv_psum = sem("fkv_psum", 8)
        fkv_ready = sem("fkv_ready", 8)
        kv_psum = sem("kv_psum", 1)
        kvbd_ready = sem("kvbd_ready", 2)
        z_psum = sem("z_psum", 1)
        z_ready = sem("z_ready", 2)
        low_psum = sem("low_psum", 4)
        low_ready = sem("low_ready", 4)
        wbc_psum = sem("wbc_psum", 24)
        wv_prod = sem("wv_prod", 24)
        wv_pool = sem("wv_pool", pool_adds(7))
        wv_own = sem("wv_own", own_adds(7))
        wv_acc = sem("wv_acc", 8)
        hsumT_ready = sem("hsumT_ready", 4)
        wo_psum = sem("wo_psum", 4)
        d_ready = sem("d_ready", 8)
        xk_ready = sem("xk_ready", 8)
        xr_ready = sem("xr_ready", 8)
        k_psum = sem("k_psum", 8)
        relu_ready = sem("relu_ready", 8)
        kact_ready = sem("kact_ready", 8)
        r_psum = sem("r_psum", 8)
        gate_ready = sem("gate_ready", 8)
        v_psum = sem("v_psum", 8)
        gated_ready = sem("gated_ready", 8)
        z_out = sem("z_out", NPROJ)
        z_sb = sem("z_sb", NPROJ)
        q_copied = sem("q_copied", 16 * 2 * KQ)
        sconv = sem("sconv", 12)
        p_ready = sem("p_ready", 1)
        p_inv_ready = sem("p_inv_ready", 1)
        p_anchor_ready = sem("p_anchor_ready", 1)
        ratio_step = sem("ratio_step", 4)
        phi_ready = sem("phi_ready", 1)
        prest_ready = sem("prest_ready", 1)
        pmid_ready = sem("pmid_ready", 1)
        p3_ready = sem("p3_ready", 1)
        den_step = sem("den_step", 4)
        kconv = sem("kconv", 3)
        k1_conv = sem("k1_conv", 6)
        turn_psum = sem("turn_psum", NPAIR)
        turn_rounded = sem("turn_rounded", NPAIR)
        turn_ready = sem("turn_ready", NPAIR)
        abs_ready = sem("abs_ready", NPAIR)
        trig_ready = sem("trig_ready", NPAIR)
        pbc_psum = sem("pbc_psum", NPAIR)
        weighted = sem("weighted", (K2 - NDECAY) // 2)
        num_re_ready = sem("num_re_ready", NPAIR)
        num_ready = sem("num_ready", NPAIR)
        prod_re = sem("prod_re", NPAIR)
        prod_im_even = sem("prod_im_even", NPAIR // 2)
        prod_im_odd = sem("prod_im_odd", NPAIR // 2)
        y_psum = sem("y_psum", 2 * 8)
        y_sb = sem("y_sb", 4)
        ibc_psum = sem("ibc_psum", 4)
        yn_ready = sem("yn_ready", 4)
        tanh_ready = sem("tanh_ready", 4)
        ys_ready = sem("ys_ready", 4)
        wout_psum = sem("wout_psum", 4)

        def sum_bank(hf):
            return 0 if hf else 2

        block = ctx.enter_context(nc.Block())

        PRO_DVE, PRO_ACT, PRO_POOL = 1 + NTAP * NC, 6, 2 + NC * 7

        @block.sync
        def _(sp):
            def load(dst, src, signal):
                sp.dma_start(dst, src).then_inc(signal, 16)

            def load_x(seq):
                sp.dma_start(x_in[:], x_dram[seq].rearrange("(t p) c -> p t c", p=P))\
                    .then_inc(x_loaded, 16)

            chunked = "(c p) n -> p c n"
            load(slope[:, 0:1], w["slopes"], slopes_in)
            load_x(0)
            for dst, src in ((wqkv[:], "Wqkv"), (conv_a[:], "conv_w")):
                load(dst, w[src].rearrange(chunked, p=P), attn_in)
            load(ident[:], k["ident"], attn_in)
            load(headsum[:].rearrange("p s c m -> p (s c m)"), k["headsum"], attn_in)
            load(mask[:].rearrange("p t s w -> p (t s w)"), k["mask"], attn_in)
            load(sameheads[:], k["sameheads"], attn_in)
            load(headof[:].rearrange("p c h -> p (c h)"), k["headof"], attn_in)
            load(kernelof[:].rearrange("p q a m -> p (q a m)"), k["kernelof"], attn_in)
            for dst, src in ((wo[:], "Wo"), (wr[:], "WrT"), (wk[:], "WkT")):
                load(dst, w[src].rearrange(chunked, p=P), attn_in)
            for c in range(NC):
                load(mu_r[:, c:c + 1], w["mu_r"][P * c:P * c + P, :], attn_in)
                load(mu_k[:, c:c + 1], w["mu_k"][P * c:P * c + P, :], attn_in)
            load(spread_f, k["spread"], phase_in)
            load(pairof_f, k["pairof"], phase_in)
            sp.dma_start(log_time[:], k["dist"]).then_inc(out_stored, 16)
            for dst, src in ((wv[:], "WvT"), (w_out[:], "W_out"), (theta[:], "theta"),
                             (w_in_s[:].rearrange("p c r k -> p c (r k)"), "W_in_s")):
                load(dst, w[src].rearrange(chunked, p=P), phase_in)
            w_in = w["W_in"].rearrange(chunked, p=P)
            load(wq_raw, w_in[:, :, C + K2:], phase_in)
            load(gains[:, 0:4, :].rearrange("p n h -> p (n h)"), w["gains"].to_broadcast([P, 4 * H2]), phase_in)
            load(w_in_k[:], w_in[:, :, 0:C], phase_in)
            load(conv_bs[:], w["conv_s"], phase_in)
            load(score_scale[:], w["score_scale"], phase_in)
            load(conv_bk[:], w["conv_kT"].rearrange(chunked, p=P), phase_in)
            load(phasesum[:].rearrange("p a m -> p (a m)"), k["phasesum"], phase_in)
            load(kind[:], k["kind"], phase_in)

            def store(seq):
                sp.wait_ge(out_ready, nth(seq, out_ready, 8))
                sp.dma_start(out_dram[seq].rearrange("(t p) c -> p t c", p=P), x_out[:])\
                    .then_inc(out_stored, 16)

            def copy_queries(seq):
                for q in range(KQ):
                    sp.wait_ge(z_sb, nth(seq, z_sb, 6 + 2 * q + 2))
                    sp.dma_start(qpT[64:128, 2 * q], qpT[0:64, 2 * q]).then_inc(q_copied, 16)
                    sp.dma_start(qpT[0:64, 2 * q + 1], qpT[64:128, 2 * q + 1]).then_inc(q_copied, 16)

            with sp.Fori(0, NSEQ - 1) as seq:
                sp.wait_ge(xh_ready, nth(seq, xh_ready, 2))
                load_x(seq + 1)
                copy_queries(seq)
                store(seq)
            sp.wait_ge(xh_ready, NSEQ * per["xh_ready"])
            load_x(NSEQ - 1)
            copy_queries(NSEQ - 1)
            store(NSEQ - 1)
            sp.wait_ge(x_loaded, (NSEQ + 1) * 16)
            sp.wait_ge(out_stored, (NSEQ + 1) * 16)

        ATTN_LOADS, PHASE_LOADS = 11 + 2 * NC, 14

        @block.gpsimd
        def _(pool):
            pool.memset(eps[:], EPS)
            pool.memset(half_pi[:], float(np.pi / 2))
            pool.memset(hT[:, :, 0:1], 0.0)
            pool.memset(round_c[:], ROUND).then_inc(fills, 1)
            pool.wait_ge(fills, 1)
            pool.memset(minus_half[:], -0.5).then_inc(out_ready, 4)

            def phase_weights():
                steps = [0]

                def link(i):
                    steps[0] += 1
                    i.then_inc(pro_pool, 1)
                    pool.wait_ge(pro_pool, steps[0])

                pool.wait_ge(phase_in, 16 * PHASE_LOADS)
                link(pool.tensor_tensor(gains[:, 4], gains[:, 0], gains[:, 2], ALU.mult))
                link(pool.tensor_tensor(gains[:, 5], gains[:, 1], gains[:, 3], ALU.mult))
                pool.wait_ge(pro_act, PRO_ACT)
                g_re = gains[:, 4:5, :].unsqueeze(3).to_broadcast([P, KQ, H2, M2])
                g_im = gains[:, 5:6, :].unsqueeze(3).to_broadcast([P, KQ, H2, M2])
                for c in range(NC):
                    raw = wq_raw[:, c].rearrange("p (q h m r) -> p q h m r", q=KQ, h=H2, m=M2)
                    q_re, q_im = raw[:, :, :, :, 0], raw[:, :, :, :, 1]
                    for part, (a, b, op) in enumerate(((q_re, q_im, ALU.subtract), (q_im, q_re, ALU.add))):
                        dst = w_in_q[:, c, :, part].rearrange("p q (h m) -> p q h m", h=H2)
                        link(pool.tensor_tensor(wq_part, b, g_im, ALU.mult))
                        link(pool.tensor_tensor(dst, a, g_re, ALU.mult))
                        link(pool.tensor_tensor(dst, dst, wq_part, op))
                    link(pool.tensor_tensor(theta_w[:, c].rearrange("p i (a m) -> p (i a) m", m=M2),
                                            ident[:].unsqueeze(2).to_broadcast([P, P, M2]),
                                            theta[:, c:c + 1, :].to_broadcast([P, P, M2]), ALU.mult))

            def rstd_of(seq, ln):
                for hf in range(2):
                    n = 2 * ln + hf + 1
                    cols = slice(TH * hf, TH * hf + TH)
                    pool.wait_ge(mv_ready, nth(seq, mv_ready, n))
                    pool.tensor_tensor(veps[:, cols], mv[:, cols, 1], eps[:], ALU.add)\
                        .then_inc(veps_ready, 1)
                    pool.wait_ge(veps_ready, nth(seq, veps_ready, n))
                    pool.tensor_tensor(rstd[:, cols], veps[:, cols], minus_half[:], ALU.pow)\
                        .then_inc(rstd_ready, 1)

            def ripple(seq):
                for hf in range(2):
                    pool.wait_ge(h_ready, nth(seq, h_ready, TH * (hf + 1)))
                    pool.wait_ge(out_ready, nth(seq, out_ready, 2 * hf + 2))
                    t = slice(TH * hf, TH * hf + TH)
                    pool.tensor_tensor(xs[:, t, :], x_in[:, t, :], h[:, t, :], ALU.add)\
                        .then_inc(xh_ready, 1)
                for hf in range(2):
                    for g in range(4):
                        first = 1 if 4 * hf + g in OWN_FIRST else 0
                        if (hf, g) == (1, 3):
                            break
                        for a in range(first, 2):
                            u = 12 * hf + 3 * g + a + 1
                            pool.wait_ge(wv_prod, nth(seq, wv_prod, u + 1))
                            if a == 1 and first:
                                pool.wait_ge(wv_own, nth(seq, wv_own, own_adds(4 * hf + g)))
                            elif a == 1:
                                pool.wait_ge(wv_pool, nth(seq, wv_pool, pool_adds(4 * hf + g) - 1))
                            pool.tensor_tensor(prods[:, u % NPROD], prods[:, u % NPROD],
                                               prods[:, (u - 1) % NPROD], ALU.add)\
                                .then_inc(wv_pool, 1)

            def conv_k1(seq):
                pool.wait_ge(zpads_ready, nth(seq, zpads_ready, 1))
                pool.wait_ge(z_sb, nth(seq, z_sb, AFTER_K[1]))
                for j in range(KS - 1):
                    if j:
                        pool.wait_ge(k1_conv, nth(seq, k1_conv, 2 * j))
                    pool.tensor_tensor(k1_tap, z_raw[:, 1, j:j + S], conv_bk[:, 1, j:j + 1].to_broadcast([P, S]),
                                       ALU.mult).then_inc(k1_conv, 1)
                    pool.wait_ge(k1_conv, nth(seq, k1_conv, 2 * j + 1))
                    pool.tensor_tensor(zc[:, 1], zc[:, 1], k1_tap, ALU.add).then_inc(k1_conv, 1)

            def phase(seq):
                conv_k1(seq)
                pool.wait_ge(q_copied, nth(seq, q_copied, 16 * 2 * KQ))
                for n, i in enumerate(ORDER):
                    g = num_ring[n % NNUM]
                    pool.wait_ge(num_re_ready, nth(seq, num_re_ready, n + 1))
                    pool.tensor_tensor(g[:, 0], g[:, 0], qpT[:, 2 * (i // 4)], ALU.mult)\
                        .then_inc(prod_re, 1)
                    if n % 2 == 0:
                        pool.wait_ge(num_ready, nth(seq, num_ready, n + 1))
                        pool.tensor_tensor(g[:, 1], g[:, 1], qpT[:, 2 * (i // 4) + 1], ALU.mult)\
                            .then_inc(prod_im_even, 1)

            rstd_of(0, 0)
            phase_weights()
            with pool.Fori(0, NSEQ) as seq:
                ripple(seq)
                rstd_of(seq, 1)
                rstd_of(seq, 2)
                phase(seq)
                rstd_of(seq, 3)
                rstd_of(seq + 1, 0)

        @block.scalar
        def _(act):
            act.wait_ge(fills, 1)
            act.wait_ge(slope_step, 1)
            act.activation(slope[:, 2:3], slope[:, 1:2], ACT.Exp, scale=-1.0).then_inc(slope_act, 1)
            act.wait_ge(slope_step, 2)
            act.activation(slope[:, 4:5], slope[:, 3:4], ACT.Ln).then_inc(slope_act, 1)

            def normalise(seq, ln, x, hf):
                for t in range(TH * hf, TH * hf + TH):
                    if t % TH == 0:
                        act.wait_ge(neg_mr_ready, nth(seq, neg_mr_ready, 2 * ln + hf + 1))
                    act.activation(h[:, t, :], x[:, t, :], ACT.Identity, bias=neg_mr[:, t:t + 1],
                                   scale=rstd[:, t:t + 1]).then_inc(h_ready, 1)

            def evacuate_hT(seq, ln, hf):
                for c in range(NC):
                    act.wait_ge(hT_psum, nth(seq, hT_psum, 4 * ln + 2 * hf + c + 1))
                    a = 1 + HALF * hf
                    act.activation(hT[:, c, a:a + HALF], PS[:, 2 * hf + c], ACT.Copy)\
                        .then_inc(hT_ready, 1)

            def qkv_out(seq, ns):
                for n in ns:
                    hf, m = n // 6, n % 6
                    c = m % 2
                    a = HALF * hf
                    bank = PS[:, 4 + n % 4]
                    act.wait_ge(qkv_psum, nth(seq, qkv_psum, n + 1))
                    if m < 4:
                        e = 4 * hf + m
                        dst = (fkT if m < 2 else fqT)[:, c, a:a + HALF]
                        act.activation(dst, bank, ACT.Exp)
                        if e >= 4:
                            act.wait_ge(elu_ready, nth(seq, elu_ready, e - 3))
                        act.activation(relus[:, e % 4], bank, ACT.Relu).then_inc(exp_ready, 1)
                    if m < 2:
                        dst = kT[:, c, PAD + a:PAD + a + HALF]
                    elif m < 4:
                        dst = qT[:, c, a:a + HALF]
                    else:
                        dst = vT[:, c, PAD + a:PAD + a + HALF]
                    act.activation(dst, bank, ACT.Copy).then_inc(qkv_sb, 1)

            def ripple(seq):
                act.wait_ge(out_ready, nth(seq, out_ready, 4))
                qkv_out(seq, range(4))
                evacuate_hT(seq, 0, 1)
                qkv_out(seq, range(4, 12))
                act.wait_ge(qk_summed, nth(seq, qk_summed, 10))
                act.wait_ge(out_stored, nth(seq, out_stored, 16))
                act.activation(sT, PS[:, 0], ACT.Copy).then_inc(sT_ready, 1)
                for t in range(T):
                    act.wait_ge(fkv_psum, nth(seq, fkv_psum, t + 1))
                    act.activation(fkv[:, t, :, 0:2 * P],
                                   PS[:, 4 + t % 4].rearrange("p (c n) -> p c n", c=NC), ACT.Copy)\
                        .then_inc(fkv_ready, 1)
                    if t == 5:
                        softmax_exp(seq, 0)
                high_part(seq, 0)
                middle_part(seq, 0)
                evacuate_w3T(seq, 0, 0)
                act.wait_ge(qk_summed, nth(seq, qk_summed, 21))
                act.activation(sT, PS[:, 0], ACT.Copy).then_inc(sT_ready, 1)
                evacuate_w3T(seq, 0, 1)
                softmax_exp(seq, 1)
                low_out(seq, 0)
                low_out(seq, 1)
                high_part(seq, 1)
                low_out(seq, 2)
                middle_part(seq, 1)
                low_out(seq, 3)
                evacuate_w3T(seq, 1, 0)
                evacuate_w3T(seq, 1, 1)
                for hf in range(2):
                    if hf == 1:
                        normalise(seq, 1, xs, 0)
                    for c in range(NC):
                        act.wait_ge(wv_acc, nth(seq, wv_acc, 4 * hf + 4))
                        act.activation(hsumT[:, c, HALF * hf:HALF * hf + HALF], PS[:, sum_bank(hf) + c], ACT.Copy)\
                            .then_inc(hsumT_ready, 1)

            def softmax_exp(seq, hf):
                act.wait_ge(soft, nth(seq, soft, 14 * hf + 6))
                t = slice(TH * hf, TH * hf + TH)
                act.activation(sm[:, t], sm[:, t], ACT.Exp, scale=float(D) ** -0.5)\
                    .then_inc(exps_ready, 1)

            def low_out(seq, n):
                act.wait_ge(low_psum, nth(seq, low_psum, n + 1))
                c, hf = n % 2, n // 2
                act.activation(low_num[:, c, HALF * hf:HALF * hf + HALF], PS[:, 0], ACT.Copy)\
                    .then_inc(low_ready, 1)

            def high_part(seq, hf):
                act.wait_ge(soft, nth(seq, soft, 14 * hf + 12))
                if hf == 1:
                    act.wait_ge(w3T_psum, nth(seq, w3T_psum, 2))
                t = slice(TH * hf, TH * hf + TH)
                act.activation(w3.rearrange("p t s q w -> p (t s) q w")[:, :, 0],
                               sm[:, t].rearrange("p t s w -> p (t s) w"), ACT.Copy).then_inc(whi_ready, 1)

            def middle_part(seq, hf):
                act.wait_ge(soft, nth(seq, soft, 14 * hf + 13))
                act.activation(w3.rearrange("p t s q w -> p (t s) q w")[:, :, 1], wrest, ACT.Copy)\
                    .then_inc(wmid_ready, 1)

            def evacuate_w3T(seq, hf, which):
                bank = PS[0:96, 1].bitcast(bf16).rearrange("p (s n) -> p s n", s=2)
                act.wait_ge(w3T_psum, nth(seq, w3T_psum, 2 * hf + 1 + which))
                dst, src = (w3T[:, hf, 2], bank[:, 0]) if which else (w3T[:, hf, 0:2], bank)
                act.activation(dst, src, ACT.Copy).then_inc(w3T_ready, 1)

            def ffn(seq, f):
                def keys(hf):
                    for m in range(NC):
                        n = 4 * f + 2 * hf + m + 1
                        a = slice(HALF * hf, HALF * hf + HALF)
                        act.wait_ge(k_psum, nth(seq, k_psum, n))
                        act.activation(kact[:, m, a], PS[:, 4 + 2 * hf + m], ACT.Relu)\
                            .then_inc(relu_ready, 1)
                        act.wait_ge(relu_ready, nth(seq, relu_ready, n))
                        act.activation(kact[:, m, a], kact[:, m, a], ACT.Square)\
                            .then_inc(kact_ready, 1)

                def gates(hf):
                    for tp in (2 * hf, 2 * hf + 1):
                        act.wait_ge(r_psum, nth(seq, r_psum, 4 * f + tp + 1))
                        act.activation(gate[:, tp], PS[:, tp], ACT.Tanh, scale=0.5)\
                            .then_inc(gate_ready, 1)

                keys(0)
                gates(0)
                keys(1)
                if f == 1:
                    normalise(seq + 1, 0, x_in, 0)
                gates(1)
                if f == 1:
                    evacuate_hT(seq + 1, 0, 0)
                    normalise(seq + 1, 0, x_in, 1)

            def rounded(seq, n):
                act.wait_ge(turn_psum, nth(seq, turn_psum, n + 1))
                if n >= 2:
                    act.wait_ge(trig_ready, nth(seq, trig_ready, n - 1))
                a = 2 * (n % 2)
                act.activation(turns[:, n % 2].rearrange("p (b n) -> p b n", b=2), PS[:, a:a + 2],
                               ACT.Identity, bias=round_c[:]).then_inc(turn_rounded, 1)

            def phase_project(seq):
                for n, (what, c, hf) in enumerate(PROJECTIONS):
                    bank = PS[:, 4 + n % 4]
                    a = HALF * hf
                    if n == FIRST_HALF:
                        evacuate_hT(seq, 2, 1)
                    act.wait_ge(z_out, nth(seq, z_out, n + 1))
                    if what == "q":
                        act.activation(qpT[0:64, 2 * c, a:a + HALF], bank[0:64], ACT.Copy)
                        act.activation(qpT[64:128, 2 * c + 1, a:a + HALF], bank[64:128], ACT.Copy)\
                            .then_inc(z_sb, 1)
                    else:
                        raw = zs_raw if what == "s" else z_raw[:, c]
                        first = zs if what == "s" else zc[:, c]
                        tap = conv_bs[:, KS - 1:KS] if what == "s" else conv_bk[:, c, KS - 1:KS]
                        act.activation(first[:, a:a + HALF], bank, ACT.Copy, scale=tap)
                        act.activation(raw[:, KS - 1 + a:KS - 1 + a + HALF], bank, ACT.Copy)\
                            .then_inc(z_sb, 1)
                    if n == EXP_AT:
                        act.wait_ge(sconv, nth(seq, sconv, 12))
                        act.activation(pw, zs, ACT.Exp).then_inc(p_ready, 1)
                        act.activation(p_inv, zs, ACT.Exp, scale=kind[:, 2:3]).then_inc(p_inv_ready, 1)
                        act.wait_ge(p_ready, nth(seq, p_ready, 1))
                        act.activation(p_anchor, pw, ACT.Copy, scale=kind[:, 1:2]).then_inc(p_anchor_ready, 1)
                    if n == HIGH_AT:
                        act.wait_ge(ratio_step, nth(seq, ratio_step, 4))
                        act.activation(p3[0:96], ratio[0:96], ACT.Copy).then_inc(phi_ready, 1)
                    if n == TURN_AT:
                        rounded(seq, 0)
                    if n == MID_AT:
                        act.wait_ge(prest_ready, nth(seq, prest_ready, 1))
                        act.activation(p3[0:64], prest[0:64], ACT.Copy).then_inc(pmid_ready, 1)

            def phase_units(seq):
                def sums_out(c):
                    for hf in range(2):
                        act.wait_ge(y_psum, nth(seq, y_psum, 8 * c + 8))
                        act.activation(yT[:, c, HALF * hf:HALF * hf + HALF], PS[:, 6 + hf], ACT.Copy)\
                            .then_inc(y_sb, 1)

                rounded(seq, 1)
                for n in range(NPAIR):
                    act.wait_ge(turn_ready, nth(seq, turn_ready, n + 1))
                    if n >= 3:
                        act.wait_ge(num_ready, nth(seq, num_ready, n - 2))
                    slot = trig_ring[n % 3]
                    act.activation(slot[:, 0], turns[:, n % 2], ACT.Abs).then_inc(abs_ready, 1)
                    act.activation(slot[:, 1], turns[:, n % 2], ACT.Sin, scale=-TWO_PI)
                    act.wait_ge(abs_ready, nth(seq, abs_ready, n + 1))
                    act.activation(slot[:, 0], slot[:, 0], ACT.Sin, bias=half_pi[:],
                                   scale=-TWO_PI).then_inc(trig_ready, 1)
                    if n + 2 < NPAIR:
                        rounded(seq, n + 2)
                    if n == SUMS_AT:
                        sums_out(0)
                for n in range(4):
                    c, a = n // 2, HALF * (n % 2)
                    if n == 2:
                        sums_out(1)
                    act.wait_ge(yn_ready, nth(seq, yn_ready, n + 1))
                    act.activation(thT[:, c, a:a + HALF], yT[:, c, a:a + HALF], ACT.Tanh, scale=0.5)\
                        .then_inc(tanh_ready, 1)

            normalise(0, 0, x_in, 0)
            evacuate_hT(0, 0, 0)
            normalise(0, 0, x_in, 1)
            act.wait_ge(phase_in, 16 * PHASE_LOADS)
            act.activation(spread[:].rearrange("p j c m -> p (j c m)"), spread_f, ACT.Copy).then_inc(pro_act, 1)
            act.activation(pairof[:].rearrange("p i m -> p (i m)"), pairof_f, ACT.Copy).then_inc(pro_act, 1)
            act.activation(theta[:], theta[:], ACT.Copy, scale=float(1 / (2 * np.pi))).then_inc(pro_act, 1)
            act.activation(wv[:], wv[:], ACT.Copy, scale=0.5).then_inc(pro_act, 1)
            act.activation(w_out[:], w_out[:], ACT.Copy, scale=0.5).then_inc(pro_act, 1)
            act.wait_ge(out_stored, 16)
            act.wait_ge(slope_step, 11)
            act.activation(log_time[:], log_time[:], ACT.Copy, scale=slope[:, 7:8]).then_inc(pro_act, 1)
            with act.Fori(0, NSEQ) as seq:
                ripple(seq)
                evacuate_hT(seq, 1, 0)
                normalise(seq, 1, xs, 1)
                evacuate_hT(seq, 1, 1)
                ffn(seq, 0)
                normalise(seq, 2, xs, 0)
                evacuate_hT(seq, 2, 0)
                normalise(seq, 2, xs, 1)
                phase_project(seq)
                phase_units(seq)
                normalise(seq, 3, xs, 0)
                evacuate_hT(seq, 3, 0)
                normalise(seq, 3, xs, 1)
                evacuate_hT(seq, 3, 1)
                ffn(seq, 1)

        @block.vector
        def _(dve):
            def moments(seq, ln, x, hf):
                n = 2 * ln + hf + 1
                if ln == 0:
                    dve.wait_ge(x_loaded, nth(seq, x_loaded, 16))
                else:
                    dve.wait_ge(xs_ready, nth(seq, xs_ready, 4 * (ln - 1) + 2 * hf + 2))
                for t in range(TH * hf, TH * hf + TH):
                    last = dve.bn_stats(stats[:, t], x[:, t, :])
                last.then_inc(stats_ready, 1)
                dve.wait_ge(stats_ready, nth(seq, stats_ready, n))
                dve.tensor_copy(count[:], stats[:, TH * hf, 0:1])
                for t in range(TH * hf, TH * hf + TH):
                    last = dve.bn_aggr(mv[:, t], stats[:, t])
                last.then_inc(mv_ready, 1)

            def shift_of(seq, ln, hf):
                n = 2 * ln + hf + 1
                t = slice(TH * hf, TH * hf + TH)
                dve.wait_ge(rstd_ready, nth(seq, rstd_ready, n))
                dve.scalar_tensor_tensor(neg_mr[:, t], mv[:, t, 0], -1.0, rstd[:, t], ALU.mult, ALU.mult)\
                    .then_inc(neg_mr_ready, 1)

            def ripple(seq):
                for buf in (kT, vT):
                    dve.memset(buf[:, :, 0:PAD], 0.0)
                dve.memset(fkv[:, :, :, 2 * P:2 * P + 1], 1.0).then_inc(pads_ready, 1)
                dve.wait_ge(pads_ready, nth(seq, pads_ready, 1))

                def scores(u):
                    hf, o = (0, u) if u < 10 else (1, u - 10)
                    a = HALF * hf
                    if u % 10 == 0 and u < 20:
                        dve.wait_ge(qkv_sb, nth(seq, qkv_sb, 6 * hf + 4))
                    if u >= 4:
                        dve.wait_ge(qk_summed, nth(seq, qk_summed, u - 3))
                    b = PAD + a - OFFS[o]
                    dve.tensor_tensor(prods[:, u % 4], qT[:, :, a:a + HALF], kT[:, :, b:b + HALF],
                                      ALU.mult).then_inc(qk_prod, 1)

                def elu(e):
                    hf, m = e // 4, e % 4
                    dst = (fkT if m < 2 else fqT)[:, m % 2, HALF * hf:HALF * hf + HALF]
                    dve.wait_ge(exp_ready, nth(seq, exp_ready, e + 1))
                    dve.scalar_tensor_tensor(dst, dst, 1.0, relus[:, e % 4], ALU.min, ALU.add)\
                        .then_inc(elu_ready, 1)

                def chained(hf, n, i):
                    i.then_inc(soft, 1)
                    dve.wait_ge(soft, nth(seq, soft, 14 * hf + n))

                def over_slots(hf, n, op, src, dst):
                    chained(hf, n, dve.tensor_tensor(smx[:, :, 0:48], src[:, :, 0:48], src[:, :, 48:96], op))
                    chained(hf, n + 1, dve.tensor_tensor(smx[:, :, 48:72], smx[:, :, 0:24], smx[:, :, 24:48], op))
                    chained(hf, n + 2, dve.tensor_tensor(smx[:, :, 72:80], smx[:, :, 48:56], smx[:, :, 56:64], op))
                    chained(hf, n + 3, dve.tensor_tensor(dst, smx[:, :, 72:80], smx[:, :, 64:72], op))

                def soft_max(hf):
                    t = slice(TH * hf, TH * hf + TH)
                    flat = sm[:, t].rearrange("p t s w -> p t (s w)")
                    bank = PS[:, 1].rearrange("p (t j w) -> p t j w", t=TH, j=NJ)
                    dve.wait_ge(stok_psum, nth(seq, stok_psum, hf + 1))
                    for s in range(NS):
                        last = dve.tensor_tensor(sm[:, t, s].rearrange("p t (j h) -> p t j h", j=NJ),
                                                 bank[:, :, :, s * H:s * H + H],
                                                 mask[:, t, s].rearrange("p t (j h) -> p t j h", j=NJ), ALU.add)
                    chained(hf, 1, last)
                    over_slots(hf, 2, ALU.max, flat, srec)
                    chained(hf, 6, dve.tensor_tensor(
                        flat.rearrange("p t (o h) -> p t o h", h=H), flat.rearrange("p t (o h) -> p t o h", h=H),
                        srec.unsqueeze(2).to_broadcast([P, TH, NS * NJ, H]), ALU.subtract))

                def soft_norm(hf):
                    t = slice(TH * hf, TH * hf + TH)
                    flat = sm[:, t].rearrange("p t s w -> p t (s w)")
                    dve.wait_ge(exps_ready, nth(seq, exps_ready, hf + 1))
                    over_slots(hf, 7, ALU.add, flat, srec)
                    chained(hf, 11, dve.reciprocal(srec, srec))
                    chained(hf, 12, dve.tensor_tensor(
                        flat.rearrange("p t (o h) -> p t o h", h=H), flat.rearrange("p t (o h) -> p t o h", h=H),
                        srec.unsqueeze(2).to_broadcast([P, TH, NS * NJ, H]), ALU.mult))

                def soft_split(hf):
                    t = slice(TH * hf, TH * hf + TH)
                    flat = sm[:, t].rearrange("p t s w -> p (t s) w")
                    parts = w3.rearrange("p t s q w -> p (t s) q w")
                    dve.wait_ge(whi_ready, nth(seq, whi_ready, hf + 1))
                    chained(hf, 13, dve.tensor_tensor(wrest, flat, parts[:, :, 0], ALU.subtract))
                    dve.wait_ge(wmid_ready, nth(seq, wmid_ready, hf + 1))
                    chained(hf, 14, dve.tensor_tensor(parts[:, :, 2], wrest, parts[:, :, 1], ALU.subtract))

                def low_state():
                    dve.wait_ge(kv_psum, nth(seq, kv_psum, 1))
                    for c in range(NC):
                        dve.tensor_tensor(kvbd[:, c], PS[:, 2 + c, 0:P], sameheads[:], ALU.mult)
                        dve.tensor_scalar(zsel[:, c], headof[:, c], PS[:, 2 + c, P:P + 1], None, ALU.mult)\
                            .then_inc(kvbd_ready, 1)

                def low_z():
                    dve.wait_ge(z_psum, nth(seq, z_psum, 1))
                    dve.tensor_scalar(zrec, PS[:, 0, 0:S // 4], 1e-6, None, ALU.add).then_inc(z_ready, 1)
                    dve.wait_ge(z_ready, nth(seq, z_ready, 1))
                    dve.reciprocal(zrec, zrec).then_inc(z_ready, 1)

                def values(hf, o):
                    u = 12 * hf + o
                    a = HALF * hf
                    dve.wait_ge(wbc_psum, nth(seq, wbc_psum, u + 1))
                    if u >= NPROD:
                        v = u - NPROD
                        if v % 3 == 2:
                            dve.wait_ge(wv_acc, nth(seq, wv_acc, v // 3 + 1))
                        elif v % 3 == 1:
                            dve.wait_ge(wv_pool, nth(seq, wv_pool, pool_adds(v // 3)))
                        elif v // 3 not in OWN_FIRST:
                            dve.wait_ge(wv_pool, nth(seq, wv_pool, pool_adds(v // 3) - 1))
                    pair = 4 + 2 * (u % 2)
                    dst = prods[:, u % NPROD]
                    if o == LOW:
                        dve.wait_ge(low_ready, nth(seq, low_ready, 4))
                        dve.tensor_tensor(dst, PS[:, pair:pair + 2], low_num[:, :, a:a + HALF], ALU.mult)\
                            .then_inc(wv_prod, 1)
                        return
                    if o == 0 and hf == 0:
                        dve.wait_ge(qkv_sb, nth(seq, qkv_sb, 12))
                    b = PAD + a - OFFS[o]
                    if OFFS[o] < KCONV:
                        j = KCONV - 1 - OFFS[o]
                        dve.scalar_tensor_tensor(dst[:, 0], PS[:, pair], conv_a[:, 0, j:j + 1],
                                                 vT[:, 0, b:b + HALF], ALU.add, ALU.mult)
                        dve.scalar_tensor_tensor(dst[:, 1], PS[:, pair + 1], conv_a[:, 1, j:j + 1],
                                                 vT[:, 1, b:b + HALF], ALU.add, ALU.mult)\
                            .then_inc(wv_prod, 1)
                    else:
                        dve.tensor_tensor(dst, PS[:, pair:pair + 2], vT[:, :, b:b + HALF], ALU.mult)\
                            .then_inc(wv_prod, 1)

                for u in range(21):
                    scores(u)
                    if u < 4:
                        elu(u)
                    if 10 <= u < 14:
                        elu(u - 6)
                    if u == 13:
                        soft_max(0)
                    if u == 14:
                        soft_norm(0)
                    if u == 16:
                        soft_split(0)
                    if u == 18:
                        low_state()
                dve.wait_ge(qk_summed, nth(seq, qk_summed, 21))

                def own_add(hf, o):
                    u, g = 12 * hf + o, o // 3
                    if o % 3 == 1 and 4 * hf + g in OWN_FIRST:
                        dve.wait_ge(wv_prod, nth(seq, wv_prod, u + 1))
                        dve.tensor_tensor(prods[:, u % NPROD], prods[:, u % NPROD], prods[:, (u - 1) % NPROD],
                                          ALU.add).then_inc(wv_own, 1)
                        dve.wait_ge(wv_own, nth(seq, wv_own, own_adds(4 * hf + g)))

                for o in range(NO + 1):
                    values(0, o)
                    own_add(0, o)
                    if o == 1:
                        soft_max(1)
                    if o == 3:
                        soft_norm(1)
                    if o == 4:
                        low_z()
                    if o == 6:
                        soft_split(1)
                for o in range(NO + 1):
                    values(1, o)
                    own_add(1, o)
                    if o == LN_AT:
                        for tp in (0, 1):
                            residual(seq, 0, tp, wo_psum, 2 + tp % 2)
                        moments(seq, 1, xs, 0)
                shift_of(seq, 1, 0)

            def between(seq, ln, add_pair):
                add_pair(0)
                add_pair(1)
                moments(seq, ln, xs, 0)
                shift_of(seq, ln, 0)
                add_pair(2)
                add_pair(3)
                moments(seq, ln, xs, 1)
                shift_of(seq, ln, 1)

            def residual(seq, layer, tp, ready, bank):
                dve.wait_ge(ready, nth(seq, ready, tp + 1))
                if layer == 0:
                    dve.wait_ge(xh_ready, nth(seq, xh_ready, 2))
                x = xs[:, 2 * tp:2 * tp + 2, :]
                dve.tensor_tensor(x, x, PS[:, bank].rearrange("p (t c) -> p t c", t=2), ALU.add)\
                    .then_inc(xs_ready, 1)

            def mix_keys(seq, f, hf):
                a = HALF * hf
                for c in range(NC):
                    n = 4 * f + 2 * hf + c + 1
                    dve.wait_ge(hT_ready, nth(seq, hT_ready, (4 if f == 0 else 12) + 2 * hf + c + 1))
                    dve.tensor_tensor(dT[:, c, a:a + HALF], hT[:, c, a + 1:a + 1 + HALF],
                                      hT[:, c, a:a + HALF], ALU.subtract).then_inc(d_ready, 1)
                    dve.wait_ge(d_ready, nth(seq, d_ready, n))
                    dve.scalar_tensor_tensor(xkT[:, c, a:a + HALF], dT[:, c, a:a + HALF], mu_k[:, c:c + 1],
                                             hT[:, c, a:a + HALF], ALU.mult, ALU.add).then_inc(xk_ready, 1)

            def mix_gates(seq, f, hf):
                a = HALF * hf
                for c in range(NC):
                    dve.wait_ge(d_ready, nth(seq, d_ready, 4 * f + 2 * hf + c + 1))
                    dve.scalar_tensor_tensor(xrT[:, c, a:a + HALF], dT[:, c, a:a + HALF], mu_r[:, c:c + 1],
                                             hT[:, c, a:a + HALF], ALU.mult, ALU.add).then_inc(xr_ready, 1)

            def ffn(seq, f):
                for hf in range(2):
                    mix_keys(seq, f, hf)
                    mix_gates(seq, f, hf)

            def ffn_out(seq, f, tp):
                n = 4 * f + tp + 1
                dve.wait_ge(gate_ready, nth(seq, gate_ready, n))
                dve.wait_ge(v_psum, nth(seq, v_psum, n))
                dve.scalar_tensor_tensor(gated[:, tp], gate[:, tp], 1.0, PS[:, 4 + tp], ALU.add, ALU.mult)\
                    .then_inc(gated_ready, 1)
                dve.wait_ge(gated_ready, nth(seq, gated_ready, n))
                t = slice(2 * tp, 2 * tp + 2)
                add = gated[:, tp].rearrange("p (t c) -> p t c", t=2)
                if f == 0:
                    dve.tensor_tensor(xs[:, t, :], xs[:, t, :], add, ALU.add).then_inc(xs_ready, 1)
                else:
                    dve.tensor_tensor(x_out[:, t, :], xs[:, t, :], add, ALU.add).then_inc(out_ready, 1)

            def phase(seq):
                dve.memset(z_raw[:, :, 0:KS - 1], 0.0)
                dve.memset(pz[:, 0:1], 0.0)
                dve.memset(zs_raw[:, 0:KS - 1], 0.0).then_inc(zpads_ready, 1)
                dve.wait_ge(zpads_ready, nth(seq, zpads_ready, 1))

                def s_step(n, i):
                    i.then_inc(sconv, 1)
                    dve.wait_ge(sconv, nth(seq, sconv, n))

                def k_conv(j):
                    if j == 0:
                        dve.wait_ge(z_sb, nth(seq, z_sb, AFTER_K[0]))
                    else:
                        dve.wait_ge(kconv, nth(seq, kconv, j))
                    dve.scalar_tensor_tensor(zc[:, 0], z_raw[:, 0, j:j + S], conv_bk[:, 0, j:j + 1], zc[:, 0],
                                             ALU.mult, ALU.add).then_inc(kconv, 1)

                def ratio_to(n, i):
                    i.then_inc(ratio_step, 1)
                    dve.wait_ge(ratio_step, nth(seq, ratio_step, n))

                def turn(n):
                    a = 2 * (n % 2)
                    dve.wait_ge(turn_rounded, nth(seq, turn_rounded, n + 1))
                    t = turns[:, n % 2].rearrange("p (b n) -> p b n", b=2)
                    dve.scalar_tensor_tensor(t, t, -ROUND, PS[:, a:a + 2], ALU.add, ALU.subtract)\
                        .then_inc(turn_ready, 1)

                for hf in range(2):
                    a, n = HALF * hf, 6 * hf
                    half = zs[:, a:a + HALF]
                    dve.wait_ge(z_sb, nth(seq, z_sb, AFTER_S[hf]))
                    for j in range(KS - 1):
                        s_step(n + j + 1, dve.scalar_tensor_tensor(half, zs_raw[:, a + j:a + j + HALF],
                                                                   conv_bs[:, j:j + 1], half, ALU.mult, ALU.add))
                    s_step(n + 4, dve.tensor_scalar(half, half, score_scale[:], 20.0, ALU.mult, ALU.min))
                    s_step(n + 5, dve.scalar_tensor_tensor(half, half, -20.0, log_time[:, a:a + HALF],
                                                           ALU.max, ALU.add))
                    s_step(n + 6, dve.tensor_scalar(half, half, LOG_MIN, None, ALU.max))
                k_conv(0)
                k_conv(1)
                dve.wait_ge(p_ready, nth(seq, p_ready, 1))
                dve.wait_ge(p_inv_ready, nth(seq, p_inv_ready, 1))
                ratio_to(1, dve.tensor_tensor(ratio, pw, p_inv, ALU.mult))
                ratio_to(2, dve.scalar_tensor_tensor(ratio, ratio, -2.0, p_inv, ALU.add, ALU.mult))
                ratio_to(3, dve.scalar_tensor_tensor(ratio, pz[:, 0:S], kind[:, 2:3], ratio, ALU.mult, ALU.mult))
                dve.wait_ge(p_anchor_ready, nth(seq, p_anchor_ready, 1))
                ratio_to(4, dve.tensor_tensor(ratio, ratio, p_anchor, ALU.add))
                k_conv(2)
                dve.wait_ge(phi_ready, nth(seq, phi_ready, 1))
                dve.tensor_tensor(prest[0:64], ratio[0:64], p3[0:64], ALU.subtract).then_inc(prest_ready, 1)
                turn(0)
                dve.wait_ge(pmid_ready, nth(seq, pmid_ready, 1))
                dve.tensor_tensor(p3[32:64], prest[32:64], p3[32:64], ALU.subtract).then_inc(p3_ready, 1)

                def denominators():
                    dve.tensor_tensor_scan(den, pw, pw, 0.0, ALU.add, ALU.bypass).then_inc(den_step, 1)
                    dve.wait_ge(den_step, nth(seq, den_step, 1))
                    for q in range(4):
                        r = slice(32 * q, 32 * q + 32)
                        dve.tensor_scalar(den_inv[r], den[r, 256 * q:256 * q + 256], 0.0001, None, ALU.max)
                        last = dve.tensor_scalar(p_back[r], pw[r, 256 * q:256 * q + 256], kind[r, 0:1],
                                                 kind[r, 1:2], ALU.mult, ALU.add)
                    last.then_inc(den_step, 1)

                def invert_denominators():
                    dve.wait_ge(den_step, nth(seq, den_step, 2))
                    dve.reciprocal(den_inv, den_inv).then_inc(den_step, 1)
                    dve.wait_ge(den_step, nth(seq, den_step, 3))
                    dve.tensor_tensor(den_inv, den_inv, p_back, ALU.mult).then_inc(den_step, 1)

                turn(1)
                denominators()
                for n, i in enumerate(ORDER):
                    if 2 <= n + 1 < NPAIR:
                        turn(n + 1)
                    g = num_ring[n % NNUM]
                    flat = PS[:, 4:6].rearrange("p b n -> p (b n)")
                    dve.wait_ge(trig_ready, nth(seq, trig_ready, n + 1))
                    dve.wait_ge(pbc_psum, nth(seq, pbc_psum, n + 1))
                    if n >= NNUM:
                        dve.wait_ge(y_psum, nth(seq, y_psum, n - NNUM + 1))
                    if i < NDECAY // 2:
                        if n == 0:
                            dve.wait_ge(p3_ready, nth(seq, p3_ready, 1))
                        if n == 1:
                            dve.wait_ge(k1_conv, nth(seq, k1_conv, 6))
                        for a, done in ((0, num_re_ready), (1, num_ready)):
                            if n == 2:
                                dve.wait_ge(den_step, nth(seq, den_step, 2))
                            dve.tensor_tensor_scan(g[:, a], flat, trig_ring[n % 3][:, a], 0.0, ALU.mult, ALU.add)\
                                .then_inc(done, 1)
                    else:
                        for a in range(2):
                            last = dve.tensor_tensor(g[:, a], trig_ring[n % 3][:, a], flat, ALU.mult)
                        last.then_inc(weighted, 1)
                        dve.wait_ge(weighted, nth(seq, weighted, 1 + (n == NPAIR - 1)))
                        for a, done in ((0, num_re_ready), (1, num_ready)):
                            dve.tensor_tensor_scan(g[:, a], g[:, a], g[:, a], 0.0, ALU.add, ALU.bypass)\
                                .then_inc(done, 1)
                    if n == 0:
                        invert_denominators()
                        dve.wait_ge(q_copied, nth(seq, q_copied, 16 * 2 * KQ))
                    if n % 2 == 1:
                        dve.wait_ge(num_ready, nth(seq, num_ready, n + 1))
                        dve.tensor_tensor(g[:, 1], g[:, 1], qpT[:, 2 * (i // 4) + 1], ALU.mult)\
                            .then_inc(prod_im_odd, 1)
                for c in range(NC):
                    for n in (2 * c, 2 * c + 1):
                        y = yT[:, c, HALF * (n % 2):HALF * (n % 2) + HALF]
                        dve.wait_ge(y_sb, nth(seq, y_sb, n + 1))
                        dve.wait_ge(ibc_psum, nth(seq, ibc_psum, n + 1))
                        dve.tensor_tensor(y, y, PS[:, n], ALU.mult).then_inc(yn_ready, 1)
                    for n in (2 * c, 2 * c + 1):
                        a = HALF * (n % 2)
                        y = yT[:, c, a:a + HALF]
                        dve.wait_ge(tanh_ready, nth(seq, tanh_ready, n + 1))
                        dve.scalar_tensor_tensor(y, thT[:, c, a:a + HALF], 1.0, y, ALU.add, ALU.mult)\
                            .then_inc(ys_ready, 1)

            def minus_softplus():
                steps = [2]

                def link(i):
                    steps[0] += 1
                    i.then_inc(slope_step, 1)
                    dve.wait_ge(slope_step, steps[0])

                dve.wait_ge(slopes_in, 16)
                dve.scalar_tensor_tensor(slope[:, 1:2], slope[:, 0:1], -1.0, slope[:, 0:1], ALU.mult, ALU.max)\
                    .then_inc(slope_step, 1)
                dve.wait_ge(slope_act, 1)
                dve.tensor_scalar(slope[:, 3:4], slope[:, 2:3], 1.0, None, ALU.add).then_inc(slope_step, 1)
                dve.wait_ge(slope_act, 2)
                link(dve.tensor_scalar(slope[:, 5:6], slope[:, 3:4], -1.0, None, ALU.add))
                link(dve.tensor_scalar(slope[:, 6:7], slope[:, 5:6], 0.0, None, ALU.is_equal))
                link(dve.tensor_tensor(slope[:, 4:5], slope[:, 4:5], slope[:, 6:7], ALU.add))
                link(dve.tensor_tensor(slope[:, 5:6], slope[:, 5:6], slope[:, 6:7], ALU.add))
                link(dve.reciprocal(slope[:, 5:6], slope[:, 5:6]))
                link(dve.tensor_tensor(slope[:, 4:5], slope[:, 4:5], slope[:, 5:6], ALU.mult))
                link(dve.scalar_tensor_tensor(slope[:, 4:5], slope[:, 4:5], -1.0, slope[:, 2:3], ALU.mult, ALU.mult))
                link(dve.tensor_scalar(slope[:, 6:7], slope[:, 0:1], 0.0, None, ALU.max))
                dve.tensor_tensor(slope[:, 7:8], slope[:, 4:5], slope[:, 6:7], ALU.subtract)\
                    .then_inc(slope_step, 1)

            minus_softplus()
            moments(0, 0, x_in, 0)
            moments(0, 0, x_in, 1)
            shift_of(0, 0, 0)
            shift_of(0, 0, 1)
            dve.wait_ge(attn_in, 16 * ATTN_LOADS)
            dve.tensor_copy(ident_b[:], ident[:]).then_inc(pro_dve, 1)
            for c in range(NC):
                for n, tap in enumerate(TAPS):
                    j = KCONV - 1 - tap
                    dve.tensor_scalar(tap_w[:, n, c], ident[:], conv_a[:, c, j:j + 1], None, ALU.mult)\
                        .then_inc(pro_dve, 1)
            dve.wait_ge(pro_dve, PRO_DVE)
            dve.wait_ge(phase_in, 16 * PHASE_LOADS)
            dve.wait_ge(pro_act, PRO_ACT)
            with dve.Fori(0, NSEQ) as seq:
                ripple(seq)
                mix_keys(seq, 0, 0)
                for tp in (2, 3):
                    residual(seq, 0, tp, wo_psum, 2 + tp % 2)
                moments(seq, 1, xs, 1)
                shift_of(seq, 1, 1)
                mix_gates(seq, 0, 0)
                mix_keys(seq, 0, 1)
                mix_gates(seq, 0, 1)
                between(seq, 2, lambda tp: ffn_out(seq, 0, tp))
                phase(seq)
                between(seq, 3, lambda tp: residual(seq, 2, tp, wout_psum, 4 + tp))
                ffn(seq, 1)
                moments(seq + 1, 0, x_in, 0)
                moments(seq + 1, 0, x_in, 1)
                shift_of(seq + 1, 0, 0)
                shift_of(seq + 1, 0, 1)
                for tp in range(4):
                    ffn_out(seq, 1, tp)

        @block.tensor
        def _(pe):
            pe.wait_ge(attn_in, 16 * ATTN_LOADS)
            pe.wait_ge(fills, 1)

            def transpose_h(seq, ln, hf):
                for t in range(TH):
                    pe.wait_ge(h_ready, nth(seq, h_ready, T * ln + TH * hf + t + 1))
                    for c in range(NC):
                        tile = pe.transpose(PS[:, 2 * hf + c, P * t:P * t + P],
                                            h[:, TH * hf + t, P * c:P * c + P], ident[:])
                        if t == TH - 1:
                            tile.then_inc(hT_psum, 1)

            def project(bank, weight, hf, src=None, lead=1):
                src = hT if src is None else src
                a = lead + HALF * hf
                for c in range(NC):
                    last = pe.matmul(PS[:, bank], weight[:, c], src[:, c, a:a + HALF],
                                     start=(c == 0), stop=(c == NC - 1))
                return last

            def project_tokens(bank, tp, src, weight):
                for t in range(2):
                    for c in range(NC):
                        a = P * (2 * tp + t)
                        last = pe.matmul(PS[:, bank, C * t:C * t + C], src[:, c, a:a + P], weight[:, c, :],
                                         start=(c == 0), stop=(c == NC - 1))
                return last

            def ripple(seq):
                def qkv(n):
                    hf, m = n // 6, n % 6
                    col = (C, C + P, 0, P, 2 * C, 2 * C + P)[m]
                    if m == 0:
                        pe.wait_ge(hT_ready, nth(seq, hT_ready, 2 * hf + 2))
                    if n >= 4:
                        pe.wait_ge(qkv_sb, nth(seq, qkv_sb, n - 3))
                    else:
                        pe.wait_ge(out_ready, nth(seq, out_ready, n + 1))
                    project(4 + n % 4, wqkv[:, :, col:col + P], hf).then_inc(qkv_psum, 1)

                def scores(us):
                    hf = 0 if us[0] < 10 else 1
                    if us[0] == 10:
                        pe.wait_ge(sT_ready, nth(seq, sT_ready, 1))
                    for c in range(NC):
                        for u in us:
                            o = u - 10 * hf
                            j, s = o % NJ, o // NJ
                            if c == 0:
                                pe.wait_ge(qk_prod, nth(seq, qk_prod, u + 1))
                            last_o = j + NJ * ((9 + hf - j) // NJ)
                            mm = pe.matmul(PS[32 * j:32 * j + 32, 0], headsum[:, s, c], prods[:, u % 4, c],
                                           start=(o < NJ and c == 0), stop=(o == last_o and c == NC - 1))
                            if c == NC - 1:
                                mm.then_inc(qk_summed, 1)

                def scores_to_tokens(hf):
                    pe.wait_ge(sT_ready, nth(seq, sT_ready, hf + 1))
                    if hf == 1:
                        pe.wait_ge(w3T_ready, nth(seq, w3T_ready, 2))
                    for t in range(TH):
                        last = pe.transpose(PS[:, 1, P * t:P * t + P], sT[:, P * t:P * t + P], ident[:])
                    last.then_inc(stok_psum, 1)

                def fkv_tile(t):
                    pe.wait_ge(elu_ready, nth(seq, elu_ready, 4 * (t // TH) + 2))
                    if t == 0:
                        pe.wait_ge(qkv_sb, nth(seq, qkv_sb, 12))
                    if t >= 4:
                        pe.wait_ge(fkv_ready, nth(seq, fkv_ready, t - 3))
                    a = P * t
                    for c in range(NC):
                        pe.transpose(PS[:, 4 + t % 4, 2 * P * c:2 * P * c + P], fkT[:, c, a:a + P], ident[:])
                        last = pe.transpose(PS[:, 4 + t % 4, 2 * P * c + P:2 * P * c + 2 * P],
                                            vT[:, c, PAD + a:PAD + a + P], ident[:])
                    last.then_inc(fkv_psum, 1)

                def kv_sum():
                    pe.wait_ge(fkv_ready, nth(seq, fkv_ready, T))
                    for c in range(NC):
                        for t in range(T):
                            last = pe.matmul(PS[:, 2 + c, 0:P + 1], fkv[:, t, c, 0:P], fkv[:, t, c, P:2 * P + 1],
                                             start=(t == 0), stop=(t == T - 1))
                    last.then_inc(kv_psum, 1)

                def low_z():
                    pe.wait_ge(elu_ready, nth(seq, elu_ready, 8))
                    pe.wait_ge(sT_ready, nth(seq, sT_ready, 2))
                    for c in range(NC):
                        for q in range(4):
                            last = pe.matmul(PS[32 * q:32 * q + 32, 0, 0:S // 4], zsel[:, c],
                                             fqT[:, c, S // 4 * q:S // 4 * q + S // 4],
                                             start=(c == 0), stop=(c == NC - 1))
                    last.then_inc(z_psum, 1)

                def low(n):
                    c, hf = n % 2, n // 2
                    if n == 0:
                        pe.wait_ge(z_ready, nth(seq, z_ready, 1))
                    else:
                        pe.wait_ge(low_ready, nth(seq, low_ready, n))
                    pe.matmul(PS[:, 0], kvbd[:, c], fqT[:, c, HALF * hf:HALF * hf + HALF],
                              start=True, stop=True).then_inc(low_psum, 1)

                def weights_to_channels(hf, groups):
                    if groups[0] == 0:
                        pe.wait_ge(soft, nth(seq, soft, 14 * hf + 14))
                    else:
                        pe.wait_ge(w3T_ready, nth(seq, w3T_ready, 2 * hf + 1))
                    bank = PS[0:96, 1].bitcast(bf16).rearrange("p (s n) -> p s n", s=2)
                    for s in groups:
                        for t in range(TH):
                            last = pe.transpose(bank[:, s % 2, P * t:P * t + P],
                                                w3[:, t, s].rearrange("p q w -> p (q w)"), ident_b[:])
                    last.then_inc(w3T_psum, 1)

                def spread_weight(hf, o):
                    u = 12 * hf + o
                    if o == 0 or o == 2 * NJ:
                        pe.wait_ge(w3T_ready, nth(seq, w3T_ready, 2 * hf + 1 + (o > 0)))
                    if u >= 2:
                        pe.wait_ge(wv_prod, nth(seq, wv_prod, u - 1))
                    pair = 4 + 2 * (u % 2)
                    if o == LOW:
                        pe.wait_ge(z_ready, nth(seq, z_ready, 2))
                        for c in range(NC):
                            for b in range(2):
                                last = pe.matmul(PS[:, pair + c, 256 * b:256 * b + 256],
                                                 kernelof[:, 2 * hf + b, c], zrec, start=True, stop=True)
                        last.then_inc(wbc_psum, 1)
                        return
                    for c in range(NC):
                        last = pe.matmul(PS[:, pair + c], spread[:, o % NJ, c], w3T[:, hf, o // NJ],
                                         start=True, stop=True)
                    last.then_inc(wbc_psum, 1)

                def tap(hf, n):
                    if n == 0 and hf == 0:
                        pe.wait_ge(kvbd_ready, nth(seq, kvbd_ready, 2))
                    elif n == 0:
                        pe.wait_ge(low_ready, nth(seq, low_ready, 4))
                        pe.wait_ge(w3T_ready, nth(seq, w3T_ready, 4))
                    for c in range(NC):
                        b = PAD + HALF * hf - TAPS[n]
                        pe.matmul(PS[:, sum_bank(hf) + c], tap_w[:, n, c], vT[:, c, b:b + HALF],
                                  start=(n == 0), stop=False)

                def accumulate(hf, g):
                    u = 12 * hf + 3 * g + 2
                    if (hf, g) == (1, 3):
                        pe.wait_ge(wv_own, nth(seq, wv_own, own_adds(7)))
                        for c in range(NC):
                            pe.matmul(PS[:, sum_bank(hf) + c], ident[:], prods[:, (u - 1) % NPROD, c],
                                      start=False, stop=False)
                        pe.wait_ge(wv_prod, nth(seq, wv_prod, u + 1))
                    else:
                        pe.wait_ge(wv_pool, nth(seq, wv_pool, pool_adds(4 * hf + g)))
                    for c in range(NC):
                        last = pe.matmul(PS[:, sum_bank(hf) + c], ident[:], prods[:, u % NPROD, c], start=False, stop=(g == 3))
                    last.then_inc(wv_acc, 1)

                def out_tokens(tp):
                    pe.wait_ge(hsumT_ready, nth(seq, hsumT_ready, 2 * (tp // 2) + 2))
                    if tp >= 2:
                        pe.wait_ge(xs_ready, nth(seq, xs_ready, tp - 1))
                    project_tokens(2 + tp % 2, tp, hsumT, wo).then_inc(wo_psum, 1)

                for n in range(4):
                    qkv(n)
                transpose_h(seq, 0, 1)
                for n in (4, 5):
                    qkv(n)
                for p in range(5):
                    scores((2 * p, 2 * p + 1))
                    qkv(6 + p)
                qkv(11)
                for p in range(5):
                    scores((10 + 2 * p, 11 + 2 * p))
                    if p == 0:
                        scores_to_tokens(0)
                        for t in range(4):
                            fkv_tile(t)
                    if p == 1:
                        for t in range(4, T):
                            fkv_tile(t)
                    if p == 2:
                        kv_sum()
                weights_to_channels(0, (0, 1))
                scores((20,))
                between = {1: [(weights_to_channels, 0, (2,)), (scores_to_tokens, 1)], 2: [(tap, 0, 0)], 3: [(low_z,)], 4: [(tap, 0, 1)],
                           5: [(low, 0)], 6: [(accumulate, 0, 0), (low, 1)], 7: [(tap, 0, 2), (low, 2)],
                           8: [(accumulate, 0, 1), (low, 3)], 10: [(weights_to_channels, 1, (0, 1))],
                           11: [(accumulate, 0, 2), (weights_to_channels, 1, (2,))]}
                for o in range(NO + 1):
                    spread_weight(0, o)
                    for what, *which in between.get(o, ()):
                        what(*which)
                between = {0: [(tap, 1, 0)], 1: [(accumulate, 0, 3)], 2: [(tap, 1, 1)], 4: [(tap, 1, 2)],
                           5: [(accumulate, 1, 0)], 7: [(out_tokens, 0)], 8: [(accumulate, 1, 1)],
                           9: [(out_tokens, 1)], 10: [(accumulate, 1, 2)]}
                for o in range(NO + 1):
                    spread_weight(1, o)
                    for what, *which in between.get(o, ()):
                        what(*which)
                accumulate(1, 3)
                pe.wait_ge(hsumT_ready, nth(seq, hsumT_ready, 4))
                transpose_h(seq, 1, 0)
                for tp in (2, 3):
                    out_tokens(tp)

            def ffn(seq, f):
                def keys(hf):
                    for c in range(NC):
                        pe.wait_ge(xk_ready, nth(seq, xk_ready, 4 * f + 2 * hf + c + 1))
                        for m in range(NC):
                            mm = pe.matmul(PS[:, 4 + 2 * hf + m], wk[:, c, P * m:P * m + P],
                                           xkT[:, c, HALF * hf:HALF * hf + HALF],
                                           start=(c == 0), stop=(c == NC - 1))
                            if c == NC - 1:
                                mm.then_inc(k_psum, 1)

                def gates(hf):
                    pe.wait_ge(xr_ready, nth(seq, xr_ready, 4 * f + 2 * hf + 2))
                    pe.wait_ge(hT_ready, nth(seq, hT_ready, 4 * (1 + 2 * f) + 2 * hf + 2))
                    for tp in (2 * hf, 2 * hf + 1):
                        project_tokens(tp, tp, xrT, wr).then_inc(r_psum, 1)

                def outputs(hf):
                    pe.wait_ge(kact_ready, nth(seq, kact_ready, 4 * f + 2 * hf + 2))
                    for tp in (2 * hf, 2 * hf + 1):
                        project_tokens(4 + tp, tp, kact, wv).then_inc(v_psum, 1)

                keys(0)
                transpose_h(seq, 1 + 2 * f, 1)
                gates(0)
                keys(1)
                outputs(0)
                gates(1)
                if f == 1:
                    pe.wait_ge(gate_ready, nth(seq, gate_ready, 6))
                    transpose_h(seq + 1, 0, 0)
                outputs(1)

            def phase(seq):
                def turn(n):
                    i = ORDER[n]
                    if n == 0:
                        pe.wait_ge(kconv, nth(seq, kconv, 3))
                    if n == 8:
                        pe.wait_ge(k1_conv, nth(seq, k1_conv, 6))
                    if n >= 2:
                        pe.wait_ge(turn_ready, nth(seq, turn_ready, n - 1))
                    for hf in range(2):
                        last = pe.matmul(PS[:, 2 * (n % 2) + hf], theta_w[:, i // 8, i % 8],
                                         zc[:, i // 8, HALF * hf:HALF * hf + HALF], start=True, stop=True)
                    last.then_inc(turn_psum, 1)

                for n, (what, c, hf) in enumerate(PROJECTIONS):
                    if what == "s":
                        weight = w_in_s[:].rearrange("p c r k -> p c (r k)")
                    elif what == "k":
                        weight = w_in_k[:, :, P * c:P * c + P]
                    else:
                        weight = w_in_q[:, :, c].rearrange("p c r f -> p c (r f)")
                    if n == FIRST_HALF:
                        transpose_h(seq, 2, 1)
                    if what == "q" and c == 0:
                        pe.wait_ge(pro_pool, PRO_POOL)
                    if n == TURN_AT + 1:
                        turn(0)
                    pe.wait_ge(hT_ready, nth(seq, hT_ready, 8 + 2 * hf + 2))
                    if n >= 4:
                        pe.wait_ge(z_sb, nth(seq, z_sb, n - 3))
                    else:
                        pe.wait_ge(xs_ready, nth(seq, xs_ready, 4 + n + 1))
                    project(4 + n % 4, weight, hf).then_inc(z_out, 1)

                def spread_decay(n):
                    if n == 0:
                        pe.wait_ge(p3_ready, nth(seq, p3_ready, 1))
                        pe.wait_ge(z_sb, nth(seq, z_sb, NPROJ))
                    else:
                        pe.wait_ge(num_ready, nth(seq, num_ready, n))
                    for hf in range(2):
                        last = pe.matmul(PS[:, 4 + hf], pairof[:, ORDER[n]], p3[0:96, HALF * hf:HALF * hf + HALF],
                                         start=True, stop=True)
                    last.then_inc(pbc_psum, 1)

                def head_sums(n, part):
                    if n == 8 and part == 0:
                        pe.wait_ge(y_sb, nth(seq, y_sb, 2))
                    if part == 0:
                        pe.wait_ge(prod_re, nth(seq, prod_re, n + 2))
                    else:
                        pe.wait_ge(prod_im_even, nth(seq, prod_im_even, n // 2 + 1))
                        pe.wait_ge(prod_im_odd, nth(seq, prod_im_odd, n // 2 + 1))
                    for hf in range(2):
                        for m in (n, n + 1):
                            i = ORDER[m]
                            g = 32 * (i % 8 // 2)
                            mm = pe.matmul(PS[g:g + 32, 6 + hf], phasesum[:, i % 2],
                                           num_ring[m % NNUM][:, part, HALF * hf:HALF * hf + HALF],
                                           start=(i % 2 == 0 and part == 0), stop=(i % 2 == 1 and part == 1))
                            if part == 1 and hf == 1:
                                mm.then_inc(y_psum, 1)

                turn(1)
                for n in range(NPAIR):
                    if n + 2 < NPAIR:
                        turn(n + 2)
                    spread_decay(n)
                    if n >= 3:
                        head_sums(n - 3 if n % 2 else n - 4, 1 - n % 2)
                pe.wait_ge(turn_ready, nth(seq, turn_ready, NPAIR))
                pe.wait_ge(den_step, nth(seq, den_step, 4))
                for n in range(4):
                    c, hf = n // 2, n % 2
                    for b in range(2):
                        q = 2 * hf + b
                        last = pe.matmul(PS[:, n, 256 * b:256 * b + 256], kernelof[:, q, c], den_inv,
                                         start=True, stop=True)
                    last.then_inc(ibc_psum, 1)
                head_sums(NPAIR - 4, 1)
                head_sums(NPAIR - 2, 0)
                head_sums(NPAIR - 2, 1)
                for c, tp in ((0, 0), (0, 1), (1, 0), (1, 1), (0, 2), (1, 2), (0, 3), (1, 3)):
                    if c == 0 and tp >= 2:
                        pe.wait_ge(y_sb, nth(seq, y_sb, 4))
                    pe.wait_ge(ys_ready, nth(seq, ys_ready, 2 * c + tp // 2 + 1))
                    for t in range(2):
                        a = P * (2 * tp + t)
                        last = pe.matmul(PS[:, 4 + tp, C * t:C * t + C], yT[:, c, a:a + P], w_out[:, c, :],
                                         start=(c == 0 and t == 0), stop=(c == NC - 1 and t == 1))
                    if c == NC - 1:
                        last.then_inc(wout_psum, 1)

            transpose_h(0, 0, 0)
            pe.wait_ge(pro_dve, PRO_DVE)
            with pe.Fori(0, NSEQ) as seq:
                ripple(seq)
                ffn(seq, 0)
                transpose_h(seq, 2, 0)
                phase(seq)
                transpose_h(seq, 3, 0)
                ffn(seq, 1)


_WEIGHTS = {
    "Wqkv": "L0_attn_a_Wqkv", "Wo": "L0_attn_a_Wo", "conv_w": "L0_attn_a_conv_w",
    "W_in": "L0_attn_b_W_in", "W_out": "L0_attn_b_W_out", "mu_r": "L0_ffn_mu_r", "mu_k": "L0_ffn_mu_k",
}


def kernel(**inputs):
    import numpy as _np
    import concourse.bacc as _bacc
    from concourse import mybir as _mybir
    from concourse.bass_utils import run_bass_kernel_spmd as _run

    get = lambda name: _np.asarray(inputs[name])
    weights = {name: get(full) for name, full in _WEIGHTS.items()}
    for name in ("W_r", "W_k", "W_v"):
        weights[name.replace("_", "") + "T"] = get("L0_ffn_" + name).T
    for name in ("mu_r", "mu_k"):
        weights[name] = weights[name][:, None]
    conv_k = get("L0_attn_b_conv_k")[:, 0, :].T
    weights["conv_kT"] = conv_k[:C]
    weights["conv_s"] = _np.tile(conv_k[C:], (4, 1))
    weights["W_in_s"] = _np.tile(weights["W_in"][:, C:C + K2], (1, 4))
    weights["theta"] = get("L0_attn_b_theta").reshape(C, M2)
    slopes = _np.concatenate([get("L0_attn_b_decay_slopes"), get("L0_attn_b_anchor_slopes")])
    weights["slopes"] = _np.tile(slopes, 4)[:, None]
    weights["score_scale"] = _np.tile(get("L0_attn_b_score_scale"), 4)[:, None]
    weights["gains"] = _np.concatenate([get("L0_attn_b_norm_scale"), _np.diagonal(get("L0_attn_b_W_re")),
                                        _np.diagonal(get("L0_attn_b_W_im"))])[None, :]

    nc = _bacc.Bacc("TRN2", target_bir_lowering=False, num_devices=1)
    arrays = {}

    def dram(name, a):
        a = _np.ascontiguousarray(a)
        arrays[name] = a
        return nc.dram_tensor(name, a.shape, _mybir.dt.from_np(a.dtype), kind="ExternalInput").ap()

    w = {name: dram(f"in_{name}_dram", a) for name, a in weights.items()}
    k = {name: dram(f"const_{name}_dram", a) for name, a in constants().items()}
    x = dram("in_x_dram", inputs["L0_attn_a_x"])
    out = nc.dram_tensor("out_0_dram", (NSEQ, S, C), _mybir.dt.float32, kind="ExternalOutput").ap()
    build(nc, w, k, x, out)
    r = _run(nc, [arrays], core_ids=[0])
    return r.results[0]["out_0_dram"]
```
